# Optimizing a Trainium2 kernel written in Bass

```python
import numpy as np
import jax
import jax.numpy as jnp

def _softmax(x, axis=-1):
    return jax.nn.softmax(x, axis=axis)

def _gelu(x):
    return jax.nn.gelu(x, approximate=True)

def _silu(x):
    return jax.nn.silu(x)

def _sigmoid(x):
    return jax.nn.sigmoid(x)

def _layernorm(x, axis=-1, eps=1e-05):
    m = jnp.mean(x, axis=axis, keepdims=True)
    v = jnp.var(x, axis=axis, keepdims=True)
    return (x - m) / jnp.sqrt(v + eps)

def _scatter_add(tgt, idx, src, axis=0):
    return tgt.at[idx].add(src)

def _segment_sum(src, seg, n):
    return jax.ops.segment_sum(src, seg, n)
kernel_name = 'mk_vit_tower_d1_tok_img768_r4_b7e218'

def setup_inputs(seed: int=0):
    np.random.seed(seed)
    _w = jnp.asarray

    def _rec_inputs():
        import jax
        import jax.numpy as jnp
        _rk = jax.random.key(seed)
        x = -0.000356955 + 1 * jax.random.normal(jax.random.fold_in(_rk, 1), (128, 3, 224, 224), jnp.float32)
        return x
    x = _rec_inputs()

    def _L0_tok_setup():
        import jax, jax.numpy as jnp
        import numpy as np
        P = 16
        IMG = 224
        C = 3
        HID = 192
        NP = (IMG // P) ** 2
        PATCH_DIM = C * P * P

        def _extract_patches(images):
            B, c, H, Wd = images.shape
            x = images.reshape(B, c, H // P, P, Wd // P, P)
            x = x.transpose(0, 2, 4, 1, 3, 5)
            return x.reshape(B, H // P * (Wd // P), c * P * P)
        key = jax.random.key(seed)
        k1, k2, k3, k4 = jax.random.split(key, 4)
        images = jax.random.normal(k1, (128, C, IMG, IMG), dtype=jnp.float32)
        W = jax.random.normal(k2, (HID, PATCH_DIM), dtype=jnp.float32) * PATCH_DIM ** (-0.5)
        b = jax.random.normal(k3, (HID,), dtype=jnp.float32) * 0.01
        pos = jax.random.normal(k4, (1, NP, HID), dtype=jnp.float32)
        return {'images': images, 'W': W, 'b': b, 'pos': pos}
    _L0_tok_all = _L0_tok_setup()
    _L0_tok_in = {k: v for k, v in _L0_tok_all.items() if k in ('W', 'b', 'pos')}
    del _L0_tok_all

    def _L0_attn_setup():
        import jax, jax.numpy as jnp
        import numpy as np
        D_MODEL = 192
        D_STATE = 64
        D_CONV = 4
        EXPAND = 2
        D_INNER = EXPAND * D_MODEL
        HEADDIM = 64
        NHEADS = D_INNER // HEADDIM
        NGROUPS = 1
        CONV_DIM = D_INNER + 2 * NGROUPS * D_STATE
        D_IN_PROJ = 2 * D_INNER + 2 * NGROUPS * D_STATE + NHEADS
        B_SZ = 2
        SEQ = 1024
        EPS = 1e-05

        def _silu(u):
            return u * jax.nn.sigmoid(u)

        def _causal_conv1d(x, w, b):
            K = w.shape[1]
            L = x.shape[1]
            xp = jnp.pad(x, ((0, 0), (K - 1, 0), (0, 0)))
            y = b
            for k in range(K):
                y = y + xp[:, k:k + L, :] * w[:, k]
            return y

        def _selective_scan(xh, dt, A, Bm, Cm):
            dA = jnp.exp(dt * A)
            dA_t = jnp.moveaxis(dA, 1, 0)
            dt_t = jnp.moveaxis(dt, 1, 0)
            x_t = jnp.moveaxis(xh, 1, 0)
            B_t = jnp.moveaxis(Bm, 1, 0)
            C_t = jnp.moveaxis(Cm, 1, 0)
            h0 = jnp.zeros((xh.shape[0], NHEADS, HEADDIM, D_STATE), xh.dtype)

            def step(h, inp):
                da, dtv, xv, bv, cv = inp
                dBx = (dtv[:, :, None] * xv)[..., None] * bv[:, None, None, :]
                h = h * da[:, :, None, None] + dBx
                y = jnp.einsum('bhpn,bn->bhp', h, cv)
                return (h, y)
            _, ys = jax.lax.scan(step, h0, (dA_t, dt_t, x_t, B_t, C_t))
            return jnp.moveaxis(ys, 0, 1)

        def _mamba2(xn, in_proj_w, conv_w, conv_b, dt_bias, A_log, D_param, rms_w, out_proj_w):
            zxbcdt = xn @ in_proj_w
            z = zxbcdt[..., :D_INNER]
            xBC = zxbcdt[..., D_INNER:D_INNER + CONV_DIM]
            dt = zxbcdt[..., D_INNER + CONV_DIM:]
            xBC = _silu(_causal_conv1d(xBC, conv_w, conv_b))
            xh = xBC[..., :D_INNER]
            Bm = xBC[..., D_INNER:D_INNER + NGROUPS * D_STATE]
            Cm = xBC[..., D_INNER + NGROUPS * D_STATE:]
            dt = jax.nn.softplus(dt + dt_bias)
            A = -jnp.exp(A_log)
            B, L = (xh.shape[0], xh.shape[1])
            xh = xh.reshape(B, L, NHEADS, HEADDIM)
            y = _selective_scan(xh, dt, A, Bm, Cm)
            y = y + xh * D_param[None, None, :, None]
            y = y.reshape(B, L, D_INNER)
            y = y * _silu(z)
            y = y * jax.lax.rsqrt(jnp.mean(y * y, axis=-1, keepdims=True) + EPS) * rms_w
            return y @ out_proj_w
        key = jax.random.key(seed)
        ks = jax.random.split(key, 10)
        s = 0.02
        return {'x': jax.random.normal(ks[0], (B_SZ, SEQ, D_MODEL), jnp.float32), 'ln_w': jnp.ones((D_MODEL,), jnp.float32), 'ln_b': jnp.zeros((D_MODEL,), jnp.float32), 'in_proj_w': jax.random.normal(ks[1], (D_MODEL, D_IN_PROJ), jnp.float32) * s, 'conv_w': jax.random.normal(ks[2], (CONV_DIM, D_CONV), jnp.float32) * s, 'conv_b': jnp.zeros((CONV_DIM,), jnp.float32), 'dt_bias': jax.random.uniform(ks[3], (NHEADS,), jnp.float32, -4.6, -2.0), 'A_log': jnp.log(jnp.arange(1, NHEADS + 1, dtype=jnp.float32)), 'D_param': jnp.ones((NHEADS,), jnp.float32), 'rms_w': jnp.ones((D_INNER,), jnp.float32), 'out_proj_w': jax.random.normal(ks[4], (D_INNER, D_MODEL), jnp.float32) * s, 'gate_w': jax.random.normal(ks[5], (D_MODEL, D_MODEL), jnp.float32) * s, 'gate_b': jnp.zeros((D_MODEL,), jnp.float32), 'out_w': jax.random.normal(ks[6], (D_MODEL, D_MODEL), jnp.float32) * s, 'out_b': jnp.zeros((D_MODEL,), jnp.float32)}
    _L0_attn_all = _L0_attn_setup()
    _L0_attn_in = {k: v for k, v in _L0_attn_all.items() if k in ('ln_w', 'ln_b', 'in_proj_w', 'conv_w', 'conv_b', 'dt_bias', 'A_log', 'D_param', 'rms_w', 'out_proj_w', 'gate_w', 'gate_b', 'out_w', 'out_b')}
    del _L0_attn_all

    def _L0_ffn_setup():
        import jax, jax.numpy as jnp
        import numpy as np
        B, S, H, I = (4, 512, 192, 384)
        E, K = (3, 2)
        INIT = 0.02

        def _expert(x, gw, uw, dw):
            return jax.nn.silu(x @ gw) * (x @ uw) @ dw
        key = jax.random.key(seed)
        ks = jax.random.split(key, 8)
        f32 = jnp.float32
        return {'x': jax.random.normal(ks[0], (B, S, H), f32), 'shared_gate': jax.random.normal(ks[1], (H, I), f32) * INIT, 'shared_up': jax.random.normal(ks[2], (H, I), f32) * INIT, 'shared_down': jax.random.normal(ks[3], (I, H), f32) * INIT, 'routed_gate': jax.random.normal(ks[4], (E, H, I), f32) * INIT, 'routed_up': jax.random.normal(ks[5], (E, H, I), f32) * INIT, 'routed_down': jax.random.normal(ks[6], (E, I, H), f32) * INIT, 'router_w': jax.random.normal(ks[7], (H, E), f32) * INIT, 'routing_bias': jnp.zeros((E,), f32)}
    _L0_ffn_all = _L0_ffn_setup()
    _L0_ffn_in = {k: v for k, v in _L0_ffn_all.items() if k in ('shared_gate', 'shared_up', 'shared_down', 'routed_gate', 'routed_up', 'routed_down', 'router_w', 'routing_bias')}
    del _L0_ffn_all
    return {'x': x, 'L0_tok_W': _L0_tok_in['W'], 'L0_tok_b': _L0_tok_in['b'], 'L0_tok_pos': _L0_tok_in['pos'], 'L0_attn_ln_w': _L0_attn_in['ln_w'], 'L0_attn_ln_b': _L0_attn_in['ln_b'], 'L0_attn_in_proj_w': _L0_attn_in['in_proj_w'], 'L0_attn_conv_w': _L0_attn_in['conv_w'], 'L0_attn_conv_b': _L0_attn_in['conv_b'], 'L0_attn_dt_bias': _L0_attn_in['dt_bias'], 'L0_attn_A_log': _L0_attn_in['A_log'], 'L0_attn_D_param': _L0_attn_in['D_param'], 'L0_attn_rms_w': _L0_attn_in['rms_w'], 'L0_attn_out_proj_w': _L0_attn_in['out_proj_w'], 'L0_attn_gate_w': _L0_attn_in['gate_w'], 'L0_attn_gate_b': _L0_attn_in['gate_b'], 'L0_attn_out_w': _L0_attn_in['out_w'], 'L0_attn_out_b': _L0_attn_in['out_b'], 'L0_ffn_shared_gate': _L0_ffn_in['shared_gate'], 'L0_ffn_shared_up': _L0_ffn_in['shared_up'], 'L0_ffn_shared_down': _L0_ffn_in['shared_down'], 'L0_ffn_routed_gate': _L0_ffn_in['routed_gate'], 'L0_ffn_routed_up': _L0_ffn_in['routed_up'], 'L0_ffn_routed_down': _L0_ffn_in['routed_down'], 'L0_ffn_router_w': _L0_ffn_in['router_w'], 'L0_ffn_routing_bias': _L0_ffn_in['routing_bias']}

def reference(x, L0_tok_W, L0_tok_b, L0_tok_pos, L0_attn_ln_w, L0_attn_ln_b, L0_attn_in_proj_w, L0_attn_conv_w, L0_attn_conv_b, L0_attn_dt_bias, L0_attn_A_log, L0_attn_D_param, L0_attn_rms_w, L0_attn_out_proj_w, L0_attn_gate_w, L0_attn_gate_b, L0_attn_out_w, L0_attn_out_b, L0_ffn_shared_gate, L0_ffn_shared_up, L0_ffn_shared_down, L0_ffn_routed_gate, L0_ffn_routed_up, L0_ffn_routed_down, L0_ffn_router_w, L0_ffn_routing_bias):
    import jax
    import jax.numpy as jnp

    def _L0_tok_ref(images, W, b, pos):
        import jax, jax.numpy as jnp
        import numpy as np
        P = 16
        IMG = 224
        C = 3
        HID = 192
        NP = (IMG // P) ** 2
        PATCH_DIM = C * P * P

        def _extract_patches(images):
            B, c, H, Wd = images.shape
            x = images.reshape(B, c, H // P, P, Wd // P, P)
            x = x.transpose(0, 2, 4, 1, 3, 5)
            return x.reshape(B, H // P * (Wd // P), c * P * P)
        patches = _extract_patches(images)
        emb = jnp.einsum('bnd,hd->bnh', patches, W) + b
        return emb + pos

    def _L0_attn_ref(x, ln_w, ln_b, in_proj_w, conv_w, conv_b, dt_bias, A_log, D_param, rms_w, out_proj_w, gate_w, gate_b, out_w, out_b):
        import jax, jax.numpy as jnp
        import numpy as np
        D_MODEL = 192
        D_STATE = 64
        D_CONV = 4
        EXPAND = 2
        D_INNER = EXPAND * D_MODEL
        HEADDIM = 64
        NHEADS = D_INNER // HEADDIM
        NGROUPS = 1
        CONV_DIM = D_INNER + 2 * NGROUPS * D_STATE
        D_IN_PROJ = 2 * D_INNER + 2 * NGROUPS * D_STATE + NHEADS
        B_SZ = 2
        SEQ = 1024
        EPS = 1e-05

        def _silu(u):
            return u * jax.nn.sigmoid(u)

        def _causal_conv1d(x, w, b):
            K = w.shape[1]
            L = x.shape[1]
            xp = jnp.pad(x, ((0, 0), (K - 1, 0), (0, 0)))
            y = b
            for k in range(K):
                y = y + xp[:, k:k + L, :] * w[:, k]
            return y

        def _selective_scan(xh, dt, A, Bm, Cm):
            dA = jnp.exp(dt * A)
            dA_t = jnp.moveaxis(dA, 1, 0)
            dt_t = jnp.moveaxis(dt, 1, 0)
            x_t = jnp.moveaxis(xh, 1, 0)
            B_t = jnp.moveaxis(Bm, 1, 0)
            C_t = jnp.moveaxis(Cm, 1, 0)
            h0 = jnp.zeros((xh.shape[0], NHEADS, HEADDIM, D_STATE), xh.dtype)

            def step(h, inp):
                da, dtv, xv, bv, cv = inp
                dBx = (dtv[:, :, None] * xv)[..., None] * bv[:, None, None, :]
                h = h * da[:, :, None, None] + dBx
                y = jnp.einsum('bhpn,bn->bhp', h, cv)
                return (h, y)
            _, ys = jax.lax.scan(step, h0, (dA_t, dt_t, x_t, B_t, C_t))
            return jnp.moveaxis(ys, 0, 1)

        def _mamba2(xn, in_proj_w, conv_w, conv_b, dt_bias, A_log, D_param, rms_w, out_proj_w):
            zxbcdt = xn @ in_proj_w
            z = zxbcdt[..., :D_INNER]
            xBC = zxbcdt[..., D_INNER:D_INNER + CONV_DIM]
            dt = zxbcdt[..., D_INNER + CONV_DIM:]
            xBC = _silu(_causal_conv1d(xBC, conv_w, conv_b))
            xh = xBC[..., :D_INNER]
            Bm = xBC[..., D_INNER:D_INNER + NGROUPS * D_STATE]
            Cm = xBC[..., D_INNER + NGROUPS * D_STATE:]
            dt = jax.nn.softplus(dt + dt_bias)
            A = -jnp.exp(A_log)
            B, L = (xh.shape[0], xh.shape[1])
            xh = xh.reshape(B, L, NHEADS, HEADDIM)
            y = _selective_scan(xh, dt, A, Bm, Cm)
            y = y + xh * D_param[None, None, :, None]
            y = y.reshape(B, L, D_INNER)
            y = y * _silu(z)
            y = y * jax.lax.rsqrt(jnp.mean(y * y, axis=-1, keepdims=True) + EPS) * rms_w
            return y @ out_proj_w
        mu = jnp.mean(x, axis=-1, keepdims=True)
        var = jnp.mean((x - mu) ** 2, axis=-1, keepdims=True)
        x_norm = (x - mu) * jax.lax.rsqrt(var + EPS) * ln_w + ln_b
        y = _mamba2(x_norm, in_proj_w, conv_w, conv_b, dt_bias, A_log, D_param, rms_w, out_proj_w)
        gate = jax.nn.sigmoid(x_norm @ gate_w + gate_b)
        y_gated = y * gate
        return x + y_gated @ out_w + out_b

    def _L0_ffn_ref(x, shared_gate, shared_up, shared_down, routed_gate, routed_up, routed_down, router_w, routing_bias):
        import jax, jax.numpy as jnp
        import numpy as np
        B, S, H, I = (4, 512, 192, 384)
        E, K = (3, 2)
        INIT = 0.02

        def _expert(x, gw, uw, dw):
            return jax.nn.silu(x @ gw) * (x @ uw) @ dw
        shared_out = _expert(x, shared_gate, shared_up, shared_down)
        routing_probs = jax.nn.sigmoid(x @ router_w + routing_bias)
        scores, indices = jax.lax.top_k(routing_probs, K)
        scores = scores / scores.sum(axis=-1, keepdims=True)
        combine_w = (jax.nn.one_hot(indices, E, dtype=x.dtype) * scores[..., None]).sum(axis=-2)
        g = jnp.einsum('bsh,ehi->ebsi', x, routed_gate)
        u = jnp.einsum('bsh,ehi->ebsi', x, routed_up)
        h = jax.nn.silu(g) * u
        out_e = jnp.einsum('ebsi,eih->ebsh', h, routed_down)
        combined = jnp.einsum('ebsh,bse->bsh', out_e, combine_w)
        return shared_out + combined
    h = _L0_tok_ref(x, L0_tok_W, L0_tok_b, L0_tok_pos)
    h = h + _L0_attn_ref(_layernorm(h, axis=-1), L0_attn_ln_w, L0_attn_ln_b, L0_attn_in_proj_w, L0_attn_conv_w, L0_attn_conv_b, L0_attn_dt_bias, L0_attn_A_log, L0_attn_D_param, L0_attn_rms_w, L0_attn_out_proj_w, L0_attn_gate_w, L0_attn_gate_b, L0_attn_out_w, L0_attn_out_b)
    h = h + _L0_ffn_ref(_layernorm(h, axis=-1), L0_ffn_shared_gate, L0_ffn_shared_up, L0_ffn_shared_down, L0_ffn_routed_gate, L0_ffn_routed_up, L0_ffn_routed_down, L0_ffn_router_w, L0_ffn_routing_bias)
    return h

_drawn_inputs = setup_inputs


def setup_inputs(seed=0):
    import zlib

    import numpy as np

    out = dict(_drawn_inputs(seed))
    spreads = {'L0_attn_ln_w': (1.0, 0.6),
     'L0_attn_ln_b': (0.0, 0.8),
     'L0_attn_conv_b': (0.0, 0.347),
     'L0_attn_D_param': (1.0, 0.6),
     'L0_attn_rms_w': (1.0, 0.6),
     'L0_attn_gate_b': (0.0, 0.8),
     'L0_attn_out_b': (0.0, 0.1),
     'L0_ffn_routing_bias': (0.0, 0.8)}
    factors = {'L0_tok_b': 7.86,
     'L0_attn_conv_w': 8.0,
     'L0_attn_dt_bias': 8.0,
     'L0_attn_A_log': 8.0,
     'L0_attn_gate_w': 8.0,
     'L0_ffn_shared_gate': 8.0,
     'L0_ffn_shared_up': 8.0,
     'L0_ffn_shared_down': 8.0,
     'L0_ffn_routed_gate': 8.0,
     'L0_ffn_routed_up': 8.0,
     'L0_ffn_routed_down': 8.0,
     'L0_ffn_router_w': 8.0}
    for name, (base, spread) in spreads.items():
        noise = np.random.default_rng([zlib.crc32(name.encode()), seed]).standard_normal(out[name].shape)
        drawn = base * np.exp(spread * noise) if base else spread * noise
        out[name] = jnp.asarray(drawn.astype(out[name].dtype))
    for name, factor in factors.items():
        out[name] = (out[name] * factor).astype(out[name].dtype)
    return out
```

```python
from contextlib import ExitStack

import concourse.bass as bass
from concourse import mybir
from concourse.alu_op_type import AluOpType as ALU

F32 = mybir.dt.float32
F16 = mybir.dt.float16
BF16 = mybir.dt.bfloat16
ACT = mybir.ActivationFunctionType

BATCH, TOKENS, MODEL = 128, 196, 192
SEQS = 2
GROUPS = BATCH // SEQS
T = SEQS * TOKENS
H = TOKENS // 2
TILES = T // H
KA, KB = 128, 64
PATCH = 768
KP = PATCH // 128
INNER, STATE, HEADS, HD = 384, 64, 6, 64
TAPS = 4
NI = INNER // 128
EXPERTS = 4
ROUTED = 3
FF = 384
NF = FF // 128
FTILES = EXPERTS * NF
EPS = 1e-5
CAUSAL = TOKENS + H
WSCALE = 64.0

COL_Z, COL_X, COL_BC, COL_DT, COL_GATE = 0, 384, 768, 896, 902
W1_COLS = COL_GATE + MODEL
PROJ = {"z0": (0, 128), "z1": (128, 128), "z2": (256, 128), "x0": (384, 128), "x1": (512, 128), "x2": (640, 128),
        "bc": (COL_BC, 128), "ga": (COL_GATE, KA), "gb": (COL_GATE + KA, KB)}
PROJ_AT = {name: n for n, name in enumerate(PROJ)}

ORDER = ["embed0", "f0", "embed1", "f1", "norm1", "f2", "ta", "tb", "f3", "dt", "x0", "d00", "x1", "soft", "d01",
         "x2", "conv0", "d02", "bc", "conv1", "silu0", "d03", "f4", "cum", "conv2", "silu1", "cumt", "f5", "z0", "conv3", "silu2",
         "z1", "silu3", "f6", "g0", "d10", "g1", "d11", "xt0", "xt1", "d12", "xt2", "xt3", "d13",
         "cb0", "z2", "f7", "cb1", "ga", "w0", "f8", "w1", "cb2", "cb3", "y0", "f9", "w2", "d20", "w3", "gb", "d21", "cb4", "cb5", "y1", "d22",
         "w4", "d23", "w5", "f10", "y2", "f11", "oa", "ob", "f12", "gate", "ss", "d30", "ow0", "ow1", "split", "d31", "norm2", "d32", "d33",
         "t2a", "t2b", "route", "store"]

OTHER_STEPS = ("norm", "soft", "conv", "silu", "w", "gate", "split", "store")
UNITS = [u for u in ORDER if not (u[0] in "fdw" and u[1:].isdigit()) and u.rstrip("0123456789") not in OTHER_STEPS]
UNIT_BANK = {u: (1 if u == "route" else n % 2) for n, u in enumerate(UNITS)}
UNIT_NTH = {u: sum(UNIT_BANK[w] == UNIT_BANK[u] for w in UNITS[:n]) + 1 for n, u in enumerate(UNITS)}
PER_BANK = [sum(b == k for b in UNIT_BANK.values()) for k in range(2)]

CONSTS = 15


class Count:

    def __init__(self, sem, per):
        self.sem, self.per = sem, per

    def at(self, group, nth):
        i, off = group
        return i * self.per + (self.per * off + nth)

    def any(self, group, nth):
        i, off = group
        return not isinstance(i, int) or self.per * (i + off) + nth > 0


class Nth(Count):

    def __init__(self, sem, per, nth):
        super().__init__(sem, per)
        self.nth = nth

    def at(self, group, back=0):
        return super().at(group, self.nth + back)

    def any(self, group, back=0):
        return super().any(group, self.nth + back)


class Chain(Count):

    def __init__(self, sem):
        super().__init__(sem, 0)
        self.marks = 0

    def begin(self, group):
        if self.marks:
            self.per = self.marks
        self.marks = 0
        self.group = group

    def mark(self):
        self.marks += 1
        return self.sem

    def now(self):
        return self.at(self.group, self.marks)


def build(nc, D):
    with ExitStack() as ctx:
        def sb(name, shape, dt=F32):
            return ctx.enter_context(nc.sbuf_tensor(name, shape, dt))

        def sem(name):
            return ctx.enter_context(nc.semaphore(name))

        bank = [ctx.enter_context(nc.psum_tensor(f"mix{b}", [128, 512], F32)) for b in range(2)]
        gate_ps = [ctx.enter_context(nc.psum_tensor(f"gate{b}", [128, 512], F32)) for b in range(2)]
        up_ps = [ctx.enter_context(nc.psum_tensor(f"up{b}", [128, 512], F32)) for b in range(2)]
        down_ps = [ctx.enter_context(nc.psum_tensor(f"down{b}", [128, 512], F32)) for b in range(2)]

        ident = sb("ident", [128, 128])
        upper = sb("upper", [H, H])
        ones = sb("ones", [128, H])
        causal = sb("causal", [H, CAUSAL])
        pick = sb("pick", [96, HEADS, H], BF16)
        power = sb("power", [128, 8])
        zb, zt = sb("zb", [128, NI, T]), sb("zt", [128, NI, T])
        w1a_raw = zb[:, :, :].rearrange("p k t -> p (k t)")[:, 0:W1_COLS]
        w1b_raw = zt[:, :, :].rearrange("p k t -> p (k t)")[:, 0:W1_COLS]
        w1a_hi, w1a_lo = sb("w1a_hi", [KA, W1_COLS], F16), sb("w1a_lo", [KA, W1_COLS], F16)
        w1b_hi, w1b_lo = sb("w1b_hi", [128, W1_COLS], F16), sb("w1b_lo", [KB, W1_COLS], F16)
        lnwa, lnwb, lnba, lnbb = sb("lnwa", [KA, 1]), sb("lnwb", [128, 1]), sb("lnba", [KA, 1]), sb("lnbb", [KB, 1])
        conv = sb("conv", [128, 4, SEQS, TOKENS])
        wf_raw = conv[:, :, :, :].rearrange("p k s t -> p (k s t)")[:, 0:EXPERTS * FF]
        gua_hi = [sb(f"{n}a_hi", [KA, EXPERTS * FF], F16) for n in ("wg", "wu")]
        gua_lo = [sb(f"{n}a_lo", [KA, EXPERTS * FF], F16) for n in ("wg", "wu")]
        gub_hi = [sb(f"{n}b_hi", [128, EXPERTS * FF], F16) for n in ("wg", "wu")]
        gub_lo = [sb(f"{n}b_lo", [KB, EXPERTS * FF], F16) for n in ("wg", "wu")]
        wgt_rows = sb("wgt", [128, HEADS, SEQS, CAUSAL])
        wgt = wgt_rows[0:H, :, :, :]
        down_raw = wgt_rows[:, :, :, :].rearrange("p h s n -> p (h s n)")[:, 0:FTILES * MODEL]
        down_hi, down_lo = sb("down_hi", [128, FTILES * MODEL], F16), sb("down_lo", [128, FTILES * MODEL], F16)
        tok_hi, tok_lo = sb("tok_hi", [128, KP * MODEL], F16), sb("tok_lo", [128, KP * MODEL], F16)
        outp = sb("outp", [128, NI * MODEL])
        rms = sb("rms", [128, NI])
        owa, owb = sb("owa", [KA, MODEL]), sb("owb", [KB, MODEL])
        ra_raw, rb_raw = sb("ra_raw", [KA, ROUTED]), sb("rb_raw", [128, ROUTED])
        ra_hi, ra_lo = sb("ra_hi", [KA, ROUTED], F16), sb("ra_lo", [KA, ROUTED], F16)
        rb_hi, rb_lo = sb("rb_hi", [128, ROUTED], F16), sb("rb_lo", [KB, ROUTED], F16)
        pos = sb("pos", [H, 2 * MODEL])
        tokb = sb("tokb", [H, MODEL])
        outb = sb("outb", [H, MODEL])
        convw, convb = sb("convw", [128, 4, TAPS]), sb("convb", [128, 4])
        dpar, dhalf = sb("dpar", [128, NI]), sb("dhalf", [128, NI])
        alog, aneg = sb("alog", [H, HEADS]), sb("aneg", [H, HEADS])
        dtb, dtbias = sb("dtb", [H, HEADS]), sb("dtbias", [H, HEADS])
        gba, gbb = sb("gba", [KA, 1]), sb("gbb", [KB, 1])
        rbias = sb("rbias", [H, ROUTED])
        pbias = sb("pbias", [128, len(PROJ)])
        gbias = sb("gbias", [128, 2])

        patches = sb("patches", [128, KP * T])
        pat_hi, pat_lo = sb("pat_hi", [128, KP * T], F16), sb("pat_lo", [128, KP * T], F16)
        h1 = sb("h1", [H, TILES, MODEL])
        base = sb("base", [H, TILES, MODEL])
        xn = sb("xn", [H, TILES, MODEL])
        stats, small = sb("stats", [H, TILES, 6]), sb("small", [H, 8, TILES])
        roots_in, roots = sb("roots_in", [H, 8]), sb("roots", [H, 8])
        xa_hi, xa_lo, xb_hl = sb("xa_hi", [KA, T], F16), sb("xa_lo", [KA, T], F16), sb("xb_hl", [128, T], F16)
        dt_raw = sb("dt_raw", [H, TILES, HEADS])
        sp = sb("sp", [H, 8, TILES * HEADS])
        dta = sb("dta", [H, TILES, HEADS])
        dth = sb("dth", [H, TILES, HEADS])
        cumf = sb("cumf", [HEADS, T])
        cumres = sb("cumres", [HEADS, 2, T])
        cumpart = sb("cumpart", [96, T], BF16)
        ncum = sb("ncum", [H, TILES, HEADS])
        xpad = sb("xpad", [128, 4, SEQS, TAPS - 1 + TOKENS])
        convt = sb("convt", [128, 4, SEQS, TOKENS])
        xs = sb("xs", [128, NI, T])
        bs, cs = sb("bs", [STATE, T]), sb("cs", [STATE, T])
        zs = sb("zs", [128, NI, T])
        gt = sb("gt", [128, 2, T])
        gm = sb("gm", [H, SEQS, CAUSAL])
        xdt = sb("xdt", [H, TILES, INNER])
        decay = sb("decay", [H, 2, SEQS, CAUSAL])
        y1 = sb("y1", [128, NI, T])
        y2 = sb("y2", [128, NI, T])
        sq = sb("sq", [128, NI, T])
        gated = sb("gated", [128, 2, T])
        rinv_in, rinv = sb("rinv_in", [H, TILES]), sb("rinv", [H, TILES])
        h2 = sb("h2", [H, TILES, MODEL])
        fa_hi, fa_lo, fb_hl = sb("fa_hi", [KA, T], F16), sb("fa_lo", [KA, T], F16), sb("fb_hl", [128, T], F16)
        rl = sb("rl", [H, TILES, ROUTED])
        rs = sb("rs", [H, 6, TILES, ROUTED])
        comb = sb("comb", [H, TILES, ROUTED])
        ft = sb("ft", [128, 2, T])
        fg = sb("fg", [128, 2, T])
        fh = sb("fh", [128, 2, T])
        fh_hi, fh_lo = sb("fh_hi", [128, 2, NF, T], F16), sb("fh_lo", [128, 2, NF, T], F16)
        acc = sb("acc", [H, TILES, MODEL])

        s_staged = sem("staging_loaded")
        s_load, s_const, s_prep = sem("weights_loaded"), sem("constants_ready"), sem("prologue_step")
        s_wfree, s_bias = sem("staging_split"), sem("bias_products")
        bank_full, bank_emptied = [sem(f"mix{b}_full") for b in range(2)], [sem(f"mix{b}_emptied") for b in range(2)]
        full = {u: Nth(bank_full[UNIT_BANK[u]], PER_BANK[UNIT_BANK[u]], UNIT_NTH[u]) for u in UNITS}
        emptied = {u: Nth(bank_emptied[UNIT_BANK[u]], PER_BANK[UNIT_BANK[u]], UNIT_NTH[u]) for u in UNITS}
        patch_in = Count(sem("patches_loaded"), 16)
        patch_hi = Count(sem("patches_hi"), 1)
        patch_lo = Count(sem("patches_lo"), 1)
        roots_asked, roots_done = Count(sem("roots_asked"), 2), Count(sem("roots_done"), 3)
        xn_ready = Count(sem("xn_ready"), 2)
        h1_ready = Count(sem("h1_and_scale_ready"), 1)
        base_ready = Count(sem("base_ready"), 1)
        hi_ready = Count(sem("act_hi_ready"), 4)
        soft_in, soft_e = Count(sem("softplus_in"), 1), Count(sem("softplus_exp"), 1)
        dta_ready = Count(sem("dta_ready"), 1)
        cum_ready = Count(sem("cum_ready"), 2)
        conv_ready, convt_ready = Count(sem("conv_ready"), 4), Count(sem("conv_tanh"), 4)
        silu_ready = Count(sem("silu_ready"), 4)
        decay_ready, wgt_ready = Count(sem("decay_ready"), HEADS), Count(sem("wgt_ready"), HEADS)
        y2_ready = Count(sem("y2_ready"), NI)
        sq_ready, sqsum_ready = Count(sem("squares"), NI), Count(sem("square_sums"), 1)
        router_e = Count(sem("router_exp"), 1)
        gate_full, up_full = Count(sem("gate_full"), FTILES), Count(sem("up_full"), FTILES)
        ft_ready = Count(sem("expert_tanh"), FTILES)
        fh_ready = Count(sem("fh_ready"), FTILES)
        fhi_ready, flo_ready = Count(sem("fh_hi_ready"), FTILES), Count(sem("fh_lo_ready"), FTILES)
        down_full, down_free = Count(sem("down_full"), 4 * EXPERTS), Count(sem("down_emptied"), 4 * EXPERTS)
        stored = Count(sem("stored"), 16)
        dve_mix, dve_ffn = Chain(sem("dve_mixer_step")), Chain(sem("dve_expert_step"))
        act_mix, pool_mix = Chain(sem("act_mixer_step")), Chain(sem("pool_mixer_step"))

        def before(g):
            return g[0], g[1] - 1

        def turns(eng, steps, begin=None):
            def turn(i, mixer, experts, split):
                if begin:
                    begin(i, mixer, experts)
                for name in ORDER:
                    is_expert = name[0] in "fd" and name[1:].isdigit() or name == "store"
                    if name not in steps:
                        continue
                    if name == "split":
                        if split:
                            steps[name]((i, 1))
                    elif is_expert:
                        if experts:
                            steps[name]((i, -1))
                    elif mixer:
                        steps[name]((i, 0))
            turn(0, True, False, True)
            turn(1, True, True, True)
            with eng.Fori(2, GROUPS - 1) as i:
                turn(i, True, True, True)
            turn(GROUPS - 1, True, True, False)
            turn(GROUPS, False, True, False)

        block = ctx.enter_context(nc.Block())

        loads = [
            (w1a_raw, D["w1"][0:KA, :]), (w1b_raw[0:KB, :], D["w1"][KA:MODEL, :]), (w1b_raw[KB:128, :], D["w1"][KA:MODEL, :]),
            (lnwa, D["ln_w"][0:KA, :]), (lnwb[0:KB, :], D["ln_w"][KA:MODEL, :]), (lnwb[KB:128, :], D["ln_w"][KA:MODEL, :]),
            (lnba, D["ln_b"][0:KA, :]), (lnbb, D["ln_b"][KA:MODEL, :]),
            (down_raw, D["down"]), (outp, D["out_proj"]), (rms, D["rms_w"]), (owa, D["out_w"][0:KA, :]), (owb, D["out_w"][KA:MODEL, :]),
            (ra_raw, D["router_w"][0:KA, :]), (rb_raw[0:KB, :], D["router_w"][KA:MODEL, :]), (rb_raw[KB:128, :], D["router_w"][KA:MODEL, :]),
            (pos, D["pos"]), (tokb, D["tok_b"]), (outb, D["out_b"]), (convw, D["conv_w"]), (convb, D["conv_b"]), (dpar, D["D"]),
            (alog, D["A_log"]), (dtb, D["dt_bias"]), (gba, D["gate_b"][0:KA, :]), (gbb, D["gate_b"][KA:MODEL, :]), (rbias, D["routing_bias"]),
        ]
        staged = [("tok", D["tok_w"])] + [(f"{n}{p}", D[f"experts_{n}"]) for n in ("gate", "up") for p in "ab"]

        @block.sync
        def _(sp_eng):
            def load_patches(g):
                i, off = g
                if patch_lo.any(g, 0):
                    sp_eng.wait_ge(patch_lo.sem, patch_lo.at(g, 0))
                at = i + off
                src = D["patches"][at] if isinstance(at, int) else D["patches"][bass.ds(at, 1)].rearrange("g p n -> (g p) n")
                sp_eng.dma_start(patches[:, :], src).then_inc(patch_in.sem, 16)

            def store(g):
                i, off = g
                sp_eng.wait_ge(down_free.sem, down_free.at(g, 4 * EXPERTS))
                at = i + off
                dst = D["out"][at] if isinstance(at, int) else D["out"][bass.ds(at, 1)].rearrange("g p n -> (g p) n")
                sp_eng.dma_start(dst, acc[:, :, :].rearrange("p j n -> p (j n)")).then_inc(stored.sem, 16)

            load_patches((0, 0))
            for n, (dst, src) in enumerate(loads):
                sp_eng.dma_start(dst if isinstance(dst, bass.AP) else dst[:], src).then_inc(s_load, 16)
            for n, (name, src) in enumerate(staged):
                if n:
                    sp_eng.wait_ge(s_wfree, n)
                if name == "tok":
                    sp_eng.dma_start(wf_raw[:, 0:KP * MODEL], src).then_inc(s_staged, 16)
                elif name[-1] == "a":
                    sp_eng.dma_start(wf_raw[:, :], src[0:KA, :]).then_inc(s_staged, 16)
                else:
                    sp_eng.dma_start(wf_raw[0:KB, :], src[KA:MODEL, :]).then_inc(s_staged, 16)
                    sp_eng.dma_start(wf_raw[KB:128, :], src[KA:MODEL, :]).then_inc(s_staged, 16)
            turns(sp_eng, {"embed0": lambda g: None, "split": load_patches, "store": store})
            sp_eng.wait_ge(stored.sem, 16 * GROUPS)

        @block.gpsimd
        def _(pool):
            gp = nc.gpsimd

            fills = ((ident, 0.0), (upper, 1.0), (causal, 0.25), (ones, 1.0), (power, -0.5), (pick, 0.0), (cumpart, 0.0),
                     (xpad, 0.0))
            for tensor, value in fills:
                gp.memset(tensor[:], value).then_inc(s_const, 1)
            pool.wait_ge(s_const, len(fills))
            gp.affine_select(out=ident[:, :], in_=ident[:, :], compare_op=ALU.not_equal, fill=1.0, base=0,
                             pattern=[[-1, 128]], channel_multiplier=1).then_inc(s_const, 1)
            pool.wait_ge(s_const, len(fills) + 1)
            for n, part in enumerate((upper[:, :], causal[:, 0:TOKENS], causal[:, TOKENS:CAUSAL])):
                gp.affine_select(out=part, in_=part, compare_op=ALU.is_ge, fill=0.0, base=0,
                                 pattern=[[1, part.shape[1]]], channel_multiplier=-1).then_inc(s_const, 1)
                pool.wait_ge(s_const, len(fills) + 2 + n)
            for n in range(3):
                rows = pick[32 * n:32 * n + 32, :, :]
                gp.affine_select(out=rows, in_=rows, compare_op=ALU.not_equal, fill=1.0, base=0,
                                 pattern=[[-1, HEADS], [0, H]], channel_multiplier=1).then_inc(s_const, 1)
                pool.wait_ge(s_const, len(fills) + 5 + n)

            def split_lo(g):
                pool.wait_ge(patch_hi.sem, patch_hi.at(g, 1))
                gp.tensor_tensor(pat_lo[:, :], patches[:, :], pat_hi[:, :], ALU.subtract).then_inc(patch_lo.sem, 1)

            def root(out, in_, cols):
                gp.tensor_tensor(out, in_, power[0:H, 0:cols], ALU.pow).then_inc(roots_done.sem, 1)

            def norm1(g):
                pool.wait_ge(roots_asked.sem, roots_asked.at(g, 1))
                root(roots[:, :], roots_in[:, :], 8)

            def ta(g):
                pool.wait_ge(h1_ready.sem, h1_ready.at(g, 1))
                flat = [t[:, :, :].rearrange("p j n -> p (j n)") for t in (base, h1)]
                gp.tensor_tensor(flat[0], flat[0], flat[1], ALU.add).then_inc(pool_mix.mark(), 1)
                pool.wait_ge(pool_mix.sem, pool_mix.now())
                gp.tensor_tensor(base[:, :, :], base[:, :, :], outb[:, :].unsqueeze(1).to_broadcast([H, TILES, MODEL]),
                                 ALU.add).then_inc(base_ready.sem, 1)

            def sum_squares(g):
                pool.wait_ge(sq_ready.sem, sq_ready.at(g, NI))
                gp.tensor_tensor(sq[:, 0, :], sq[:, 0, :], sq[:, 1, :], ALU.add).then_inc(pool_mix.mark(), 1)
                pool.wait_ge(pool_mix.sem, pool_mix.now())
                gp.tensor_tensor(sq[:, 0, :], sq[:, 0, :], sq[:, 2, :], ALU.add).then_inc(sqsum_ready.sem, 1)

            def ss(g):
                pool.wait_ge(emptied["ss"].sem, emptied["ss"].at(g))
                root(rinv[:, :], rinv_in[:, :], TILES)

            def norm2(g):
                pool.wait_ge(roots_asked.sem, roots_asked.at(g, 2))
                root(roots[:, 0:TILES], roots_in[:, 0:TILES], TILES)

            def lo(g, t):
                if t:
                    pool.wait_ge(fhi_ready.sem, fhi_ready.at(g, t))
                    e, k = divmod(t - 1, NF)
                    gp.tensor_tensor(fh_lo[:, e % 2, k, :], fh[:, (t - 1) % 2, :], fh_hi[:, e % 2, k, :],
                                     ALU.subtract).then_inc(flo_ready.sem, 1)

            steps = {"split": split_lo, "norm1": norm1, "ta": ta, "oa": sum_squares, "ss": ss, "norm2": norm2}
            for t in range(FTILES + 1):
                steps[f"f{t}"] = lambda g, t=t: lo(g, t)
            split_lo((0, 0))
            turns(pool, steps, lambda i, m, e: pool_mix.begin((i, 0)) if m else None)

        @block.scalar
        def _(act):
            A = nc.scalar.activation

            def split_hi(g):
                act.wait_ge(patch_in.sem, patch_in.at(g, 16))
                if not (isinstance(g[0], int) and g == (0, 0)):
                    if full["embed1"].any(before(g)):
                        act.wait_ge(full["embed1"].sem, full["embed1"].at(before(g)))
                A(pat_hi[:, :], patches[:, :], ACT.Copy).then_inc(patch_hi.sem, 1)

            def hi_a(g, u, out, n):
                act.wait_ge(full[u].sem, full[u].at(g))
                A(out, bank[UNIT_BANK[u]][0:out.shape[0], 0:T], ACT.Copy).then_inc(hi_ready.sem, 1)

            def ta(g):
                if full["gb"].any(before(g)):
                    act.wait_ge(full["gb"].sem, full["gb"].at(before(g)))
                hi_a(g, "ta", xa_hi[:, :], 1)

            def tb(g):
                hi_a(g, "tb", xb_hl[0:KB, :], 2)

            def t2a(g):
                if up_full.any(before(g), FTILES):
                    act.wait_ge(up_full.sem, up_full.at(before(g), FTILES))
                if full["route"].any(before(g)):
                    act.wait_ge(full["route"].sem, full["route"].at(before(g)))
                hi_a(g, "t2a", fa_hi[:, :], 3)

            def t2b(g):
                hi_a(g, "t2b", fb_hl[0:KB, :], 4)

            def project_x(g, k):
                u = f"x{k}" if k < NI else "bc"
                act.wait_ge(full[u].sem, full[u].at(g))
                if conv_ready.any(g, k + 1 - 4):
                    act.wait_ge(conv_ready.sem, conv_ready.at(g, k + 1 - 4))
                n = PROJ_AT[u]
                ins = A(xpad[:, k, :, TAPS - 1:], bank[UNIT_BANK[u]][:, 0:T].rearrange("p (s t) -> p s t", s=SEQS),
                        ACT.Identity, bias=pbias[:, n:n + 1], scale=1.0 / WSCALE)
                ins.then_inc(emptied[u].sem, 1)

            def tanh_conv(g, k):
                act.wait_ge(conv_ready.sem, conv_ready.at(g, k + 1))
                if silu_ready.any(g, k + 1 - 4):
                    act.wait_ge(silu_ready.sem, silu_ready.at(g, k + 1 - 4))
                A(convt[:, k, :, :], conv[:, k, :, :], ACT.Tanh, scale=0.5).then_inc(convt_ready.sem, 1)

            def project_z(g, k):
                u = f"z{k}"
                act.wait_ge(full[u].sem, full[u].at(g))
                if y2_ready.any(g, k + 1 - NI):
                    act.wait_ge(y2_ready.sem, y2_ready.at(g, k + 1 - NI))
                n = PROJ_AT[u]
                A(zb[:, k, :], bank[UNIT_BANK[u]][:, 0:T], ACT.Identity, bias=pbias[:, n:n + 1], scale=1.0 / WSCALE).then_inc(act_mix.mark(), 1)
                act.wait_ge(act_mix.sem, act_mix.now())
                A(zt[:, k, :], zb[:, k, :], ACT.Tanh, scale=0.5).then_inc(emptied[u].sem, 1)

            def gate_tanh(g, k):
                u = ("ga", "gb")[k]
                rows = (KA, KB)[k]
                act.wait_ge(full[u].sem, full[u].at(g))
                if emptied[("oa", "ob")[k]].any(before(g)):
                    act.wait_ge(emptied[("oa", "ob")[k]].sem, emptied[("oa", "ob")[k]].at(before(g)))
                A(gt[0:rows, k, :], bank[UNIT_BANK[u]][0:rows, 0:T], ACT.Tanh, bias=gbias[0:rows, k:k + 1],
                  scale=0.5 / WSCALE).then_inc(emptied[u].sem, 1)

            def soft(g):
                act.wait_ge(soft_in.sem, soft_in.at(g, 1))
                A(sp[:, 1, :], sp[:, 0, :], ACT.Exp, scale=-1.0).then_inc(soft_e.sem, 1)

            def decays(g, h):
                u = f"cb{h}"
                act.wait_ge(full[u].sem, full[u].at(g))
                if h == 0:
                    act.wait_ge(emptied["cumt"].sem, emptied["cumt"].at(g))
                if wgt_ready.any(g, h + 1 - 2):
                    act.wait_ge(wgt_ready.sem, wgt_ready.at(g, h + 1 - 2))
                ps = bank[UNIT_BANK[u]]
                for s in range(SEQS):
                    t0 = s * TOKENS
                    A(decay[:, h % 2, s, 0:TOKENS], ps[0:H, t0:t0 + TOKENS], ACT.Exp, bias=ncum[:, 2 * s, h:h + 1])
                    ins = A(decay[:, h % 2, s, TOKENS:CAUSAL], ps[0:H, t0 + H:t0 + TOKENS], ACT.Exp,
                            bias=ncum[:, 2 * s + 1, h:h + 1])
                ins.then_inc(emptied[u].sem, 1)

            def square(g, m):
                act.wait_ge(y2_ready.sem, y2_ready.at(g, m + 1))
                if m == 0:
                    if full["ss"].any(before(g)):
                        act.wait_ge(full["ss"].sem, full["ss"].at(before(g)))
                A(sq[:, m, :], y2[:, m, :], ACT.Square).then_inc(sq_ready.sem, 1)

            def expert(g, t):
                if t < FTILES:
                    act.wait_ge(gate_full.sem, gate_full.at(g, t + 1))
                    if fh_ready.any(g, t + 1 - 2):
                        act.wait_ge(fh_ready.sem, fh_ready.at(g, t + 1 - 2))
                    A(ft[:, t % 2, :], gate_ps[t % 2][:, 0:T], ACT.Tanh, scale=0.5).then_inc(ft_ready.sem, 1)
                if t:
                    e, k = divmod(t - 1, NF)
                    act.wait_ge(fh_ready.sem, fh_ready.at(g, t))
                    if down_full.any(g, 4 * (e - 1)):
                        act.wait_ge(down_full.sem, down_full.at(g, 4 * (e - 1)))
                    A(fh_hi[:, e % 2, k, :], fh[:, (t - 1) % 2, :], ACT.Copy).then_inc(fhi_ready.sem, 1)

            def route_exp(g):
                act.wait_ge(emptied["route"].sem, emptied["route"].at(g))
                A(rs[:, 0, :, :], rl[:, :, :], ACT.Exp, scale=-1.0).then_inc(router_e.sem, 1)

            steps = {"ta": ta, "tb": tb, "t2a": t2a, "t2b": t2b, "soft": soft, "route": route_exp, "split": split_hi,
                     "oa": lambda g: [square(g, m) for m in range(NI)],
                     "ga": lambda g: gate_tanh(g, 0), "gb": lambda g: gate_tanh(g, 1)}
            for k in range(4):
                steps[f"x{k}" if k < NI else "bc"] = lambda g, k=k: project_x(g, k)
                steps[f"conv{k}"] = lambda g, k=k: tanh_conv(g, k)
            for k in range(NI):
                steps[f"z{k}"] = lambda g, k=k: project_z(g, k)
            for h in range(HEADS):
                steps[f"cb{h}"] = lambda g, h=h: decays(g, h)
            for t in range(FTILES + 1):
                steps[f"f{t}"] = lambda g, t=t: expert(g, t)
            act.wait_ge(s_load, 16 * len(loads))
            A(aneg[:, :], alog[:, :], ACT.Exp).then_inc(s_bias, 1)
            split_hi((0, 0))
            turns(act, steps, lambda i, m, e: act_mix.begin((i, 0)) if m else None)

        @block.vector
        def _(dve):
            V = nc.vector
            prep = Chain(s_prep)
            prep.begin((0, 0))

            dve.wait_ge(s_load, 16 * len(loads))
            dve.wait_ge(s_bias, 1 + 1)
            V.tensor_scalar(aneg[:, :], aneg[:, :], -1.0, None, ALU.mult).then_inc(prep.mark(), 1)
            np_ = len(PROJ)
            V.tensor_copy(pbias[:, 0:np_ - 1], bank[0][:, 0:np_ - 1]).then_inc(prep.mark(), 1)
            V.tensor_copy(pbias[0:KB, np_ - 1:np_], bank[0][0:KB, np_ - 1:np_]).then_inc(prep.mark(), 1)
            V.tensor_tensor(dtbias[:, :], bank[0][0:H, 16:16 + HEADS], dtb[:, :], ALU.add).then_inc(prep.mark(), 1)
            dve.wait_ge(s_prep, prep.now())
            ia, ib = PROJ_AT["ga"], PROJ_AT["gb"]
            V.tensor_tensor(gbias[:, 0:1], pbias[:, ia:ia + 1], gba[:, :], ALU.add).then_inc(prep.mark(), 1)
            V.tensor_tensor(gbias[0:KB, 1:2], pbias[0:KB, ib:ib + 1], gbb[:, :], ALU.add).then_inc(prep.mark(), 1)
            dve.wait_ge(s_prep, prep.now())
            V.tensor_scalar(gbias[:, 0:1], gbias[:, 0:1], 0.5, None, ALU.mult).then_inc(prep.mark(), 1)
            V.tensor_scalar(gbias[0:KB, 1:2], gbias[0:KB, 1:2], 0.5, None, ALU.mult).then_inc(prep.mark(), 1)
            V.tensor_scalar(dhalf[:, :], dpar[:, :], 0.5, None, ALU.mult).then_inc(prep.mark(), 1)
            for s in range(2):
                V.tensor_tensor(pos[:, s * MODEL:(s + 1) * MODEL], pos[:, s * MODEL:(s + 1) * MODEL], tokb[:, :], ALU.add).then_inc(prep.mark(), 1)
            for k in range(NI):
                V.tensor_scalar(outp[:, k * MODEL:(k + 1) * MODEL], outp[:, k * MODEL:(k + 1) * MODEL], rms[:, k:k + 1],
                                    None, ALU.mult).then_inc(prep.mark(), 1)
            V.tensor_scalar(w1a_raw[:, :], w1a_raw[:, :], lnwa[:, 0:1], WSCALE, ALU.mult, ALU.mult).then_inc(prep.mark(), 1)
            V.tensor_scalar(w1b_raw[:, :], w1b_raw[:, :], lnwb[:, 0:1], WSCALE, ALU.mult, ALU.mult).then_inc(prep.mark(), 1)
            dve.wait_ge(s_prep, prep.now())

            def split(hi, lo, raw):
                V.tensor_copy(hi, raw).then_inc(prep.mark(), 1)
                dve.wait_ge(s_prep, prep.now())
                rows = lo.shape[0]
                return V.tensor_tensor(lo, raw[0:rows], hi[0:rows], ALU.subtract)

            split(w1a_hi[:, :], w1a_lo[:, :], w1a_raw[:, :]).then_inc(prep.mark(), 1)
            split(w1b_hi[:, :], w1b_lo[:, :], w1b_raw[:, :]).then_inc(prep.mark(), 1)
            split(ra_hi[:, :], ra_lo[:, :], ra_raw[:, :]).then_inc(prep.mark(), 1)
            split(rb_hi[:, :], rb_lo[:, :], rb_raw[:, :]).then_inc(prep.mark(), 1)
            split(down_hi[:, :], down_lo[:, :], down_raw[:, :]).then_inc(prep.mark(), 1)
            pieces = 0
            for name, _ in staged:
                pieces += 2 if name[-1] == "b" else 1
                dve.wait_ge(s_staged, 16 * pieces)
                if name == "tok":
                    hi, lo, raw = tok_hi[:, :], tok_lo[:, :], wf_raw[:, 0:KP * MODEL]
                else:
                    w = 0 if name.startswith("gate") else 1
                    hi, lo = (gua_hi, gua_lo) if name[-1] == "a" else (gub_hi, gub_lo)
                    hi, lo, raw = hi[w][:, :], lo[w][:, :], wf_raw[:, :]
                split(hi, lo, raw).then_inc(s_wfree, 1)
            dve.wait_ge(s_wfree, len(staged))
            dve.wait_ge(s_const, CONSTS)

            mix, ffn = dve_mix, dve_ffn

            def embed(g, s):
                u = f"embed{s}"
                dve.wait_ge(full[u].sem, full[u].at(g))
                if s == 0:
                    if base_ready.any(g, 0):
                        dve.wait_ge(base_ready.sem, base_ready.at(g, 0))
                ins = V.tensor_tensor(h1[:, 2 * s:2 * s + 2, :].rearrange("p j n -> p (j n)"),
                                      bank[UNIT_BANK[u]][0:H, 0:2 * MODEL], pos[:, :], ALU.add)
                ins.then_inc(emptied[u].sem, 1)

            def moments(src):
                for j in range(TILES):
                    ins = V.bn_stats(stats[:, j, :], src[:, j, :])
                ins.then_inc(mix.mark(), 1)
                dve.wait_ge(mix.sem, mix.now())
                me, mo, ve, vo = (stats[:, :, c] for c in (1, 4, 2, 5))
                V.tensor_tensor(small[:, 0, :], me, mo, ALU.add).then_inc(mix.mark(), 1)
                V.tensor_tensor(small[:, 1, :], me, mo, ALU.subtract).then_inc(mix.mark(), 1)
                V.tensor_tensor(small[:, 2, :], ve, vo, ALU.add).then_inc(mix.mark(), 1)
                dve.wait_ge(mix.sem, mix.now())
                V.tensor_scalar(small[:, 0, :], small[:, 0, :], 0.5, None, ALU.mult).then_inc(mix.mark(), 1)
                V.tensor_tensor(small[:, 1, :], small[:, 1, :], small[:, 1, :], ALU.mult).then_inc(mix.mark(), 1)
                dve.wait_ge(mix.sem, mix.now())
                V.scalar_tensor_tensor(small[:, 3, :], small[:, 1, :], MODEL / 4.0, small[:, 2, :], ALU.mult, ALU.add).then_inc(mix.mark(), 1)
                dve.wait_ge(mix.sem, mix.now())

            def norm1(g):
                dve.wait_ge(emptied["embed1"].sem, emptied["embed1"].at(g))
                dve.wait_ge(emptied["embed0"].sem, emptied["embed0"].at(g))
                moments(h1)
                V.tensor_scalar(roots_in[:, 0:TILES], small[:, 3, :], 1.0 / MODEL, EPS, ALU.mult, ALU.add).then_inc(mix.mark(), 1)
                dve.wait_ge(mix.sem, mix.now())
                V.tensor_scalar(roots_in[:, TILES:8], small[:, 3, :], (1.0 + EPS) / MODEL, EPS * EPS, ALU.mult,
                                ALU.add).then_inc(roots_asked.sem, 1)

            def ta(g):
                dve.wait_ge(roots_done.sem, roots_done.at(g, 1))
                if full["t2b"].any(before(g)):
                    dve.wait_ge(full["t2b"].sem, full["t2b"].at(before(g)))
                for j in range(TILES):
                    ins = V.tensor_scalar(xn[:, j, :], h1[:, j, :], small[:, 0, j:j + 1], roots[:, TILES + j:TILES + j + 1],
                                          ALU.subtract, ALU.mult)
                    if j == TILES - 1:
                        ins.then_inc(xn_ready.sem, 1)
                    else:
                        ins.then_inc(mix.mark(), 1)
                for j in range(TILES):
                    ins = V.tensor_scalar(base[:, j, :], h1[:, j, :], small[:, 0, j:j + 1], roots[:, j:j + 1],
                                          ALU.subtract, ALU.mult)
                    if j == TILES - 1:
                        ins.then_inc(h1_ready.sem, 1)
                    else:
                        ins.then_inc(mix.mark(), 1)

            def tb(g):
                dve.wait_ge(hi_ready.sem, hi_ready.at(g, 1))
                V.tensor_tensor(xa_lo[:, :], bank[UNIT_BANK["ta"]][0:KA, 0:T], xa_hi[:, :],
                                ALU.subtract).then_inc(emptied["ta"].sem, 1)
                dve.wait_ge(hi_ready.sem, hi_ready.at(g, 2))
                V.tensor_tensor(xb_hl[KB:128, :], bank[UNIT_BANK["tb"]][0:KB, 0:T], xb_hl[0:KB, :],
                                ALU.subtract).then_inc(emptied["tb"].sem, 1)

            def dt(g):
                u = "dt"
                dve.wait_ge(full[u].sem, full[u].at(g))
                cols = TILES * HEADS
                flat = dt_raw[:, :, :].rearrange("p j h -> p (j h)")
                ins = V.scalar_tensor_tensor(dt_raw[:, :, :], bank[UNIT_BANK[u]][0:H, 0:cols].rearrange("p (j h) -> p j h", j=TILES),
                                             1.0 / WSCALE, dtbias[:, :].unsqueeze(1).to_broadcast([H, TILES, HEADS]), ALU.mult, ALU.add)
                ins.then_inc(emptied[u].sem, 1)
                dve.wait_ge(emptied[u].sem, emptied[u].at(g))
                V.scalar_tensor_tensor(sp[:, 0, :], flat, -1.0, flat, ALU.mult, ALU.max).then_inc(soft_in.sem, 1)
                V.tensor_scalar(sp[:, 2, :], flat, 0.0, None, ALU.max).then_inc(mix.mark(), 1)

            def soft(g):
                dve.wait_ge(soft_e.sem, soft_e.at(g, 1))
                dve.wait_ge(mix.sem, mix.now())
                e, s, s2, p = sp[:, 1, :], sp[:, 3, :], sp[:, 4, :], sp[:, 5, :]
                V.tensor_scalar(s, e, 2.0, None, ALU.add).then_inc(mix.mark(), 1)
                dve.wait_ge(mix.sem, mix.now())
                V.reciprocal(s2, s).then_inc(mix.mark(), 1)
                dve.wait_ge(mix.sem, mix.now())
                V.tensor_tensor(s, e, s2, ALU.mult).then_inc(mix.mark(), 1)
                dve.wait_ge(mix.sem, mix.now())
                V.tensor_tensor(s2, s, s, ALU.mult).then_inc(mix.mark(), 1)
                dve.wait_ge(mix.sem, mix.now())
                V.tensor_scalar(p, s2, 1.0 / 15, None, ALU.mult).then_inc(mix.mark(), 1)
                dve.wait_ge(mix.sem, mix.now())
                for c in (13, 11, 9, 7, 5, 3):
                    V.scalar_tensor_tensor(p, p, 1.0 / c, s2, ALU.add, ALU.mult).then_inc(mix.mark(), 1)
                    dve.wait_ge(mix.sem, mix.now())
                V.scalar_tensor_tensor(p, p, 1.0, s, ALU.add, ALU.mult).then_inc(mix.mark(), 1)
                dve.wait_ge(mix.sem, mix.now())
                V.scalar_tensor_tensor(s, p, 2.0, sp[:, 2, :], ALU.mult, ALU.add).then_inc(mix.mark(), 1)
                dve.wait_ge(mix.sem, mix.now())
                V.tensor_scalar(dth[:, :, :].rearrange("p j h -> p (j h)"), s, 0.5, None, ALU.mult).then_inc(mix.mark(), 1)
                V.tensor_tensor(dta[:, :, :], s.rearrange("p (j h) -> p j h", j=TILES),
                                aneg[:, :].unsqueeze(1).to_broadcast([H, TILES, HEADS]), ALU.mult).then_inc(dta_ready.sem, 1)

            def cum(g):
                u = "cum"
                dve.wait_ge(full[u].sem, full[u].at(g))
                if full["cb5"].any(before(g)):
                    dve.wait_ge(full["cb5"].sem, full["cb5"].at(before(g)))
                ps = bank[UNIT_BANK[u]][0:HEADS, 0:T]
                V.tensor_copy(cumf[:, :], ps).then_inc(cum_ready.sem, 1)
                V.tensor_copy(cumpart[0:HEADS, :], ps).then_inc(mix.mark(), 1)
                dve.wait_ge(mix.sem, mix.now())
                ins = V.tensor_tensor(cumres[:, 0, :], ps, cumpart[0:HEADS, :], ALU.subtract)
                ins.then_inc(emptied[u].sem, 1)
                dve.wait_ge(emptied[u].sem, emptied[u].at(g))
                V.tensor_copy(cumpart[32:32 + HEADS, :], cumres[:, 0, :]).then_inc(mix.mark(), 1)
                dve.wait_ge(mix.sem, mix.now())
                V.tensor_copy(cumres[:, 1, :], cumpart[32:32 + HEADS, :]).then_inc(mix.mark(), 1)
                dve.wait_ge(mix.sem, mix.now())
                V.tensor_tensor(cumpart[64:64 + HEADS, :], cumres[:, 0, :], cumres[:, 1, :], ALU.subtract).then_inc(cum_ready.sem, 1)

            def cumt(g):
                u = "cumt"
                dve.wait_ge(full[u].sem, full[u].at(g))
                if emptied["cb5"].any(before(g)):
                    dve.wait_ge(emptied["cb5"].sem, emptied["cb5"].at(before(g)))
                V.tensor_scalar(ncum[:, :, :].rearrange("p j h -> p (j h)"), bank[UNIT_BANK[u]][0:H, 0:TILES * HEADS], -1.0, None,
                                ALU.mult).then_inc(emptied[u].sem, 1)

            def convolve(g, k):
                u = f"x{k}" if k < NI else "bc"
                dve.wait_ge(emptied[u].sem, emptied[u].at(g))
                if convt_ready.any(g, k + 1 - 4):
                    dve.wait_ge(convt_ready.sem, convt_ready.at(g, k + 1 - 4))
                for tap in range(TAPS):
                    src = xpad[:, k, :, tap:tap + TOKENS]
                    w = convw[:, k, tap:tap + 1]
                    out = conv[:, k, :, :]
                    if tap == 0:
                        V.tensor_scalar(out, src, w, convb[:, k:k + 1], ALU.mult, ALU.add).then_inc(mix.mark(), 1)
                    elif tap < TAPS - 1:
                        V.scalar_tensor_tensor(out, src, w, out, ALU.mult, ALU.add).then_inc(mix.mark(), 1)
                    else:
                        V.scalar_tensor_tensor(out, src, w, out, ALU.mult, ALU.add).then_inc(conv_ready.sem, 1)
                    if tap < TAPS - 1:
                        dve.wait_ge(mix.sem, mix.now())

            def silu(g, k):
                dve.wait_ge(convt_ready.sem, convt_ready.at(g, k + 1))
                dve.wait_ge(conv_ready.sem, conv_ready.at(g, k + 1))
                t, v = convt[:, k, :, :], conv[:, k, :, :]
                if k < NI:
                    if k == 0:
                        if y2_ready.any(g, 0):
                            dve.wait_ge(y2_ready.sem, y2_ready.at(g, 0))
                        if full["xt3"].any(before(g)):
                            dve.wait_ge(full["xt3"].sem, full["xt3"].at(before(g)))
                    V.scalar_tensor_tensor(xs[:, k, :].rearrange("p (s t) -> p s t", s=SEQS), t, 1.0, v, ALU.add,
                                           ALU.mult).then_inc(silu_ready.sem, 1)
                else:
                    if full["g1"].any(before(g)):
                        dve.wait_ge(full["g1"].sem, full["g1"].at(before(g)))
                    for n, dst in enumerate((bs, cs)):
                        rows = slice(n * STATE, (n + 1) * STATE)
                        ins = V.scalar_tensor_tensor(dst[:, :].rearrange("p (s t) -> p s t", s=SEQS), t[rows], 1.0, v[rows],
                                                     ALU.add, ALU.mult)
                        if n == 0:
                            ins.then_inc(mix.mark(), 1)
                        else:
                            ins.then_inc(silu_ready.sem, 1)

            def masked(g, s):
                u = f"g{s}"
                dve.wait_ge(full[u].sem, full[u].at(g))
                V.tensor_tensor(gm[:, s, :], bank[UNIT_BANK[u]][0:H, 0:CAUSAL], causal[:, :], ALU.mult).then_inc(
                    emptied[u].sem, 1)

            def x_dt(g, j):
                u = f"xt{j}"
                dve.wait_ge(full[u].sem, full[u].at(g))
                if j == 0:
                    if full["y2"].any(before(g)):
                        dve.wait_ge(full["y2"].sem, full["y2"].at(before(g)))
                    dve.wait_ge(mix.sem, mix.now())
                ins = V.tensor_tensor(xdt[:, j, :].rearrange("p (h d) -> p h d", h=HEADS),
                                      bank[UNIT_BANK[u]][0:H, 0:INNER].rearrange("p (h d) -> p h d", h=HEADS),
                                      dth[:, j, :].unsqueeze(2).to_broadcast([H, HEADS, HD]), ALU.mult)
                ins.then_inc(emptied[u].sem, 1)

            def weight(g, h):
                dve.wait_ge(emptied[f"cb{h}"].sem, emptied[f"cb{h}"].at(g))
                if h == 0:
                    for s in range(SEQS):
                        dve.wait_ge(emptied[f"g{s}"].sem, emptied[f"g{s}"].at(g))
                    if full["y2"].any(before(g)):
                        dve.wait_ge(full["y2"].sem, full["y2"].at(before(g)))
                V.scalar_tensor_tensor(wgt[:, h, :, :].rearrange("p s n -> p (s n)"), decay[:, h % 2, :, :].rearrange("p s n -> p (s n)"),
                                       1.0, gm[:, :, :].rearrange("p s n -> p (s n)"), ALU.min, ALU.mult).then_inc(wgt_ready.sem, 1)

            def gate_z(g, k):
                dve.wait_ge(emptied[f"z{k}"].sem, emptied[f"z{k}"].at(g))
                V.scalar_tensor_tensor(zs[:, k, :], zt[:, k, :], 1.0, zb[:, k, :], ALU.add, ALU.mult).then_inc(mix.mark(), 1)

            def y_out(g, n):
                u = f"y{n}"
                gate_z(g, n)
                dve.wait_ge(full[u].sem, full[u].at(g))
                dve.wait_ge(silu_ready.sem, silu_ready.at(g, n + 1))
                ins = V.scalar_tensor_tensor(y1[:, n, :], xs[:, n, :], dhalf[:, n:n + 1], bank[UNIT_BANK[u]][:, 0:T],
                                             ALU.mult, ALU.add)
                ins.then_inc(emptied[u].sem, 1)
                dve.wait_ge(emptied[u].sem, emptied[u].at(g))
                dve.wait_ge(mix.sem, mix.now())
                if n == 0:
                    if sq_ready.any(g, 0):
                        dve.wait_ge(sq_ready.sem, sq_ready.at(g, 0))
                    if full["ob"].any(before(g)):
                        dve.wait_ge(full["ob"].sem, full["ob"].at(before(g)))
                V.tensor_tensor(y2[:, n, :], y1[:, n, :], zs[:, n, :], ALU.mult).then_inc(y2_ready.sem, 1)

            def gate_out(g, n):
                u, rows = ("oa", "ob")[n], (KA, KB)[n]
                dve.wait_ge(full[u].sem, full[u].at(g))
                gu = ("ga", "gb")[n]
                dve.wait_ge(emptied[gu].sem, emptied[gu].at(g))
                if full["ow1"].any(before(g)):
                    dve.wait_ge(full["ow1"].sem, full["ow1"].at(before(g)))
                V.scalar_tensor_tensor(gated[0:rows, n, :], gt[0:rows, n, :], 1.0, bank[UNIT_BANK[u]][0:rows, 0:T],
                                       ALU.add, ALU.mult).then_inc(emptied[u].sem, 1)

            def ss(g):
                u = "ss"
                dve.wait_ge(full[u].sem, full[u].at(g))
                ins = V.tensor_scalar(rinv_in[:, :], bank[UNIT_BANK[u]][0:H, 0:TILES], 0.25 / INNER, EPS, ALU.mult, ALU.add)
                ins.then_inc(emptied[u].sem, 1)

            def residual(g, s):
                u = f"ow{s}"
                if s == 0:
                    dve.wait_ge(roots_done.sem, roots_done.at(g, 2))
                    V.tensor_scalar(rinv[:, :], rinv[:, :], 0.25, None, ALU.mult).then_inc(mix.mark(), 1)
                    dve.wait_ge(mix.sem, mix.now())
                    dve.wait_ge(base_ready.sem, base_ready.at(g, 1))
                    if down_free.any(before(g), TILES):
                        dve.wait_ge(down_free.sem, down_free.at(before(g), TILES))
                dve.wait_ge(full[u].sem, full[u].at(g))
                for j in (2 * s, 2 * s + 1):
                    ins = V.scalar_tensor_tensor(h2[:, j, :], bank[UNIT_BANK[u]][0:H, (j % 2) * MODEL:(j % 2 + 1) * MODEL],
                                                 rinv[:, j:j + 1], base[:, j, :], ALU.mult, ALU.add)
                    if j % 2 == 0:
                        ins.then_inc(mix.mark(), 1)
                    else:
                        ins.then_inc(emptied[u].sem, 1)

            def norm2(g):
                dve.wait_ge(mix.sem, mix.now())
                for s in range(SEQS):
                    dve.wait_ge(emptied[f"ow{s}"].sem, emptied[f"ow{s}"].at(g))
                moments(h2)
                V.tensor_scalar(roots_in[:, 0:TILES], small[:, 3, :], 1.0 / MODEL, EPS, ALU.mult, ALU.add).then_inc(roots_asked.sem, 1)

            def t2a(g):
                dve.wait_ge(roots_done.sem, roots_done.at(g, 3))
                dve.wait_ge(full["tb"].sem, full["tb"].at(g))
                for j in range(TILES):
                    ins = V.tensor_scalar(xn[:, j, :], h2[:, j, :], small[:, 0, j:j + 1], roots[:, j:j + 1],
                                          ALU.subtract, ALU.mult)
                    if j == TILES - 1:
                        ins.then_inc(xn_ready.sem, 1)
                    else:
                        ins.then_inc(mix.mark(), 1)

            def t2b(g):
                dve.wait_ge(hi_ready.sem, hi_ready.at(g, 3))
                V.tensor_tensor(fa_lo[:, :], bank[UNIT_BANK["t2a"]][0:KA, 0:T], fa_hi[:, :], ALU.subtract).then_inc(
                    emptied["t2a"].sem, 1)
                dve.wait_ge(hi_ready.sem, hi_ready.at(g, 4))
                V.tensor_tensor(fb_hl[KB:128, :], bank[UNIT_BANK["t2b"]][0:KB, 0:T], fb_hl[0:KB, :], ALU.subtract).then_inc(
                    emptied["t2b"].sem, 1)

            def route(g):
                u = "route"
                dve.wait_ge(full[u].sem, full[u].at(g))
                ins = V.tensor_tensor(rl[:, :, :], bank[UNIT_BANK[u]][0:H, 0:TILES * ROUTED].rearrange("p (j e) -> p j e", j=TILES),
                                      rbias[:, :].unsqueeze(1).to_broadcast([H, TILES, ROUTED]), ALU.add)
                ins.then_inc(emptied[u].sem, 1)

            def combine(g):
                dve.wait_ge(router_e.sem, router_e.at(g, 1))
                e, s, keep = rs[:, 0, :, :], rs[:, 2, :, :], rs[:, 3, :, :]
                tmp = rs[:, 4, :, :]
                V.tensor_scalar(e, e, 1.0, None, ALU.add).then_inc(ffn.mark(), 1)
                dve.wait_ge(ffn.sem, ffn.now())
                V.reciprocal(s, e).then_inc(ffn.mark(), 1)
                dve.wait_ge(ffn.sem, ffn.now())
                V.tensor_tensor(tmp[:, :, 0], s[:, :, 1], s[:, :, 2], ALU.min).then_inc(ffn.mark(), 1)
                dve.wait_ge(ffn.sem, ffn.now())
                V.tensor_tensor(tmp[:, :, 1], s[:, :, 0], s[:, :, 1], ALU.min).then_inc(ffn.mark(), 1)
                dve.wait_ge(ffn.sem, ffn.now())
                V.tensor_tensor(keep[:, :, 0], s[:, :, 0], tmp[:, :, 0], ALU.is_ge).then_inc(ffn.mark(), 1)
                dve.wait_ge(ffn.sem, ffn.now())
                V.tensor_tensor(keep[:, :, 2], s[:, :, 2], tmp[:, :, 1], ALU.is_gt).then_inc(ffn.mark(), 1)
                dve.wait_ge(ffn.sem, ffn.now())
                V.tensor_tensor(tmp[:, :, 2], keep[:, :, 0], keep[:, :, 2], ALU.add).then_inc(ffn.mark(), 1)
                dve.wait_ge(ffn.sem, ffn.now())
                V.tensor_scalar(keep[:, :, 1], tmp[:, :, 2], -1.0, 2.0, ALU.mult, ALU.add).then_inc(ffn.mark(), 1)
                dve.wait_ge(ffn.sem, ffn.now())
                V.tensor_tensor(s, s, keep, ALU.mult).then_inc(ffn.mark(), 1)
                dve.wait_ge(ffn.sem, ffn.now())
                V.tensor_tensor(tmp[:, :, 0], s[:, :, 0], s[:, :, 1], ALU.add).then_inc(ffn.mark(), 1)
                dve.wait_ge(ffn.sem, ffn.now())
                V.tensor_tensor(tmp[:, :, 0], tmp[:, :, 0], s[:, :, 2], ALU.add).then_inc(ffn.mark(), 1)
                dve.wait_ge(ffn.sem, ffn.now())
                V.reciprocal(tmp[:, :, 1], tmp[:, :, 0]).then_inc(ffn.mark(), 1)
                dve.wait_ge(ffn.sem, ffn.now())
                V.tensor_scalar(tmp[:, :, 1], tmp[:, :, 1], 0.5, None, ALU.mult).then_inc(ffn.mark(), 1)
                dve.wait_ge(ffn.sem, ffn.now())
                V.tensor_tensor(comb[:, :, :], s, tmp[:, :, 1:2].to_broadcast([H, TILES, ROUTED]), ALU.mult).then_inc(ffn.mark(), 1)
                dve.wait_ge(ffn.sem, ffn.now())

            def expert(g, t):
                if t == 0:
                    combine(g)
                if t == FTILES:
                    return
                dve.wait_ge(ft_ready.sem, ft_ready.at(g, t + 1))
                V.scalar_tensor_tensor(fg[:, t % 2, :], ft[:, t % 2, :], 1.0, gate_ps[t % 2][:, 0:T], ALU.add, ALU.mult).then_inc(ffn.mark(), 1)
                dve.wait_ge(ffn.sem, ffn.now())
                dve.wait_ge(up_full.sem, up_full.at(g, t + 1))
                if flo_ready.any(g, t + 1 - 2):
                    dve.wait_ge(flo_ready.sem, flo_ready.at(g, t + 1 - 2))
                V.tensor_tensor(fh[:, t % 2, :], fg[:, t % 2, :], up_ps[t % 2][:, 0:T], ALU.mult).then_inc(fh_ready.sem, 1)

            def down(g, e, j):
                n = TILES * e + j
                dve.wait_ge(down_full.sem, down_full.at(g, n + 1))
                if e == 0:
                    if j == 0:
                        if stored.any(g, 0):
                            dve.wait_ge(stored.sem, stored.at(g, 0))
                    V.scalar_tensor_tensor(acc[:, j, :], down_ps[j % 2][0:H, 0:MODEL], 0.5, h2[:, j, :], ALU.mult,
                                           ALU.add).then_inc(down_free.sem, 1)
                else:
                    dve.wait_ge(down_free.sem, down_free.at(g, n + 1 - TILES))
                    V.scalar_tensor_tensor(acc[:, j, :], down_ps[j % 2][0:H, 0:MODEL], comb[:, j, e - 1:e], acc[:, j, :],
                                           ALU.mult, ALU.add).then_inc(down_free.sem, 1)

            steps = {"norm1": norm1, "ta": ta, "tb": tb, "dt": dt, "soft": soft, "cum": cum, "cumt": cumt, "ss": ss,
                     "gate": lambda g: [gate_out(g, n) for n in range(2)], "norm2": norm2, "t2a": t2a, "t2b": t2b, "route": route}
            for s in range(SEQS):
                steps[f"embed{s}"] = lambda g, s=s: embed(g, s)
                steps[f"g{s}"] = lambda g, s=s: masked(g, s)
                steps[f"ow{s}"] = lambda g, s=s: residual(g, s)
            for k in range(4):
                steps[f"conv{k}"] = lambda g, k=k: convolve(g, k)
                steps[f"silu{k}"] = lambda g, k=k: silu(g, k)
                steps[f"xt{k}"] = lambda g, k=k: x_dt(g, k)
            for h in range(HEADS):
                steps[f"w{h}"] = lambda g, h=h: weight(g, h)
            for n in range(NI):
                steps[f"y{n}"] = lambda g, n=n: y_out(g, n)
            for t in range(FTILES + 1):
                steps[f"f{t}"] = lambda g, t=t: expert(g, t)
            for e in range(EXPERTS):
                for j in range(TILES):
                    steps[f"d{e}{j}"] = lambda g, e=e, j=j: down(g, e, j)

            def begin(i, mixer, experts):
                if mixer:
                    mix.begin((i, 0))
                if experts:
                    ffn.begin((i, -1))
            turns(dve, steps, begin)

        @block.tensor
        def _(pe):
            M = nc.tensor.matmul

            pe.wait_ge(s_load, 16 * len(loads))
            pe.wait_ge(s_const, CONSTS)
            for n, (c, width) in enumerate(PROJ.values()):
                M(bank[0][0:width, n:n + 1], w1a_raw[:, c:c + width], lnba[:, :], start=True, stop=False)
                M(bank[0][0:width, n:n + 1], w1b_raw[0:KB, c:c + width], lnbb[:, :], start=False, stop=True)
            M(bank[0][0:H, 16:16 + HEADS], lnba[:, 0:1].to_broadcast([KA, H]), w1a_raw[:, COL_DT:COL_DT + HEADS], start=True, stop=False)
            M(bank[0][0:H, 16:16 + HEADS], lnbb[:, 0:1].to_broadcast([KB, H]), w1b_raw[0:KB, COL_DT:COL_DT + HEADS], start=False,
              stop=True).then_inc(s_bias, 1)
            pe.wait_ge(s_wfree, len(staged))

            def five(out, a_hi, a_lo, b_hi, b_lo, xa, xl, xb, first=True):
                M(out, a_hi, xa, start=first, stop=False, skip_group_check=True)
                M(out, a_lo, xa, start=False, stop=False, skip_group_check=True)
                M(out, a_hi, xl, start=False, stop=False, skip_group_check=True)
                M(out, b_hi, xb, start=False, stop=False, skip_group_check=True)
                return M(out, b_lo, xb[0:KB], start=False, stop=True, skip_group_check=True)

            def five_rows(out, w, xa, xl, xb, first):
                a_hi, a_lo, b_hi, b_lo = w
                M(out, xa, a_hi, start=first, stop=False, skip_group_check=True)
                M(out, xa, a_lo, start=False, stop=False, skip_group_check=True)
                M(out, xl, a_hi, start=False, stop=False, skip_group_check=True)
                M(out, xb, b_hi, start=False, stop=False, skip_group_check=True)
                return M(out, xb[0:KB], b_lo, start=False, stop=True, skip_group_check=True)

            def embed(g, s):
                u = f"embed{s}"
                pe.wait_ge(patch_lo.sem, patch_lo.at(g, 1))
                pe.wait_ge(patch_hi.sem, patch_hi.at(g, 1))
                if emptied[u].any(g, -1):
                    pe.wait_ge(emptied[u].sem, emptied[u].at(g, -1))
                hi = pat_hi[:, :].rearrange("p (k t) -> p k t", k=KP)
                lo = pat_lo[:, :].rearrange("p (k t) -> p k t", k=KP)
                for j in (2 * s, 2 * s + 1):
                    out = bank[UNIT_BANK[u]][0:H, (j % 2) * MODEL:(j % 2 + 1) * MODEL]
                    for k in range(KP):
                        xh, xl = hi[:, k, j * H:(j + 1) * H], lo[:, k, j * H:(j + 1) * H]
                        wh, wl = tok_hi[:, k * MODEL:(k + 1) * MODEL], tok_lo[:, k * MODEL:(k + 1) * MODEL]
                        M(out, xh, wh, start=(k == 0), stop=False, skip_group_check=True)
                        M(out, xh, wl, start=False, stop=False, skip_group_check=True)
                        ins = M(out, xl, wh, start=False, stop=(k == KP - 1), skip_group_check=True)
                ins.then_inc(full[u].sem, 1)

            def transposes(g, units, nth):
                if xn_ready.any(g, nth):
                    pe.wait_ge(xn_ready.sem, xn_ready.at(g, nth))
                for u in units:
                    if emptied[u].any(g, -1):
                        pe.wait_ge(emptied[u].sem, emptied[u].at(g, -1))
                for u, c, width in zip(units, (0, KA), (KA, KB)):
                    for j in range(TILES):
                        ins = nc.tensor.transpose(bank[UNIT_BANK[u]][0:width, j * H:(j + 1) * H], xn[:, j, c:c + width],
                                                  ident[0:H, 0:H])
                    ins.then_inc(full[u].sem, 1)

            def x_ready(g):
                for u in ("ta", "tb"):
                    pe.wait_ge(emptied[u].sem, emptied[u].at(g))

            def dt(g):
                u = "dt"
                x_ready(g)
                if emptied[u].any(g, -1):
                    pe.wait_ge(emptied[u].sem, emptied[u].at(g, -1))
                c = slice(COL_DT, COL_DT + HEADS)
                for j in range(TILES):
                    t = slice(j * H, (j + 1) * H)
                    ins = five_rows(bank[UNIT_BANK[u]][0:H, j * HEADS:(j + 1) * HEADS],
                                    (w1a_hi[:, c], w1a_lo[:, c], w1b_hi[:, c], w1b_lo[:, c]), xa_hi[:, t], xa_lo[:, t], xb_hl[:, t], True)
                ins.then_inc(full[u].sem, 1)

            def project(g, u):
                c, width = PROJ[u]
                if u == "x0":
                    x_ready(g)
                if emptied[u].any(g, -1):
                    pe.wait_ge(emptied[u].sem, emptied[u].at(g, -1))
                cols = slice(c, c + width)
                five(bank[UNIT_BANK[u]][0:width, 0:T], w1a_hi[:, cols], w1a_lo[:, cols], w1b_hi[:, cols], w1b_lo[:, cols],
                            xa_hi[:, :], xa_lo[:, :], xb_hl[:, :]).then_inc(full[u].sem, 1)

            def cum(g):
                u = "cum"
                pe.wait_ge(dta_ready.sem, dta_ready.at(g, 1))
                if emptied[u].any(g, -1):
                    pe.wait_ge(emptied[u].sem, emptied[u].at(g, -1))
                for s in range(SEQS):
                    for half in range(2):
                        out = bank[UNIT_BANK[u]][0:HEADS, s * TOKENS + half * H:s * TOKENS + (half + 1) * H]
                        if half:
                            M(out, dta[:, 2 * s, :], ones[0:H, :], start=True, stop=False, skip_group_check=True)
                        ins = M(out, dta[:, 2 * s + half, :], upper[:, :], start=(half == 0), stop=True, skip_group_check=True)
                ins.then_inc(full[u].sem, 1)

            def cumt(g):
                u = "cumt"
                pe.wait_ge(cum_ready.sem, cum_ready.at(g, 1))
                if emptied[u].any(g, -1):
                    pe.wait_ge(emptied[u].sem, emptied[u].at(g, -1))
                for j in range(TILES):
                    ins = M(bank[UNIT_BANK[u]][0:H, j * HEADS:(j + 1) * HEADS], cumf[:, j * H:(j + 1) * H],
                            ident[0:HEADS, 0:HEADS], start=True, stop=True, skip_group_check=True)
                ins.then_inc(full[u].sem, 1)

            def cb_products(g, s):
                u = f"g{s}"
                pe.wait_ge(silu_ready.sem, silu_ready.at(g, 4))
                if emptied[u].any(g, -1):
                    pe.wait_ge(emptied[u].sem, emptied[u].at(g, -1))
                t0 = s * TOKENS
                M(bank[UNIT_BANK[u]][0:H, 0:TOKENS], bs[:, t0:t0 + H], cs[:, t0:t0 + TOKENS], start=True, stop=True,
                  skip_group_check=True)
                M(bank[UNIT_BANK[u]][0:H, TOKENS:CAUSAL], bs[:, t0 + H:t0 + TOKENS], cs[:, t0 + H:t0 + TOKENS], start=True,
                         stop=True, skip_group_check=True).then_inc(full[u].sem, 1)

            def x_rows(g, j):
                u = f"xt{j}"
                pe.wait_ge(silu_ready.sem, silu_ready.at(g, NI))
                if emptied[u].any(g, -1):
                    pe.wait_ge(emptied[u].sem, emptied[u].at(g, -1))
                for k in range(NI):
                    ins = nc.tensor.transpose(bank[UNIT_BANK[u]][0:H, k * 128:(k + 1) * 128], xs[:, k, j * H:(j + 1) * H], ident[:, :])
                ins.then_inc(full[u].sem, 1)

            def broadcast(g, h):
                u = f"cb{h}"
                pe.wait_ge(cum_ready.sem, cum_ready.at(g, 2))
                if emptied[u].any(g, -1):
                    pe.wait_ge(emptied[u].sem, emptied[u].at(g, -1))
                M(bank[UNIT_BANK[u]][0:H, 0:T], pick[:, h, :], cumpart[:, :], start=True, stop=True, skip_group_check=True).then_inc(full[u].sem, 1)

            def scan_out(g, n):
                u = f"y{n}"
                pe.wait_ge(wgt_ready.sem, wgt_ready.at(g, 2 * n + 2))
                for j in range(TILES):
                    pe.wait_ge(emptied[f"xt{j}"].sem, emptied[f"xt{j}"].at(g))
                if emptied[u].any(g, -1):
                    pe.wait_ge(emptied[u].sem, emptied[u].at(g, -1))
                for head in (2 * n, 2 * n + 1):
                    rows = slice((head % 2) * HD, (head % 2 + 1) * HD)
                    cols = slice(head * HD, (head + 1) * HD)
                    for s in range(SEQS):
                        t0 = s * TOKENS
                        M(bank[UNIT_BANK[u]][rows, t0:t0 + TOKENS], xdt[:, 2 * s, cols], wgt[:, head, s, 0:TOKENS],
                          start=(s == 0), stop=False, skip_group_check=True)
                        ins = M(bank[UNIT_BANK[u]][rows, t0 + H:t0 + TOKENS], xdt[:, 2 * s + 1, cols], wgt[:, head, s, TOKENS:CAUSAL],
                                start=False, stop=True, skip_group_check=True)
                ins.then_inc(full[u].sem, 1)

            def out_project(g, n):
                u, c, width = (("oa", 0, KA), ("ob", KA, KB))[n]
                pe.wait_ge(y2_ready.sem, y2_ready.at(g, NI))
                if emptied[u].any(g, -1):
                    pe.wait_ge(emptied[u].sem, emptied[u].at(g, -1))
                for k in range(NI):
                    ins = M(bank[UNIT_BANK[u]][0:width, 0:T], outp[:, k * MODEL + c:k * MODEL + c + width], y2[:, k, :],
                            start=(k == 0), stop=(k == NI - 1), skip_group_check=True)
                ins.then_inc(full[u].sem, 1)

            def square_sums(g):
                u = "ss"
                pe.wait_ge(sqsum_ready.sem, sqsum_ready.at(g, 1))
                if emptied[u].any(g, -1):
                    pe.wait_ge(emptied[u].sem, emptied[u].at(g, -1))
                for j in range(TILES):
                    ins = M(bank[UNIT_BANK[u]][0:H, j:j + 1], sq[:, 0, j * H:(j + 1) * H], ones[:, 0:1], start=True, stop=True,
                            skip_group_check=True)
                ins.then_inc(full[u].sem, 1)

            def out_rows(g, s):
                u = f"ow{s}"
                pe.wait_ge(emptied["oa"].sem, emptied["oa"].at(g))
                pe.wait_ge(emptied["ob"].sem, emptied["ob"].at(g))
                if emptied[u].any(g, -1):
                    pe.wait_ge(emptied[u].sem, emptied[u].at(g, -1))
                for j in (2 * s, 2 * s + 1):
                    out = bank[UNIT_BANK[u]][0:H, (j % 2) * MODEL:(j % 2 + 1) * MODEL]
                    t = slice(j * H, (j + 1) * H)
                    M(out, gated[0:KA, 0, t], owa[:, :], start=True, stop=False, skip_group_check=True)
                    ins = M(out, gated[0:KB, 1, t], owb[:, :], start=False, stop=True, skip_group_check=True)
                ins.then_inc(full[u].sem, 1)

            def f_ready(g):
                for u in ("t2a", "t2b"):
                    pe.wait_ge(emptied[u].sem, emptied[u].at(g))

            def route(g):
                u = "route"
                f_ready(g)
                if emptied[u].any(g, -1):
                    pe.wait_ge(emptied[u].sem, emptied[u].at(g, -1))
                for j in range(TILES):
                    t = slice(j * H, (j + 1) * H)
                    ins = five_rows(bank[UNIT_BANK[u]][0:H, j * ROUTED:(j + 1) * ROUTED],
                                    (ra_hi[:, :], ra_lo[:, :], rb_hi[:, :], rb_lo[:, :]), fa_hi[:, t], fa_lo[:, t], fb_hl[:, t], True)
                ins.then_inc(full[u].sem, 1)

            def expert(g, t):
                if t == FTILES:
                    return
                if t == 0:
                    f_ready(g)
                if fh_ready.any(g, t + 1 - 2):
                    pe.wait_ge(fh_ready.sem, fh_ready.at(g, t + 1 - 2))
                cols = slice(t * 128, (t + 1) * 128)
                for w, (ps, full) in enumerate(((gate_ps, gate_full), (up_ps, up_full))):
                    five(ps[t % 2][:, 0:T], gua_hi[w][:, cols], gua_lo[w][:, cols], gub_hi[w][:, cols], gub_lo[w][:, cols],
                         fa_hi[:, :], fa_lo[:, :], fb_hl[:, :]).then_inc(full.sem, 1)

            def down(g, e, j):
                n = TILES * e + j
                if j == 0:
                    pe.wait_ge(flo_ready.sem, flo_ready.at(g, NF * (e + 1)))
                    pe.wait_ge(fhi_ready.sem, fhi_ready.at(g, NF * (e + 1)))
                if down_free.any(g, n + 1 - 2):
                    pe.wait_ge(down_free.sem, down_free.at(g, n + 1 - 2))
                t = slice(j * H, (j + 1) * H)
                out = down_ps[j % 2][0:H, 0:MODEL]
                for k in range(NF):
                    w = slice((NF * e + k) * MODEL, (NF * e + k + 1) * MODEL)
                    hi, lo = fh_hi[:, e % 2, k, t], fh_lo[:, e % 2, k, t]
                    M(out, hi, down_hi[:, w], start=(k == 0), stop=False, skip_group_check=True)
                    M(out, hi, down_lo[:, w], start=False, stop=False, skip_group_check=True)
                    ins = M(out, lo, down_hi[:, w], start=False, stop=(k == NF - 1), skip_group_check=True)
                ins.then_inc(down_full.sem, 1)

            steps = {"ta": lambda g: transposes(g, ("ta", "tb"), 1), "t2a": lambda g: transposes(g, ("t2a", "t2b"), 2),
                     "dt": dt, "cum": cum, "cumt": cumt, "ss": square_sums, "route": route,
                     "oa": lambda g: out_project(g, 0), "ob": lambda g: out_project(g, 1)}
            for u in PROJ:
                steps[u] = lambda g, u=u: project(g, u)
            for s in range(SEQS):
                steps[f"embed{s}"] = lambda g, s=s: embed(g, s)
                steps[f"g{s}"] = lambda g, s=s: cb_products(g, s)
                steps[f"ow{s}"] = lambda g, s=s: out_rows(g, s)
            for j in range(TILES):
                steps[f"xt{j}"] = lambda g, j=j: x_rows(g, j)
            for h in range(HEADS):
                steps[f"cb{h}"] = lambda g, h=h: broadcast(g, h)
            for n in range(NI):
                steps[f"y{n}"] = lambda g, n=n: scan_out(g, n)
            for t in range(FTILES + 1):
                steps[f"f{t}"] = lambda g, t=t: expert(g, t)
            for e in range(EXPERTS):
                for j in range(TILES):
                    steps[f"d{e}{j}"] = lambda g, e=e, j=j: down(g, e, j)
            turns(pe, steps)


def kernel(**inputs):
    import numpy as np
    import concourse.bacc as bacc
    from concourse.bass_utils import run_bass_kernel_spmd

    def rows(a, n):
        return np.ascontiguousarray(np.broadcast_to(a.reshape(1, -1), (n, a.size)))

    def by_tile(a, tiles):
        return np.ascontiguousarray(a.reshape(tiles, 128, -1).transpose(1, 0, 2).reshape(128, -1))

    a = {k.removeprefix("L0_"): np.asarray(v) for k, v in inputs.items()}
    side, p = 14, 16
    x = a["x"].reshape(GROUPS, SEQS, 3, side, p, side, p).transpose(0, 2, 4, 6, 1, 3, 5)
    x = x.reshape(GROUPS, KP, 128, T).transpose(0, 2, 1, 3).reshape(GROUPS, 128, KP * T)

    def experts(shared, routed):
        return np.concatenate([a[shared][None], a[routed]], 0)

    arrays = {
        "patches": x,
        "tok_w": by_tile(a["tok_W"].T, KP),
        "tok_b": rows(a["tok_b"], H),
        "pos": a["tok_pos"].reshape(2, H, MODEL).transpose(1, 0, 2).reshape(H, 2 * MODEL),
        "ln_w": a["attn_ln_w"].reshape(MODEL, 1),
        "ln_b": a["attn_ln_b"].reshape(MODEL, 1),
        "w1": np.concatenate([a["attn_in_proj_w"], a["attn_gate_w"]], 1),
        "conv_w": a["attn_conv_w"].reshape(4, 128, TAPS).transpose(1, 0, 2),
        "conv_b": a["attn_conv_b"].reshape(4, 128).T,
        "dt_bias": rows(a["attn_dt_bias"], H),
        "A_log": rows(a["attn_A_log"], H),
        "D": np.repeat(a["attn_D_param"], HD).reshape(NI, 128).T,
        "rms_w": a["attn_rms_w"].reshape(NI, 128).T,
        "out_proj": by_tile(a["attn_out_proj_w"], NI),
        "gate_b": a["attn_gate_b"].reshape(MODEL, 1),
        "out_w": a["attn_out_w"],
        "out_b": rows(a["attn_out_b"], H),
        "experts_gate": experts("ffn_shared_gate", "ffn_routed_gate").transpose(1, 0, 2).reshape(MODEL, EXPERTS * FF),
        "experts_up": experts("ffn_shared_up", "ffn_routed_up").transpose(1, 0, 2).reshape(MODEL, EXPERTS * FF),
        "down": by_tile(experts("ffn_shared_down", "ffn_routed_down").reshape(EXPERTS * FF, MODEL), FTILES),
        "router_w": a["ffn_router_w"],
        "routing_bias": rows(a["ffn_routing_bias"], H),
    }
    arrays = {k: np.ascontiguousarray(v) for k, v in arrays.items()}
    nc = bacc.Bacc("TRN2", target_bir_lowering=False, num_devices=1)
    dram = {k: nc.dram_tensor(f"in_{k}", v.shape, F32, kind="ExternalInput").ap() for k, v in arrays.items()}
    dram["out"] = nc.dram_tensor("out", [GROUPS, H, TILES * MODEL], F32, kind="ExternalOutput").ap()
    build(nc, dram)
    out = run_bass_kernel_spmd(nc, [{f"in_{k}": v for k, v in arrays.items()}], core_ids=[0]).results[0]["out"]
    out = out.reshape(GROUPS, H, SEQS, 2, MODEL).transpose(0, 2, 3, 1, 4)
    return np.ascontiguousarray(out.reshape(BATCH, TOKENS, MODEL))
```

```python
from contextlib import ExitStack

import concourse.bass as bass
from concourse import mybir
from concourse.alu_op_type import AluOpType as ALU

F32 = mybir.dt.float32
F16 = mybir.dt.float16
BF16 = mybir.dt.bfloat16
ACT = mybir.ActivationFunctionType

BATCH, TOKENS, MODEL = 128, 196, 192
SEQS = 2
GROUPS = BATCH // SEQS
T = SEQS * TOKENS
H = TOKENS // 2
TILES = T // H
KA, KB = 128, 64
PATCH = 768
KP = PATCH // 128
INNER, STATE, HEADS, HD = 384, 64, 6, 64
TAPS = 4
NI = INNER // 128
EXPERTS = 4
ROUTED = 3
FF = 384
NF = FF // 128
FTILES = EXPERTS * NF
EPS = 1e-5
CAUSAL = TOKENS + H
WSCALE = 64.0

COL_Z, COL_X, COL_BC, COL_DT, COL_GATE = 0, 384, 768, 896, 902
W1_COLS = COL_GATE + MODEL
PROJ = {"z0": (0, 128), "z1": (128, 128), "z2": (256, 128), "x0": (384, 128), "x1": (512, 128), "x2": (640, 128),
        "bc": (COL_BC, 128), "ga": (COL_GATE, KA), "gb": (COL_GATE + KA, KB)}
PROJ_AT = {name: n for n, name in enumerate(PROJ)}

ORDER = """
    xt0 f0 embed0 f1 embed1 g0 norm1 xt1 f2 g1 f3 xt2 cb0 cb1 cb2 ta w0 w1 tb d00 w2 xt3 dt cb3 f4 f5 soft x0 x1
    f6 w3 cb4 x2 w4 cb5 d01 bc conv0 y0 w5 conv1 d10 y1 cum y2 conv2 silu0 f7 cpart silu1 d11 oa ob silu2 conv3
    gate silu3 f8 ss f9 ow0 ow1 f10 norm2 z0 z1 f11 f12 split d20 z2 sz0 d21 ga gb t2a t2b d30 store sz1 base
    route d31 sz2
""".split()
FRONT, BACK, LATE = 0, 1, 2


def stage_of(step):
    if step == "store" or step[0] in "fd" and step[1:].isdigit():
        return LATE
    back = step.rstrip("0123456789") in ("g", "cb", "w", "xt", "y", "gate", "oa", "ob", "ss", "ow", "norm", "t2a", "t2b", "route")
    return BACK if back and step != "norm1" else FRONT


OTHER_STEPS = ("norm", "soft", "conv", "silu", "w", "gate", "split", "store", "base", "sz")
MIX_BANKS = 3
UNITS = [u for u in ORDER if stage_of(u) != LATE and u.rstrip("0123456789") not in OTHER_STEPS]
UNIT_BANK = {u: n % MIX_BANKS for n, u in enumerate(UNITS)}


def nth_unit(unit, stages):
    same = [u for u in UNITS if UNIT_BANK[u] == UNIT_BANK[unit] and stage_of(u) in stages]
    return same.index(unit) + 1


def latest(*units, before=None):
    banks = [b for b in range(MIX_BANKS) if before is None or b != UNIT_BANK[before]]
    return [max((u for u in units if UNIT_BANK[u] == b), key=UNITS.index) for b in banks
            if any(UNIT_BANK[u] == b for u in units)]


CONSTS = 15


class Count:

    def __init__(self, sem, per):
        self.sem, self.per = sem, per

    def at(self, group, nth):
        i, off = group
        return i * self.per + (self.per * off + nth)

    def any(self, group, nth):
        i, off = group
        return not isinstance(i, int) or self.per * (i + off) + nth > 0


class Unit(Count):

    def __init__(self, sem, unit):
        bank = [stage_of(u) for u in UNITS if UNIT_BANK[u] == UNIT_BANK[unit]]
        super().__init__(sem, len(bank))
        self.stage, self.backs = stage_of(unit), bank.count(BACK)
        self.first = nth_unit(unit, (FRONT,)) if self.stage == FRONT else 0
        self.nth = nth_unit(unit, (FRONT, BACK))
        self.last = nth_unit(unit, (BACK,)) if self.stage == BACK else 0

    def at(self, group, back=0):
        i, off = group
        off += self.stage
        if isinstance(i, int) and i + off == 0:
            return self.first + back
        nth = self.last if isinstance(i, int) and i + off == GROUPS else self.nth
        return i * self.per + (self.per * off - self.backs + nth + back)

    def any(self, group, back=0):
        i, off = group
        return not isinstance(i, int) or (i + off >= 0 and self.at(group, back) > 0)


class Chain(Count):

    def __init__(self, sem):
        super().__init__(sem, 0)
        self.marks = 0

    def begin(self, group):
        if self.marks:
            self.per = self.marks
        self.marks = 0
        self.group = group

    def mark(self):
        self.marks += 1
        return self.sem

    def now(self):
        return self.at(self.group, self.marks)


def build(nc, D):
    with ExitStack() as ctx:
        def sb(name, shape, dt=F32):
            return ctx.enter_context(nc.sbuf_tensor(name, shape, dt))

        def sem(name):
            return ctx.enter_context(nc.semaphore(name))

        bank = [ctx.enter_context(nc.psum_tensor(f"mix{b}", [128, 512], F32)) for b in range(MIX_BANKS)]
        bankb = [b[:, :].bitcast(BF16) for b in bank]
        gate_ps = [ctx.enter_context(nc.psum_tensor(f"gate{b}", [128, 512], F32)) for b in range(2)]
        up_ps = [ctx.enter_context(nc.psum_tensor(f"up{b}", [128, 512], F32)) for b in range(2)]
        down_ps = ctx.enter_context(nc.psum_tensor("down", [128, 512], F32))

        ident = sb("ident", [128, 128])
        identb = sb("identb", [128, 128], BF16)
        upper = sb("upper", [H, H])
        ones = sb("ones", [128, H])
        causal = sb("causal", [H, CAUSAL])
        pick = sb("pick", [96, HEADS, H], BF16)
        power = sb("power", [128, 8])
        zb, zt = sb("zb", [128, NI, T]), sb("zt", [128, NI, T])
        w1a_raw = zb[:, :, :].rearrange("p k t -> p (k t)")[:, 0:W1_COLS]
        w1b_raw = zt[:, :, :].rearrange("p k t -> p (k t)")[:, 0:W1_COLS]
        w1a_hi, w1a_lo = sb("w1a_hi", [KA, W1_COLS], F16), sb("w1a_lo", [KA, W1_COLS], F16)
        w1b_hi, w1b_lo = sb("w1b_hi", [128, W1_COLS], F16), sb("w1b_lo", [KB, W1_COLS], F16)
        lnwa, lnwb, lnba, lnbb = sb("lnwa", [KA, 1]), sb("lnwb", [128, 1]), sb("lnba", [KA, 1]), sb("lnbb", [KB, 1])
        conv = sb("conv", [128, 4, SEQS, TOKENS])
        wf_raw = conv[:, :, :, :].rearrange("p k s t -> p (k s t)")[:, 0:EXPERTS * FF]
        gua_hi = [sb(f"{n}a_hi", [KA, EXPERTS * FF], F16) for n in ("wg", "wu")]
        gua_lo = [sb(f"{n}a_lo", [KA, EXPERTS * FF], F16) for n in ("wg", "wu")]
        gub_hi = [sb(f"{n}b_hi", [128, EXPERTS * FF], F16) for n in ("wg", "wu")]
        gub_lo = [sb(f"{n}b_lo", [KB, EXPERTS * FF], F16) for n in ("wg", "wu")]
        wgt_rows = sb("wgt", [128, HEADS, SEQS, CAUSAL])
        wgt = wgt_rows[0:H, :, :, :]
        down_raw = wgt_rows[:, :, :, :].rearrange("p h s n -> p (h s n)")[:, 0:FTILES * MODEL]
        down_hi, down_lo = sb("down_hi", [128, FTILES * MODEL], F16), sb("down_lo", [128, FTILES * MODEL], F16)
        tok_hi, tok_lo = sb("tok_hi", [128, KP * MODEL], F16), sb("tok_lo", [128, KP * MODEL], F16)
        outp = sb("outp", [128, NI * MODEL])
        rms = sb("rms", [128, NI])
        owa, owb = sb("owa", [KA, MODEL]), sb("owb", [KB, MODEL])
        ra_raw, rb_raw = sb("ra_raw", [KA, ROUTED]), sb("rb_raw", [128, ROUTED])
        ra_hi, ra_lo = sb("ra_hi", [KA, ROUTED], F16), sb("ra_lo", [KA, ROUTED], F16)
        rb_hi, rb_lo = sb("rb_hi", [128, ROUTED], F16), sb("rb_lo", [KB, ROUTED], F16)
        pos = sb("pos", [H, 2 * MODEL])
        tokb = sb("tokb", [H, MODEL])
        outb = sb("outb", [H, MODEL])
        convw, convb = sb("convw", [128, 4, TAPS]), sb("convb", [128, 4])
        dpar, dhalf = sb("dpar", [128, NI]), sb("dhalf", [128, NI])
        alog, aneg = sb("alog", [H, HEADS]), sb("aneg", [H, HEADS])
        dtb, dtbias = sb("dtb", [H, HEADS]), sb("dtbias", [H, HEADS])
        gba, gbb = sb("gba", [KA, 1]), sb("gbb", [KB, 1])
        rbias = sb("rbias", [H, ROUTED])
        pbias = sb("pbias", [128, len(PROJ)])
        gbias = sb("gbias", [128, 2])

        patches = sb("patches", [128, KP * T])
        pat_hi, pat_lo = sb("pat_hi", [128, KP * T], F16), sb("pat_lo", [128, KP * T], F16)
        h1 = sb("h1", [H, TILES, MODEL])
        base = sb("base", [H, TILES, MODEL])
        xn = sb("xn", [H, TILES, MODEL])
        xn2 = sb("xn2", [H, TILES, MODEL])
        stats, small = sb("stats", [H, TILES, 6]), sb("small", [H, 5, TILES])
        roots_in, roots = sb("roots_in", [H, 8]), sb("roots", [H, 8])
        stats2, small2 = sb("stats2", [H, TILES, 6]), sb("small2", [H, 5, TILES])
        roots2_in, roots2 = sb("roots2_in", [H, TILES]), sb("roots2", [H, TILES])
        xa_hi, xa_lo, xb_hl = sb("xa_hi", [KA, T], F16), sb("xa_lo", [KA, T], F16), sb("xb_hl", [128, T], F16)
        dt_raw = sb("dt_raw", [H, TILES, HEADS])
        sp = sb("sp", [H, 8, TILES * HEADS])
        dta = sb("dta", [H, TILES, HEADS])
        dth = sb("dth", [H, TILES, HEADS])
        csum = sb("csum", [H, TILES, HEADS])
        crest = sb("crest", [H, TILES, HEADS])
        cpt = sb("cpt", [H, TILES, 96], BF16)
        cumpart = sb("cumpart", [96, T], BF16)
        ncum = sb("ncum", [H, TILES, HEADS])
        xpad = sb("xpad", [128, 4, SEQS, TAPS - 1 + TOKENS])
        convt = sb("convt", [128, 4, SEQS, TOKENS])
        xs = sb("xs", [128, NI, T])
        bs, cs = sb("bs", [STATE, T]), sb("cs", [STATE, T])
        zs = sb("zs", [128, NI, T])
        gt = sb("gt", [128, 2, T])
        gm = sb("gm", [H, SEQS, CAUSAL])
        xdt = sb("xdt", [H, TILES, INNER])
        decay = sb("decay", [H, 2, SEQS, CAUSAL])
        y1 = sb("y1", [128, NI, T])
        y2 = sb("y2", [128, NI, T])
        sq = sb("sq", [128, NI, T])
        gated = sb("gated", [128, 2, T])
        rinv_in, rinv = sb("rinv_in", [H, TILES]), sb("rinv", [H, TILES])
        h2 = sb("h2", [H, TILES, MODEL])
        fa_hi, fa_lo, fb_hl = sb("fa_hi", [KA, T], F16), sb("fa_lo", [KA, T], F16), sb("fb_hl", [128, T], F16)
        rl = sb("rl", [H, TILES, ROUTED])
        rs = sb("rs", [H, 6, TILES, ROUTED])
        comb = sb("comb", [H, TILES, ROUTED])
        ft = sb("ft", [128, 2, T])
        fg = sb("fg", [128, 2, T])
        fh = sb("fh", [128, 2, T])
        fh_hi, fh_lo = sb("fh_hi", [128, 2, NF, T], F16), sb("fh_lo", [128, 2, NF, T], F16)
        acc = sb("acc", [H, TILES, MODEL])

        s_staged = sem("staging_loaded")
        s_load, s_const, s_prep = sem("weights_loaded"), sem("constants_ready"), sem("prologue_step")
        s_wfree, s_bias = sem("staging_split"), sem("bias_products")
        bank_full, bank_emptied = ([sem(f"mix{b}_{state}") for b in range(MIX_BANKS)] for state in ("full", "emptied"))
        full = {u: Unit(bank_full[UNIT_BANK[u]], u) for u in UNITS}
        emptied = {u: Unit(bank_emptied[UNIT_BANK[u]], u) for u in UNITS}
        patch_in = Count(sem("patches_loaded"), 16)
        patch_hi = Count(sem("patches_hi"), 1)
        patch_lo = Count(sem("patches_lo"), 1)
        roots_asked, roots_done = Count(sem("roots1_asked"), 1), Count(sem("roots1_done"), 1)
        roots2_asked, roots2_done = Count(sem("roots2_asked"), 1), Count(sem("roots2_done"), 2)
        xn_ready, xn2_ready = Count(sem("xn_ready"), 1), Count(sem("xn2_ready"), 1)
        shift_ready = Count(sem("shift_ready"), 1)
        normed = Count(sem("residual_norm_ready"), 1)
        base_ready = Count(sem("base_ready"), 1)
        hi_ready, hi2_ready = Count(sem("projection_hi_ready"), 2), Count(sem("expert_hi_ready"), 2)
        soft_in, soft_e = Count(sem("softplus_in"), 1), Count(sem("softplus_exp"), 1)
        dta_ready = Count(sem("dta_ready"), 1)
        ncum_ready = Count(sem("ncum_ready"), 1)
        cpt_ready = Count(sem("cum_parts_ready"), 1)
        tap0_ready = Count(sem("first_tap_ready"), 4)
        zs_ready = Count(sem("zs_ready"), NI)
        conv_ready, convt_ready = Count(sem("conv_ready"), 4), Count(sem("conv_tanh"), 4)
        silu_ready = Count(sem("silu_ready"), 4)
        decay_ready, wgt_ready = Count(sem("decay_ready"), HEADS), Count(sem("wgt_ready"), HEADS)
        y2_ready = Count(sem("y2_ready"), NI)
        sq_ready, sqsum_ready = Count(sem("squares"), NI), Count(sem("square_sums"), 1)
        router_e = Count(sem("router_exp"), 1)
        gate_full, up_full = Count(sem("gate_full"), FTILES), Count(sem("up_full"), FTILES)
        ft_ready = Count(sem("expert_tanh"), FTILES)
        fh_ready = Count(sem("fh_ready"), FTILES)
        fhi_ready, flo_ready = Count(sem("fh_hi_ready"), FTILES), Count(sem("fh_lo_ready"), FTILES)
        down_full, down_free = Count(sem("down_full"), SEQS * EXPERTS), Count(sem("down_emptied"), SEQS * EXPERTS)
        stored = Count(sem("stored"), 16)
        dve_front, dve_back, dve_late = Chain(sem("dve_front_step")), Chain(sem("dve_back_step")), Chain(sem("dve_late_step"))
        act_front = Chain(sem("act_front_step"))
        pool_front, pool_back = Chain(sem("pool_front_step")), Chain(sem("pool_back_step"))

        def before(g):
            return g[0], g[1] - 1

        def turns(eng, steps, begin=lambda *stages: None):
            def turn(i, front=True, back=True, late=True, split=True):
                runs = (front, back, late)
                begin(i, *runs)
                for name in ORDER:
                    if name not in steps:
                        continue
                    if name == "split":
                        if split:
                            steps[name]((i, 1))
                    elif runs[stage_of(name)]:
                        steps[name]((i, -stage_of(name)))
            turn(0, back=False, late=False)
            turn(1, late=False)
            turn(2)
            with eng.Fori(3, GROUPS - 1) as i:
                turn(i)
            turn(GROUPS - 1, split=False)
            turn(GROUPS, front=False, split=False)
            turn(GROUPS + 1, front=False, back=False, split=False)

        block = ctx.enter_context(nc.Block())

        loads = [
            (w1a_raw, D["w1"][0:KA, :]), (w1b_raw[0:KB, :], D["w1"][KA:MODEL, :]), (w1b_raw[KB:128, :], D["w1"][KA:MODEL, :]),
            (lnwa, D["ln_w"][0:KA, :]), (lnwb[0:KB, :], D["ln_w"][KA:MODEL, :]), (lnwb[KB:128, :], D["ln_w"][KA:MODEL, :]),
            (lnba, D["ln_b"][0:KA, :]), (lnbb, D["ln_b"][KA:MODEL, :]),
            (down_raw, D["down"]), (outp, D["out_proj"]), (rms, D["rms_w"]), (owa, D["out_w"][0:KA, :]), (owb, D["out_w"][KA:MODEL, :]),
            (ra_raw, D["router_w"][0:KA, :]), (rb_raw[0:KB, :], D["router_w"][KA:MODEL, :]), (rb_raw[KB:128, :], D["router_w"][KA:MODEL, :]),
            (pos, D["pos"]), (tokb, D["tok_b"]), (outb, D["out_b"]), (convw, D["conv_w"]), (convb, D["conv_b"]), (dpar, D["D"]),
            (alog, D["A_log"]), (dtb, D["dt_bias"]), (gba, D["gate_b"][0:KA, :]), (gbb, D["gate_b"][KA:MODEL, :]), (rbias, D["routing_bias"]),
        ]
        staged = [("tok", D["tok_w"])] + [(f"{n}{p}", D[f"experts_{n}"]) for n in ("gate", "up") for p in "ab"]

        @block.sync
        def _(sp_eng):
            def load_patches(g):
                i, off = g
                if patch_lo.any(g, 0):
                    sp_eng.wait_ge(patch_lo.sem, patch_lo.at(g, 0))
                at = i + off
                src = D["patches"][at] if isinstance(at, int) else D["patches"][bass.ds(at, 1)].rearrange("g p n -> (g p) n")
                sp_eng.dma_start(patches[:, :], src).then_inc(patch_in.sem, 16)

            def store(g):
                i, off = g
                sp_eng.wait_ge(down_free.sem, down_free.at(g, SEQS * EXPERTS))
                at = i + off
                dst = D["out"][at] if isinstance(at, int) else D["out"][bass.ds(at, 1)].rearrange("g p n -> (g p) n")
                sp_eng.dma_start(dst, acc[:, :, :].rearrange("p j n -> p (j n)")).then_inc(stored.sem, 16)

            load_patches((0, 0))
            for n, (dst, src) in enumerate(loads):
                sp_eng.dma_start(dst if isinstance(dst, bass.AP) else dst[:], src).then_inc(s_load, 16)
            for n, (name, src) in enumerate(staged):
                if n:
                    sp_eng.wait_ge(s_wfree, n)
                if name == "tok":
                    sp_eng.dma_start(wf_raw[:, 0:KP * MODEL], src).then_inc(s_staged, 16)
                elif name[-1] == "a":
                    sp_eng.dma_start(wf_raw[:, :], src[0:KA, :]).then_inc(s_staged, 16)
                else:
                    sp_eng.dma_start(wf_raw[0:KB, :], src[KA:MODEL, :]).then_inc(s_staged, 16)
                    sp_eng.dma_start(wf_raw[KB:128, :], src[KA:MODEL, :]).then_inc(s_staged, 16)
            turns(sp_eng, {"embed0": lambda g: None, "split": load_patches, "store": store})
            sp_eng.wait_ge(stored.sem, 16 * GROUPS)

        @block.gpsimd
        def _(pool):
            gp = nc.gpsimd

            fills = ((ident, 0.0), (upper, 1.0), (causal, 0.25), (ones, 1.0), (power, -0.5), (pick, 0.0), (cpt, 0.0),
                     (xpad, 0.0))
            for tensor, value in fills:
                gp.memset(tensor[:], value).then_inc(s_const, 1)
            pool.wait_ge(s_const, len(fills))
            gp.affine_select(out=ident[:, :], in_=ident[:, :], compare_op=ALU.not_equal, fill=1.0, base=0,
                             pattern=[[-1, 128]], channel_multiplier=1).then_inc(s_const, 1)
            pool.wait_ge(s_const, len(fills) + 1)
            for n, part in enumerate((upper[:, :], causal[:, 0:TOKENS], causal[:, TOKENS:CAUSAL])):
                gp.affine_select(out=part, in_=part, compare_op=ALU.is_ge, fill=0.0, base=0,
                                 pattern=[[1, part.shape[1]]], channel_multiplier=-1).then_inc(s_const, 1)
                pool.wait_ge(s_const, len(fills) + 2 + n)
            for n in range(3):
                rows = pick[32 * n:32 * n + 32, :, :]
                gp.affine_select(out=rows, in_=rows, compare_op=ALU.not_equal, fill=1.0, base=0,
                                 pattern=[[-1, HEADS], [0, H]], channel_multiplier=1).then_inc(s_const, 1)
                pool.wait_ge(s_const, len(fills) + 5 + n)

            def split_lo(g):
                pool.wait_ge(patch_hi.sem, patch_hi.at(g, 1))
                gp.tensor_tensor(pat_lo[:, :], patches[:, :], pat_hi[:, :], ALU.subtract).then_inc(patch_lo.sem, 1)

            def norm1(g):
                pool.wait_ge(roots_asked.sem, roots_asked.at(g, 1))
                gp.tensor_tensor(roots[:, :], roots_in[:, :], power[0:H, :], ALU.pow).then_inc(roots_done.sem, 1)

            def add_base(g):
                pool.wait_ge(normed.sem, normed.at(g, 1))
                flat = [t[:, :, :].rearrange("p j n -> p (j n)") for t in (base, h1)]
                gp.tensor_tensor(flat[0], flat[0], flat[1], ALU.add).then_inc(pool_front.mark(), 1)
                pool.wait_ge(pool_front.sem, pool_front.now())
                gp.tensor_tensor(base[:, :, :], base[:, :, :], outb[:, :].unsqueeze(1).to_broadcast([H, TILES, MODEL]),
                                 ALU.add).then_inc(base_ready.sem, 1)

            def gate_y(g, n):
                pool.wait_ge(emptied[f"y{n}"].sem, emptied[f"y{n}"].at(g))
                pool.wait_ge(zs_ready.sem, zs_ready.at(g, n + 1))
                if n == 0 and full["ob"].any(before(g)):
                    pool.wait_ge(full["ob"].sem, full["ob"].at(before(g)))
                    pool.wait_ge(sq_ready.sem, sq_ready.at(g, 0))
                gp.tensor_tensor(y2[:, n, :], y1[:, n, :], zs[:, n, :], ALU.mult).then_inc(y2_ready.sem, 1)

            def sum_squares(g):
                pool.wait_ge(sq_ready.sem, sq_ready.at(g, NI))
                gp.tensor_tensor(sq[:, 0, :], sq[:, 0, :], sq[:, 1, :], ALU.add).then_inc(pool_back.mark(), 1)
                pool.wait_ge(pool_back.sem, pool_back.now())
                gp.tensor_tensor(sq[:, 0, :], sq[:, 0, :], sq[:, 2, :], ALU.add).then_inc(sqsum_ready.sem, 1)

            def ss(g):
                pool.wait_ge(emptied["ss"].sem, emptied["ss"].at(g))
                gp.tensor_tensor(rinv[:, :], rinv_in[:, :], power[0:H, 0:TILES], ALU.pow).then_inc(roots2_done.sem, 1)

            def norm2(g):
                pool.wait_ge(roots2_asked.sem, roots2_asked.at(g, 1))
                gp.tensor_tensor(roots2[:, :], roots2_in[:, :], power[0:H, 0:TILES], ALU.pow).then_inc(roots2_done.sem, 1)

            def lo(g, t):
                if t:
                    pool.wait_ge(fhi_ready.sem, fhi_ready.at(g, t))
                    e, k = divmod(t - 1, NF)
                    gp.tensor_tensor(fh_lo[:, e % 2, k, :], fh[:, (t - 1) % 2, :], fh_hi[:, e % 2, k, :],
                                     ALU.subtract).then_inc(flo_ready.sem, 1)

            steps = {"split": split_lo, "norm1": norm1, "base": add_base, "oa": sum_squares, "ss": ss, "norm2": norm2}
            for n in range(NI):
                steps[f"y{n}"] = lambda g, n=n: gate_y(g, n)
            for t in range(FTILES + 1):
                steps[f"f{t}"] = lambda g, t=t: lo(g, t)
            split_lo((0, 0))

            def begin(i, front, back, late):
                if front:
                    pool_front.begin((i, 0))
                if back:
                    pool_back.begin((i, -1))
            turns(pool, steps, begin)

        @block.scalar
        def _(act):
            A = nc.scalar.activation

            def split_hi(g):
                act.wait_ge(patch_in.sem, patch_in.at(g, 16))
                if not (isinstance(g[0], int) and g == (0, 0)):
                    if full["embed1"].any(before(g)):
                        act.wait_ge(full["embed1"].sem, full["embed1"].at(before(g)))
                A(pat_hi[:, :], patches[:, :], ACT.Copy).then_inc(patch_hi.sem, 1)

            def hi_a(g, u, out, ready):
                act.wait_ge(full[u].sem, full[u].at(g))
                A(out, bank[UNIT_BANK[u]][0:out.shape[0], 0:T], ACT.Copy).then_inc(ready.sem, 1)

            def ta(g):
                if full["gb"].any(before(g)):
                    act.wait_ge(full["gb"].sem, full["gb"].at(before(g)))
                hi_a(g, "ta", xa_hi[:, :], hi_ready)

            def tb(g):
                hi_a(g, "tb", xb_hl[0:KB, :], hi_ready)

            def t2a(g):
                if up_full.any(before(g), FTILES):
                    act.wait_ge(up_full.sem, up_full.at(before(g), FTILES))
                if full["route"].any(before(g)):
                    act.wait_ge(full["route"].sem, full["route"].at(before(g)))
                hi_a(g, "t2a", fa_hi[:, :], hi2_ready)

            def t2b(g):
                hi_a(g, "t2b", fb_hl[0:KB, :], hi2_ready)

            def project_x(g, k):
                u = f"x{k}" if k < NI else "bc"
                act.wait_ge(full[u].sem, full[u].at(g))
                if conv_ready.any(g, k + 1 - 4):
                    act.wait_ge(conv_ready.sem, conv_ready.at(g, k + 1 - 4))
                n = PROJ_AT[u]
                A(xpad[:, k, :, TAPS - 1:], bank[UNIT_BANK[u]][:, 0:T].rearrange("p (s t) -> p s t", s=SEQS),
                  ACT.Identity, bias=pbias[:, n:n + 1], scale=1.0 / WSCALE).then_inc(emptied[u].sem, 1)
                act.wait_ge(emptied[u].sem, emptied[u].at(g))
                if silu_ready.any(g, k + 1 - 4):
                    act.wait_ge(silu_ready.sem, silu_ready.at(g, k + 1 - 4))
                A(conv[:, k, :, :], xpad[:, k, :, 0:TOKENS], ACT.Identity, bias=convb[:, k:k + 1],
                  scale=convw[:, k, 0:1]).then_inc(tap0_ready.sem, 1)

            def cum_parts(g):
                act.wait_ge(full["cpart"].sem, full["cpart"].at(g))
                if full["cb5"].any(before(g)):
                    act.wait_ge(full["cb5"].sem, full["cb5"].at(before(g)))
                A(cumpart[:, :], bankb[UNIT_BANK["cpart"]][0:96, 0:T], ACT.Copy).then_inc(emptied["cpart"].sem, 1)

            def norm_residual(g):
                act.wait_ge(shift_ready.sem, shift_ready.at(g, 1))
                if emptied["ow1"].any(before(g)):
                    act.wait_ge(emptied["ow1"].sem, emptied["ow1"].at(before(g)))
                for j in range(TILES):
                    ins = A(base[:, j, :], h1[:, j, :], ACT.Identity, bias=small[:, 4, j:j + 1], scale=roots[:, j:j + 1])
                ins.then_inc(normed.sem, 1)

            def tanh_conv(g, k):
                act.wait_ge(conv_ready.sem, conv_ready.at(g, k + 1))
                if silu_ready.any(g, k + 1 - 4):
                    act.wait_ge(silu_ready.sem, silu_ready.at(g, k + 1 - 4))
                A(convt[:, k, :, :], conv[:, k, :, :], ACT.Tanh, scale=0.5).then_inc(convt_ready.sem, 1)

            def project_z(g, k):
                u = f"z{k}"
                act.wait_ge(full[u].sem, full[u].at(g))
                if zs_ready.any(g, k + 1 - NI):
                    act.wait_ge(zs_ready.sem, zs_ready.at(g, k + 1 - NI))
                n = PROJ_AT[u]
                A(zb[:, k, :], bank[UNIT_BANK[u]][:, 0:T], ACT.Identity, bias=pbias[:, n:n + 1],
                  scale=1.0 / WSCALE).then_inc(act_front.mark(), 1)
                act.wait_ge(act_front.sem, act_front.now())
                A(zt[:, k, :], zb[:, k, :], ACT.Tanh, scale=0.5).then_inc(emptied[u].sem, 1)

            def gate_tanh(g, k):
                u = ("ga", "gb")[k]
                rows = (KA, KB)[k]
                act.wait_ge(full[u].sem, full[u].at(g))
                if emptied[("oa", "ob")[k]].any(before(g)):
                    act.wait_ge(emptied[("oa", "ob")[k]].sem, emptied[("oa", "ob")[k]].at(before(g)))
                A(gt[0:rows, k, :], bank[UNIT_BANK[u]][0:rows, 0:T], ACT.Tanh, bias=gbias[0:rows, k:k + 1],
                  scale=0.5 / WSCALE).then_inc(emptied[u].sem, 1)

            def soft(g):
                act.wait_ge(soft_in.sem, soft_in.at(g, 1))
                A(sp[:, 1, :], sp[:, 0, :], ACT.Exp, scale=-1.0).then_inc(soft_e.sem, 1)

            def decays(g, h):
                u = f"cb{h}"
                act.wait_ge(full[u].sem, full[u].at(g))
                if h == 0:
                    act.wait_ge(ncum_ready.sem, ncum_ready.at(g, 1))
                if wgt_ready.any(g, h + 1 - 2):
                    act.wait_ge(wgt_ready.sem, wgt_ready.at(g, h + 1 - 2))
                ps = bank[UNIT_BANK[u]]
                for s in range(SEQS):
                    t0 = s * TOKENS
                    A(decay[:, h % 2, s, 0:TOKENS], ps[0:H, t0:t0 + TOKENS], ACT.Exp, bias=ncum[:, 2 * s, h:h + 1])
                    ins = A(decay[:, h % 2, s, TOKENS:CAUSAL], ps[0:H, t0 + H:t0 + TOKENS], ACT.Exp,
                            bias=ncum[:, 2 * s + 1, h:h + 1])
                ins.then_inc(emptied[u].sem, 1)

            def square(g, m):
                act.wait_ge(y2_ready.sem, y2_ready.at(g, m + 1))
                if m == 0:
                    if full["ss"].any(before(g)):
                        act.wait_ge(full["ss"].sem, full["ss"].at(before(g)))
                A(sq[:, m, :], y2[:, m, :], ACT.Square).then_inc(sq_ready.sem, 1)

            def expert(g, t):
                if t < FTILES:
                    act.wait_ge(gate_full.sem, gate_full.at(g, t + 1))
                    if fh_ready.any(g, t + 1 - 2):
                        act.wait_ge(fh_ready.sem, fh_ready.at(g, t + 1 - 2))
                    A(ft[:, t % 2, :], gate_ps[t % 2][:, 0:T], ACT.Tanh, scale=0.5).then_inc(ft_ready.sem, 1)
                if t:
                    e, k = divmod(t - 1, NF)
                    act.wait_ge(fh_ready.sem, fh_ready.at(g, t))
                    if down_full.any(g, SEQS * (e - 1)):
                        act.wait_ge(down_full.sem, down_full.at(g, SEQS * (e - 1)))
                    A(fh_hi[:, e % 2, k, :], fh[:, (t - 1) % 2, :], ACT.Copy).then_inc(fhi_ready.sem, 1)

            def route_exp(g):
                act.wait_ge(emptied["route"].sem, emptied["route"].at(g))
                A(rs[:, 0, :, :], rl[:, :, :], ACT.Exp, scale=-1.0).then_inc(router_e.sem, 1)

            steps = {"ta": ta, "tb": tb, "t2a": t2a, "t2b": t2b, "soft": soft, "route": route_exp, "split": split_hi,
                     "cpart": cum_parts, "base": norm_residual,
                     "oa": lambda g: [square(g, m) for m in range(NI)],
                     "ga": lambda g: gate_tanh(g, 0), "gb": lambda g: gate_tanh(g, 1)}
            for k in range(4):
                steps[f"x{k}" if k < NI else "bc"] = lambda g, k=k: project_x(g, k)
                steps[f"conv{k}"] = lambda g, k=k: tanh_conv(g, k)
            for k in range(NI):
                steps[f"z{k}"] = lambda g, k=k: project_z(g, k)
            for h in range(HEADS):
                steps[f"cb{h}"] = lambda g, h=h: decays(g, h)
            for t in range(FTILES + 1):
                steps[f"f{t}"] = lambda g, t=t: expert(g, t)
            act.wait_ge(s_load, 16 * len(loads))
            A(aneg[:, :], alog[:, :], ACT.Exp).then_inc(s_bias, 1)
            split_hi((0, 0))
            turns(act, steps, lambda i, front, back, late: act_front.begin((i, 0)) if front else None)

        @block.vector
        def _(dve):
            V = nc.vector
            prep = Chain(s_prep)
            prep.begin((0, 0))

            dve.wait_ge(s_load, 16 * len(loads))
            dve.wait_ge(s_bias, 1 + 1)
            V.tensor_scalar(aneg[:, :], aneg[:, :], -1.0, None, ALU.mult).then_inc(prep.mark(), 1)
            np_ = len(PROJ)
            V.tensor_copy(pbias[:, 0:np_ - 1], bank[0][:, 0:np_ - 1]).then_inc(prep.mark(), 1)
            V.tensor_copy(pbias[0:KB, np_ - 1:np_], bank[0][0:KB, np_ - 1:np_]).then_inc(prep.mark(), 1)
            V.tensor_tensor(dtbias[:, :], bank[0][0:H, 16:16 + HEADS], dtb[:, :], ALU.add).then_inc(prep.mark(), 1)
            dve.wait_ge(s_prep, prep.now())
            ia, ib = PROJ_AT["ga"], PROJ_AT["gb"]
            V.tensor_tensor(gbias[:, 0:1], pbias[:, ia:ia + 1], gba[:, :], ALU.add).then_inc(prep.mark(), 1)
            V.tensor_tensor(gbias[0:KB, 1:2], pbias[0:KB, ib:ib + 1], gbb[:, :], ALU.add).then_inc(prep.mark(), 1)
            dve.wait_ge(s_prep, prep.now())
            V.tensor_scalar(gbias[:, 0:1], gbias[:, 0:1], 0.5, None, ALU.mult).then_inc(prep.mark(), 1)
            V.tensor_scalar(gbias[0:KB, 1:2], gbias[0:KB, 1:2], 0.5, None, ALU.mult).then_inc(prep.mark(), 1)
            V.tensor_scalar(dhalf[:, :], dpar[:, :], 0.5, None, ALU.mult).then_inc(prep.mark(), 1)
            for s in range(2):
                V.tensor_tensor(pos[:, s * MODEL:(s + 1) * MODEL], pos[:, s * MODEL:(s + 1) * MODEL], tokb[:, :], ALU.add).then_inc(prep.mark(), 1)
            for k in range(NI):
                V.tensor_scalar(outp[:, k * MODEL:(k + 1) * MODEL], outp[:, k * MODEL:(k + 1) * MODEL], rms[:, k:k + 1],
                                    None, ALU.mult).then_inc(prep.mark(), 1)
            V.tensor_scalar(w1a_raw[:, :], w1a_raw[:, :], lnwa[:, 0:1], WSCALE, ALU.mult, ALU.mult).then_inc(prep.mark(), 1)
            V.tensor_scalar(w1b_raw[:, :], w1b_raw[:, :], lnwb[:, 0:1], WSCALE, ALU.mult, ALU.mult).then_inc(prep.mark(), 1)
            dve.wait_ge(s_prep, prep.now())

            def split(hi, lo, raw):
                V.tensor_copy(hi, raw).then_inc(prep.mark(), 1)
                dve.wait_ge(s_prep, prep.now())
                rows = lo.shape[0]
                return V.tensor_tensor(lo, raw[0:rows], hi[0:rows], ALU.subtract)

            split(w1a_hi[:, :], w1a_lo[:, :], w1a_raw[:, :]).then_inc(prep.mark(), 1)
            split(w1b_hi[:, :], w1b_lo[:, :], w1b_raw[:, :]).then_inc(prep.mark(), 1)
            split(ra_hi[:, :], ra_lo[:, :], ra_raw[:, :]).then_inc(prep.mark(), 1)
            split(rb_hi[:, :], rb_lo[:, :], rb_raw[:, :]).then_inc(prep.mark(), 1)
            split(down_hi[:, :], down_lo[:, :], down_raw[:, :]).then_inc(prep.mark(), 1)
            pieces = 0
            for name, _ in staged:
                pieces += 2 if name[-1] == "b" else 1
                dve.wait_ge(s_staged, 16 * pieces)
                if name == "tok":
                    hi, lo, raw = tok_hi[:, :], tok_lo[:, :], wf_raw[:, 0:KP * MODEL]
                else:
                    w = 0 if name.startswith("gate") else 1
                    hi, lo = (gua_hi, gua_lo) if name[-1] == "a" else (gub_hi, gub_lo)
                    hi, lo, raw = hi[w][:, :], lo[w][:, :], wf_raw[:, :]
                split(hi, lo, raw).then_inc(s_wfree, 1)
            dve.wait_ge(s_wfree, len(staged))
            dve.wait_ge(s_const, CONSTS)

            V.tensor_copy(identb[:, :], ident[:, :]).then_inc(prep.mark(), 1)

            def embed(g, s):
                u = f"embed{s}"
                dve.wait_ge(full[u].sem, full[u].at(g))
                if s == 0:
                    if base_ready.any(g, 0):
                        dve.wait_ge(base_ready.sem, base_ready.at(g, 0))
                ins = V.tensor_tensor(h1[:, 2 * s:2 * s + 2, :].rearrange("p j n -> p (j n)"),
                                      bank[UNIT_BANK[u]][0:H, 0:2 * MODEL], pos[:, :], ALU.add)
                ins.then_inc(emptied[u].sem, 1)

            def moments(src, stats, small, chain):
                for j in range(TILES):
                    ins = V.bn_stats(stats[:, j, :], src[:, j, :])
                ins.then_inc(chain.mark(), 1)
                dve.wait_ge(chain.sem, chain.now())
                me, mo, ve, vo = (stats[:, :, c] for c in (1, 4, 2, 5))
                V.tensor_tensor(small[:, 0, :], me, mo, ALU.add).then_inc(chain.mark(), 1)
                V.tensor_tensor(small[:, 1, :], me, mo, ALU.subtract).then_inc(chain.mark(), 1)
                V.tensor_tensor(small[:, 2, :], ve, vo, ALU.add).then_inc(chain.mark(), 1)
                dve.wait_ge(chain.sem, chain.now())
                V.tensor_scalar(small[:, 0, :], small[:, 0, :], 0.5, None, ALU.mult).then_inc(chain.mark(), 1)
                V.tensor_tensor(small[:, 1, :], small[:, 1, :], small[:, 1, :], ALU.mult).then_inc(chain.mark(), 1)
                dve.wait_ge(chain.sem, chain.now())
                V.scalar_tensor_tensor(small[:, 3, :], small[:, 1, :], MODEL / 4.0, small[:, 2, :], ALU.mult, ALU.add).then_inc(chain.mark(), 1)
                dve.wait_ge(chain.sem, chain.now())

            def norm1(g):
                for u in latest("embed0", "embed1"):
                    dve.wait_ge(emptied[u].sem, emptied[u].at(g))
                moments(h1, stats, small, dve_front)
                V.tensor_scalar(roots_in[:, 0:TILES], small[:, 3, :], 1.0 / MODEL, EPS, ALU.mult, ALU.add).then_inc(dve_front.mark(), 1)
                dve.wait_ge(dve_front.sem, dve_front.now())
                V.tensor_scalar(roots_in[:, TILES:8], small[:, 3, :], (1.0 + EPS) / MODEL, EPS * EPS, ALU.mult,
                                ALU.add).then_inc(roots_asked.sem, 1)

            def ta(g):
                dve.wait_ge(roots_done.sem, roots_done.at(g, 1))
                if full["tb"].any(before(g)):
                    dve.wait_ge(full["tb"].sem, full["tb"].at(before(g)))
                for j in range(TILES):
                    ins = V.tensor_scalar(xn[:, j, :], h1[:, j, :], small[:, 0, j:j + 1], roots[:, TILES + j:TILES + j + 1],
                                          ALU.subtract, ALU.mult)
                    if j == TILES - 1:
                        ins.then_inc(xn_ready.sem, 1)
                    else:
                        ins.then_inc(dve_front.mark(), 1)
                V.scalar_tensor_tensor(small[:, 4, :], small[:, 0, :], -1.0, roots[:, 0:TILES], ALU.mult,
                                       ALU.mult).then_inc(shift_ready.sem, 1)

            def tb(g):
                dve.wait_ge(hi_ready.sem, hi_ready.at(g, 1))
                V.tensor_tensor(xa_lo[:, :], bank[UNIT_BANK["ta"]][0:KA, 0:T], xa_hi[:, :],
                                ALU.subtract).then_inc(emptied["ta"].sem, 1)
                dve.wait_ge(hi_ready.sem, hi_ready.at(g, 2))
                V.tensor_tensor(xb_hl[KB:128, :], bank[UNIT_BANK["tb"]][0:KB, 0:T], xb_hl[0:KB, :],
                                ALU.subtract).then_inc(emptied["tb"].sem, 1)

            def dt(g):
                u = "dt"
                dve.wait_ge(full[u].sem, full[u].at(g))
                cols = TILES * HEADS
                flat = dt_raw[:, :, :].rearrange("p j h -> p (j h)")
                ins = V.scalar_tensor_tensor(dt_raw[:, :, :], bank[UNIT_BANK[u]][0:H, 0:cols].rearrange("p (j h) -> p j h", j=TILES),
                                             1.0 / WSCALE, dtbias[:, :].unsqueeze(1).to_broadcast([H, TILES, HEADS]), ALU.mult, ALU.add)
                ins.then_inc(emptied[u].sem, 1)
                dve.wait_ge(emptied[u].sem, emptied[u].at(g))
                V.scalar_tensor_tensor(sp[:, 0, :], flat, -1.0, flat, ALU.mult, ALU.max).then_inc(soft_in.sem, 1)
                V.tensor_scalar(sp[:, 2, :], flat, 0.0, None, ALU.max).then_inc(dve_front.mark(), 1)

            def soft(g):
                dve.wait_ge(soft_e.sem, soft_e.at(g, 1))
                dve.wait_ge(dve_front.sem, dve_front.now())
                e, s, s2, p = sp[:, 1, :], sp[:, 3, :], sp[:, 4, :], sp[:, 5, :]
                V.tensor_scalar(s, e, 2.0, None, ALU.add).then_inc(dve_front.mark(), 1)
                dve.wait_ge(dve_front.sem, dve_front.now())
                V.reciprocal(s2, s).then_inc(dve_front.mark(), 1)
                dve.wait_ge(dve_front.sem, dve_front.now())
                V.tensor_tensor(s, e, s2, ALU.mult).then_inc(dve_front.mark(), 1)
                dve.wait_ge(dve_front.sem, dve_front.now())
                V.tensor_tensor(s2, s, s, ALU.mult).then_inc(dve_front.mark(), 1)
                dve.wait_ge(dve_front.sem, dve_front.now())
                V.tensor_scalar(p, s2, 1.0 / 15, None, ALU.mult).then_inc(dve_front.mark(), 1)
                dve.wait_ge(dve_front.sem, dve_front.now())
                for c in (13, 11, 9, 7, 5, 3):
                    V.scalar_tensor_tensor(p, p, 1.0 / c, s2, ALU.add, ALU.mult).then_inc(dve_front.mark(), 1)
                    dve.wait_ge(dve_front.sem, dve_front.now())
                V.scalar_tensor_tensor(p, p, 1.0, s, ALU.add, ALU.mult).then_inc(dve_front.mark(), 1)
                dve.wait_ge(dve_front.sem, dve_front.now())
                V.scalar_tensor_tensor(s, p, 2.0, sp[:, 2, :], ALU.mult, ALU.add).then_inc(dve_front.mark(), 1)
                dve.wait_ge(dve_front.sem, dve_front.now())
                if emptied["xt3"].any(before(g)):
                    dve.wait_ge(emptied["xt3"].sem, emptied["xt3"].at(before(g)))
                V.tensor_scalar(dth[:, :, :].rearrange("p j h -> p (j h)"), s, 0.5, None, ALU.mult).then_inc(dve_front.mark(), 1)
                V.tensor_tensor(dta[:, :, :], s.rearrange("p (j h) -> p j h", j=TILES),
                                aneg[:, :].unsqueeze(1).to_broadcast([H, TILES, HEADS]), ALU.mult).then_inc(dta_ready.sem, 1)

            def cum(g):
                u = "cum"
                dve.wait_ge(full[u].sem, full[u].at(g))
                flat = csum[:, :, :].rearrange("p j h -> p (j h)")
                V.tensor_copy(flat, bank[UNIT_BANK[u]][0:H, 0:TILES * HEADS]).then_inc(emptied[u].sem, 1)
                dve.wait_ge(emptied[u].sem, emptied[u].at(g))
                if full["cpart"].any(before(g)):
                    dve.wait_ge(full["cpart"].sem, full["cpart"].at(before(g)))
                part = [cpt[:, :, 32 * n:32 * n + HEADS] for n in range(3)]
                V.tensor_copy(part[0], csum[:, :, :]).then_inc(dve_front.mark(), 1)
                dve.wait_ge(dve_front.sem, dve_front.now())
                V.tensor_tensor(part[1], csum[:, :, :], part[0], ALU.subtract).then_inc(dve_front.mark(), 1)
                V.tensor_tensor(crest[:, :, :], csum[:, :, :], part[0], ALU.subtract).then_inc(dve_front.mark(), 1)
                dve.wait_ge(dve_front.sem, dve_front.now())
                V.tensor_tensor(part[2], crest[:, :, :], part[1], ALU.subtract).then_inc(cpt_ready.sem, 1)
                if emptied["cb5"].any(before(g)):
                    dve.wait_ge(emptied["cb5"].sem, emptied["cb5"].at(before(g)))
                V.tensor_scalar(ncum[:, :, :].rearrange("p j h -> p (j h)"), flat, -1.0, None, ALU.mult).then_inc(ncum_ready.sem, 1)

            def convolve(g, k):
                u = f"x{k}" if k < NI else "bc"
                dve.wait_ge(emptied[u].sem, emptied[u].at(g))
                dve.wait_ge(tap0_ready.sem, tap0_ready.at(g, k + 1))
                out = conv[:, k, :, :]
                for tap in range(1, TAPS):
                    ins = V.scalar_tensor_tensor(out, xpad[:, k, :, tap:tap + TOKENS], convw[:, k, tap:tap + 1], out, ALU.mult,
                                                 ALU.add)
                    if tap < TAPS - 1:
                        ins.then_inc(dve_front.mark(), 1)
                        dve.wait_ge(dve_front.sem, dve_front.now())
                    else:
                        ins.then_inc(conv_ready.sem, 1)

            def silu(g, k):
                dve.wait_ge(convt_ready.sem, convt_ready.at(g, k + 1))
                dve.wait_ge(conv_ready.sem, conv_ready.at(g, k + 1))
                t, v = convt[:, k, :, :], conv[:, k, :, :]
                if k < NI:
                    if k == 0:
                        if emptied["y2"].any(before(g)):
                            dve.wait_ge(emptied["y2"].sem, emptied["y2"].at(before(g)))
                        if full["xt3"].any(before(g)):
                            dve.wait_ge(full["xt3"].sem, full["xt3"].at(before(g)))
                    V.scalar_tensor_tensor(xs[:, k, :].rearrange("p (s t) -> p s t", s=SEQS), t, 1.0, v, ALU.add,
                                           ALU.mult).then_inc(silu_ready.sem, 1)
                else:
                    if full["g1"].any(before(g)):
                        dve.wait_ge(full["g1"].sem, full["g1"].at(before(g)))
                    for n, dst in enumerate((bs, cs)):
                        rows = slice(n * STATE, (n + 1) * STATE)
                        ins = V.scalar_tensor_tensor(dst[:, :].rearrange("p (s t) -> p s t", s=SEQS), t[rows], 1.0, v[rows],
                                                     ALU.add, ALU.mult)
                        if n == 0:
                            ins.then_inc(dve_front.mark(), 1)
                        else:
                            ins.then_inc(silu_ready.sem, 1)

            def masked(g, s):
                u = f"g{s}"
                dve.wait_ge(full[u].sem, full[u].at(g))
                V.tensor_tensor(gm[:, s, :], bank[UNIT_BANK[u]][0:H, 0:CAUSAL], causal[:, :], ALU.mult).then_inc(
                    emptied[u].sem, 1)

            def x_dt(g, j):
                u = f"xt{j}"
                dve.wait_ge(full[u].sem, full[u].at(g))
                if j == 0:
                    if full["y2"].any(before(g)):
                        dve.wait_ge(full["y2"].sem, full["y2"].at(before(g)))
                    dve.wait_ge(dta_ready.sem, dta_ready.at(g, 1))
                ins = V.tensor_tensor(xdt[:, j, :].rearrange("p (h d) -> p h d", h=HEADS),
                                      bank[UNIT_BANK[u]][0:H, 0:INNER].rearrange("p (h d) -> p h d", h=HEADS),
                                      dth[:, j, :].unsqueeze(2).to_broadcast([H, HEADS, HD]), ALU.mult)
                ins.then_inc(emptied[u].sem, 1)

            def weight(g, h):
                for u in latest("cb0", "g0", "g1") if h == 0 else (f"cb{h}",):
                    dve.wait_ge(emptied[u].sem, emptied[u].at(g))
                if h == 0:
                    if full["y2"].any(before(g)):
                        dve.wait_ge(full["y2"].sem, full["y2"].at(before(g)))
                V.scalar_tensor_tensor(wgt[:, h, :, :].rearrange("p s n -> p (s n)"), decay[:, h % 2, :, :].rearrange("p s n -> p (s n)"),
                                       1.0, gm[:, :, :].rearrange("p s n -> p (s n)"), ALU.min, ALU.mult).then_inc(wgt_ready.sem, 1)

            def gate_z(g, k):
                dve.wait_ge(emptied[f"z{k}"].sem, emptied[f"z{k}"].at(g))
                if y2_ready.any(g, k + 1 - NI):
                    dve.wait_ge(y2_ready.sem, y2_ready.at(g, k + 1 - NI))
                V.scalar_tensor_tensor(zs[:, k, :], zt[:, k, :], 1.0, zb[:, k, :], ALU.add, ALU.mult).then_inc(zs_ready.sem, 1)

            def y_out(g, n):
                u = f"y{n}"
                dve.wait_ge(full[u].sem, full[u].at(g))
                dve.wait_ge(silu_ready.sem, silu_ready.at(g, n + 1))
                if y2_ready.any(g, n + 1 - NI):
                    dve.wait_ge(y2_ready.sem, y2_ready.at(g, n + 1 - NI))
                ins = V.scalar_tensor_tensor(y1[:, n, :], xs[:, n, :], dhalf[:, n:n + 1], bank[UNIT_BANK[u]][:, 0:T],
                                             ALU.mult, ALU.add)
                ins.then_inc(emptied[u].sem, 1)

            def gate_out(g, n):
                u, rows = ("oa", "ob")[n], (KA, KB)[n]
                dve.wait_ge(full[u].sem, full[u].at(g))
                gu = ("ga", "gb")[n]
                dve.wait_ge(emptied[gu].sem, emptied[gu].at(g))
                if full["ow1"].any(before(g)):
                    dve.wait_ge(full["ow1"].sem, full["ow1"].at(before(g)))
                V.scalar_tensor_tensor(gated[0:rows, n, :], gt[0:rows, n, :], 1.0, bank[UNIT_BANK[u]][0:rows, 0:T],
                                       ALU.add, ALU.mult).then_inc(emptied[u].sem, 1)

            def ss(g):
                u = "ss"
                dve.wait_ge(full[u].sem, full[u].at(g))
                ins = V.tensor_scalar(rinv_in[:, :], bank[UNIT_BANK[u]][0:H, 0:TILES], 0.25 / INNER, EPS, ALU.mult, ALU.add)
                ins.then_inc(emptied[u].sem, 1)

            def residual(g, s):
                u = f"ow{s}"
                if s == 0:
                    dve.wait_ge(roots2_done.sem, roots2_done.at(g, 1))
                    V.tensor_scalar(rinv[:, :], rinv[:, :], 0.25, None, ALU.mult).then_inc(dve_back.mark(), 1)
                    dve.wait_ge(dve_back.sem, dve_back.now())
                    dve.wait_ge(base_ready.sem, base_ready.at(g, 1))
                    if down_free.any(before(g), SEQS):
                        dve.wait_ge(down_free.sem, down_free.at(before(g), SEQS))
                dve.wait_ge(full[u].sem, full[u].at(g))
                for j in (2 * s, 2 * s + 1):
                    ins = V.scalar_tensor_tensor(h2[:, j, :], bank[UNIT_BANK[u]][0:H, (j % 2) * MODEL:(j % 2 + 1) * MODEL],
                                                 rinv[:, j:j + 1], base[:, j, :], ALU.mult, ALU.add)
                    if j % 2 == 0:
                        ins.then_inc(dve_back.mark(), 1)
                    else:
                        ins.then_inc(emptied[u].sem, 1)

            def norm2(g):
                dve.wait_ge(dve_back.sem, dve_back.now())
                for u in latest("ow0", "ow1"):
                    dve.wait_ge(emptied[u].sem, emptied[u].at(g))
                moments(h2, stats2, small2, dve_back)
                V.tensor_scalar(roots2_in[:, :], small2[:, 3, :], 1.0 / MODEL, EPS, ALU.mult, ALU.add).then_inc(roots2_asked.sem, 1)

            def t2a(g):
                dve.wait_ge(roots2_done.sem, roots2_done.at(g, 2))
                if full["t2b"].any(before(g)):
                    dve.wait_ge(full["t2b"].sem, full["t2b"].at(before(g)))
                for j in range(TILES):
                    ins = V.tensor_scalar(xn2[:, j, :], h2[:, j, :], small2[:, 0, j:j + 1], roots2[:, j:j + 1],
                                          ALU.subtract, ALU.mult)
                    if j == TILES - 1:
                        ins.then_inc(xn2_ready.sem, 1)
                    else:
                        ins.then_inc(dve_back.mark(), 1)

            def t2b(g):
                dve.wait_ge(hi2_ready.sem, hi2_ready.at(g, 1))
                V.tensor_tensor(fa_lo[:, :], bank[UNIT_BANK["t2a"]][0:KA, 0:T], fa_hi[:, :], ALU.subtract).then_inc(
                    emptied["t2a"].sem, 1)
                dve.wait_ge(hi2_ready.sem, hi2_ready.at(g, 2))
                V.tensor_tensor(fb_hl[KB:128, :], bank[UNIT_BANK["t2b"]][0:KB, 0:T], fb_hl[0:KB, :], ALU.subtract).then_inc(
                    emptied["t2b"].sem, 1)

            def route(g):
                u = "route"
                dve.wait_ge(full[u].sem, full[u].at(g))
                ins = V.tensor_tensor(rl[:, :, :], bank[UNIT_BANK[u]][0:H, 0:TILES * ROUTED].rearrange("p (j e) -> p j e", j=TILES),
                                      rbias[:, :].unsqueeze(1).to_broadcast([H, TILES, ROUTED]), ALU.add)
                ins.then_inc(emptied[u].sem, 1)

            def combine(g):
                dve.wait_ge(router_e.sem, router_e.at(g, 1))
                e, s, keep = rs[:, 0, :, :], rs[:, 2, :, :], rs[:, 3, :, :]
                tmp = rs[:, 4, :, :]
                V.tensor_scalar(e, e, 1.0, None, ALU.add).then_inc(dve_late.mark(), 1)
                dve.wait_ge(dve_late.sem, dve_late.now())
                V.reciprocal(s, e).then_inc(dve_late.mark(), 1)
                dve.wait_ge(dve_late.sem, dve_late.now())
                V.tensor_tensor(tmp[:, :, 0], s[:, :, 1], s[:, :, 2], ALU.min).then_inc(dve_late.mark(), 1)
                dve.wait_ge(dve_late.sem, dve_late.now())
                V.tensor_tensor(tmp[:, :, 1], s[:, :, 0], s[:, :, 1], ALU.min).then_inc(dve_late.mark(), 1)
                dve.wait_ge(dve_late.sem, dve_late.now())
                V.tensor_tensor(keep[:, :, 0], s[:, :, 0], tmp[:, :, 0], ALU.is_ge).then_inc(dve_late.mark(), 1)
                dve.wait_ge(dve_late.sem, dve_late.now())
                V.tensor_tensor(keep[:, :, 2], s[:, :, 2], tmp[:, :, 1], ALU.is_gt).then_inc(dve_late.mark(), 1)
                dve.wait_ge(dve_late.sem, dve_late.now())
                V.tensor_tensor(tmp[:, :, 2], keep[:, :, 0], keep[:, :, 2], ALU.add).then_inc(dve_late.mark(), 1)
                dve.wait_ge(dve_late.sem, dve_late.now())
                V.tensor_scalar(keep[:, :, 1], tmp[:, :, 2], -1.0, 2.0, ALU.mult, ALU.add).then_inc(dve_late.mark(), 1)
                dve.wait_ge(dve_late.sem, dve_late.now())
                V.tensor_tensor(s, s, keep, ALU.mult).then_inc(dve_late.mark(), 1)
                dve.wait_ge(dve_late.sem, dve_late.now())
                V.tensor_tensor(tmp[:, :, 0], s[:, :, 0], s[:, :, 1], ALU.add).then_inc(dve_late.mark(), 1)
                dve.wait_ge(dve_late.sem, dve_late.now())
                V.tensor_tensor(tmp[:, :, 0], tmp[:, :, 0], s[:, :, 2], ALU.add).then_inc(dve_late.mark(), 1)
                dve.wait_ge(dve_late.sem, dve_late.now())
                V.reciprocal(tmp[:, :, 1], tmp[:, :, 0]).then_inc(dve_late.mark(), 1)
                dve.wait_ge(dve_late.sem, dve_late.now())
                V.tensor_scalar(tmp[:, :, 1], tmp[:, :, 1], 0.5, None, ALU.mult).then_inc(dve_late.mark(), 1)
                dve.wait_ge(dve_late.sem, dve_late.now())
                V.tensor_tensor(comb[:, :, :], s, tmp[:, :, 1:2].to_broadcast([H, TILES, ROUTED]), ALU.mult).then_inc(dve_late.mark(), 1)
                dve.wait_ge(dve_late.sem, dve_late.now())

            def expert(g, t):
                if t == 0:
                    combine(g)
                if t == FTILES:
                    return
                dve.wait_ge(ft_ready.sem, ft_ready.at(g, t + 1))
                V.scalar_tensor_tensor(fg[:, t % 2, :], ft[:, t % 2, :], 1.0, gate_ps[t % 2][:, 0:T], ALU.add, ALU.mult).then_inc(dve_late.mark(), 1)
                dve.wait_ge(dve_late.sem, dve_late.now())
                dve.wait_ge(up_full.sem, up_full.at(g, t + 1))
                if flo_ready.any(g, t + 1 - 2):
                    dve.wait_ge(flo_ready.sem, flo_ready.at(g, t + 1 - 2))
                V.tensor_tensor(fh[:, t % 2, :], fg[:, t % 2, :], up_ps[t % 2][:, 0:T], ALU.mult).then_inc(fh_ready.sem, 1)

            def down(g, e, s):
                n = SEQS * e + s
                dve.wait_ge(down_full.sem, down_full.at(g, n + 1))
                if n == 0:
                    if stored.any(g, 0):
                        dve.wait_ge(stored.sem, stored.at(g, 0))
                elif e:
                    dve.wait_ge(down_free.sem, down_free.at(g, n + 1 - SEQS))
                for j in (2 * s, 2 * s + 1):
                    rows = down_ps[0:H, (j % 2) * MODEL:(j % 2 + 1) * MODEL]
                    if e == 0:
                        ins = V.scalar_tensor_tensor(acc[:, j, :], rows, 0.5, h2[:, j, :], ALU.mult, ALU.add)
                    else:
                        ins = V.scalar_tensor_tensor(acc[:, j, :], rows, comb[:, j, e - 1:e], acc[:, j, :], ALU.mult, ALU.add)
                ins.then_inc(down_free.sem, 1)

            steps = {"norm1": norm1, "ta": ta, "tb": tb, "dt": dt, "soft": soft, "cum": cum, "ss": ss,
                     "gate": lambda g: [gate_out(g, n) for n in range(2)], "norm2": norm2, "t2a": t2a, "t2b": t2b, "route": route}
            for s in range(SEQS):
                steps[f"embed{s}"] = lambda g, s=s: embed(g, s)
                steps[f"g{s}"] = lambda g, s=s: masked(g, s)
                steps[f"ow{s}"] = lambda g, s=s: residual(g, s)
            for k in range(4):
                steps[f"conv{k}"] = lambda g, k=k: convolve(g, k)
                steps[f"silu{k}"] = lambda g, k=k: silu(g, k)
                steps[f"xt{k}"] = lambda g, k=k: x_dt(g, k)
            for h in range(HEADS):
                steps[f"w{h}"] = lambda g, h=h: weight(g, h)
            for n in range(NI):
                steps[f"y{n}"] = lambda g, n=n: y_out(g, n)
                steps[f"sz{n}"] = lambda g, n=n: gate_z(g, n)
            for t in range(FTILES + 1):
                steps[f"f{t}"] = lambda g, t=t: expert(g, t)
            for e in range(EXPERTS):
                for s in range(SEQS):
                    steps[f"d{e}{s}"] = lambda g, e=e, s=s: down(g, e, s)

            def begin(i, front, back, late):
                if front:
                    dve_front.begin((i, 0))
                if back:
                    dve_back.begin((i, -1))
                if late:
                    dve_late.begin((i, -2))
            turns(dve, steps, begin)

        @block.tensor
        def _(pe):
            M = nc.tensor.matmul

            pe.wait_ge(s_load, 16 * len(loads))
            pe.wait_ge(s_const, CONSTS)
            for n, (c, width) in enumerate(PROJ.values()):
                M(bank[0][0:width, n:n + 1], w1a_raw[:, c:c + width], lnba[:, :], start=True, stop=False)
                M(bank[0][0:width, n:n + 1], w1b_raw[0:KB, c:c + width], lnbb[:, :], start=False, stop=True)
            M(bank[0][0:H, 16:16 + HEADS], lnba[:, 0:1].to_broadcast([KA, H]), w1a_raw[:, COL_DT:COL_DT + HEADS], start=True, stop=False)
            M(bank[0][0:H, 16:16 + HEADS], lnbb[:, 0:1].to_broadcast([KB, H]), w1b_raw[0:KB, COL_DT:COL_DT + HEADS], start=False,
              stop=True).then_inc(s_bias, 1)
            pe.wait_ge(s_wfree, len(staged))

            def five(out, a_hi, a_lo, b_hi, b_lo, xa, xl, xb, first=True):
                M(out, a_hi, xa, start=first, stop=False, skip_group_check=True)
                M(out, a_lo, xa, start=False, stop=False, skip_group_check=True)
                M(out, a_hi, xl, start=False, stop=False, skip_group_check=True)
                M(out, b_hi, xb, start=False, stop=False, skip_group_check=True)
                return M(out, b_lo, xb[0:KB], start=False, stop=True, skip_group_check=True)

            def five_rows(out, w, xa, xl, xb, first):
                a_hi, a_lo, b_hi, b_lo = w
                M(out, xa, a_hi, start=first, stop=False, skip_group_check=True)
                M(out, xa, a_lo, start=False, stop=False, skip_group_check=True)
                M(out, xl, a_hi, start=False, stop=False, skip_group_check=True)
                M(out, xb, b_hi, start=False, stop=False, skip_group_check=True)
                return M(out, xb[0:KB], b_lo, start=False, stop=True, skip_group_check=True)

            def embed(g, s):
                u = f"embed{s}"
                pe.wait_ge(patch_lo.sem, patch_lo.at(g, 1))
                pe.wait_ge(patch_hi.sem, patch_hi.at(g, 1))
                if emptied[u].any(g, -1):
                    pe.wait_ge(emptied[u].sem, emptied[u].at(g, -1))
                hi = pat_hi[:, :].rearrange("p (k t) -> p k t", k=KP)
                lo = pat_lo[:, :].rearrange("p (k t) -> p k t", k=KP)
                for j in (2 * s, 2 * s + 1):
                    out = bank[UNIT_BANK[u]][0:H, (j % 2) * MODEL:(j % 2 + 1) * MODEL]
                    for k in range(KP):
                        xh, xl = hi[:, k, j * H:(j + 1) * H], lo[:, k, j * H:(j + 1) * H]
                        wh, wl = tok_hi[:, k * MODEL:(k + 1) * MODEL], tok_lo[:, k * MODEL:(k + 1) * MODEL]
                        M(out, xh, wh, start=(k == 0), stop=False, skip_group_check=True)
                        M(out, xh, wl, start=False, stop=False, skip_group_check=True)
                        ins = M(out, xl, wh, start=False, stop=(k == KP - 1), skip_group_check=True)
                ins.then_inc(full[u].sem, 1)

            def transposes(g, units, src, ready):
                pe.wait_ge(ready.sem, ready.at(g, 1))
                for u in units:
                    if emptied[u].any(g, -1):
                        pe.wait_ge(emptied[u].sem, emptied[u].at(g, -1))
                for u, c, width in zip(units, (0, KA), (KA, KB)):
                    for j in range(TILES):
                        ins = nc.tensor.transpose(bank[UNIT_BANK[u]][0:width, j * H:(j + 1) * H], src[:, j, c:c + width],
                                                  ident[0:H, 0:H])
                    ins.then_inc(full[u].sem, 1)

            def x_ready(g, u):
                for part in latest("ta", "tb", before=u):
                    pe.wait_ge(emptied[part].sem, emptied[part].at(g))

            def dt(g):
                u = "dt"
                x_ready(g, u)
                if emptied[u].any(g, -1):
                    pe.wait_ge(emptied[u].sem, emptied[u].at(g, -1))
                c = slice(COL_DT, COL_DT + HEADS)
                for j in range(TILES):
                    t = slice(j * H, (j + 1) * H)
                    ins = five_rows(bank[UNIT_BANK[u]][0:H, j * HEADS:(j + 1) * HEADS],
                                    (w1a_hi[:, c], w1a_lo[:, c], w1b_hi[:, c], w1b_lo[:, c]), xa_hi[:, t], xa_lo[:, t], xb_hl[:, t], True)
                ins.then_inc(full[u].sem, 1)

            def project(g, u):
                c, width = PROJ[u]
                if u == "x0":
                    x_ready(g, u)
                if emptied[u].any(g, -1):
                    pe.wait_ge(emptied[u].sem, emptied[u].at(g, -1))
                cols = slice(c, c + width)
                five(bank[UNIT_BANK[u]][0:width, 0:T], w1a_hi[:, cols], w1a_lo[:, cols], w1b_hi[:, cols], w1b_lo[:, cols],
                            xa_hi[:, :], xa_lo[:, :], xb_hl[:, :]).then_inc(full[u].sem, 1)

            def cum(g):
                u = "cum"
                pe.wait_ge(dta_ready.sem, dta_ready.at(g, 1))
                if emptied[u].any(g, -1):
                    pe.wait_ge(emptied[u].sem, emptied[u].at(g, -1))
                halves = dta[:, :, :].rearrange("p (s f) h -> p f s h", s=SEQS)
                out = bank[UNIT_BANK[u]][0:H, 0:TILES * HEADS].rearrange("p (s f h) -> p f s h", s=SEQS, f=2)
                M(out[:, 0], upper[:, :], halves[:, 0], start=True, stop=True, skip_group_check=True)
                M(out[:, 1], ones[0:H, :], halves[:, 0], start=True, stop=False, skip_group_check=True)
                M(out[:, 1], upper[:, :], halves[:, 1], start=False, stop=True, skip_group_check=True).then_inc(full[u].sem, 1)

            def cum_parts(g):
                u = "cpart"
                pe.wait_ge(cpt_ready.sem, cpt_ready.at(g, 1))
                if emptied[u].any(g, -1):
                    pe.wait_ge(emptied[u].sem, emptied[u].at(g, -1))
                for j in range(TILES):
                    ins = nc.tensor.transpose(bankb[UNIT_BANK[u]][0:96, j * H:(j + 1) * H], cpt[:, j, :], identb[0:H, 0:H])
                ins.then_inc(full[u].sem, 1)

            def cb_products(g, s):
                u = f"g{s}"
                pe.wait_ge(silu_ready.sem, silu_ready.at(g, 4))
                if emptied[u].any(g, -1):
                    pe.wait_ge(emptied[u].sem, emptied[u].at(g, -1))
                t0 = s * TOKENS
                M(bank[UNIT_BANK[u]][0:H, 0:TOKENS], bs[:, t0:t0 + H], cs[:, t0:t0 + TOKENS], start=True, stop=True,
                  skip_group_check=True)
                M(bank[UNIT_BANK[u]][0:H, TOKENS:CAUSAL], bs[:, t0 + H:t0 + TOKENS], cs[:, t0 + H:t0 + TOKENS], start=True,
                         stop=True, skip_group_check=True).then_inc(full[u].sem, 1)

            def x_rows(g, j):
                u = f"xt{j}"
                pe.wait_ge(silu_ready.sem, silu_ready.at(g, NI))
                if emptied[u].any(g, -1):
                    pe.wait_ge(emptied[u].sem, emptied[u].at(g, -1))
                for k in range(NI):
                    ins = nc.tensor.transpose(bank[UNIT_BANK[u]][0:H, k * 128:(k + 1) * 128], xs[:, k, j * H:(j + 1) * H], ident[:, :])
                ins.then_inc(full[u].sem, 1)

            def broadcast(g, h):
                u = f"cb{h}"
                for part in latest("cpart", before=u):
                    pe.wait_ge(emptied[part].sem, emptied[part].at(g))
                if emptied[u].any(g, -1):
                    pe.wait_ge(emptied[u].sem, emptied[u].at(g, -1))
                M(bank[UNIT_BANK[u]][0:H, 0:T], pick[:, h, :], cumpart[:, :], start=True, stop=True, skip_group_check=True).then_inc(full[u].sem, 1)

            def scan_out(g, n):
                u = f"y{n}"
                pe.wait_ge(wgt_ready.sem, wgt_ready.at(g, 2 * n + 2))
                for x in latest("xt0", "xt1", "xt2", "xt3", before=u):
                    pe.wait_ge(emptied[x].sem, emptied[x].at(g))
                if emptied[u].any(g, -1):
                    pe.wait_ge(emptied[u].sem, emptied[u].at(g, -1))
                for head in (2 * n, 2 * n + 1):
                    rows = slice((head % 2) * HD, (head % 2 + 1) * HD)
                    cols = slice(head * HD, (head + 1) * HD)
                    for s in range(SEQS):
                        t0 = s * TOKENS
                        M(bank[UNIT_BANK[u]][rows, t0:t0 + TOKENS], xdt[:, 2 * s, cols], wgt[:, head, s, 0:TOKENS],
                          start=(s == 0), stop=False, skip_group_check=True)
                        ins = M(bank[UNIT_BANK[u]][rows, t0 + H:t0 + TOKENS], xdt[:, 2 * s + 1, cols], wgt[:, head, s, TOKENS:CAUSAL],
                                start=False, stop=True, skip_group_check=True)
                ins.then_inc(full[u].sem, 1)

            def out_project(g, n):
                u, c, width = (("oa", 0, KA), ("ob", KA, KB))[n]
                pe.wait_ge(y2_ready.sem, y2_ready.at(g, NI))
                if emptied[u].any(g, -1):
                    pe.wait_ge(emptied[u].sem, emptied[u].at(g, -1))
                for k in range(NI):
                    ins = M(bank[UNIT_BANK[u]][0:width, 0:T], outp[:, k * MODEL + c:k * MODEL + c + width], y2[:, k, :],
                            start=(k == 0), stop=(k == NI - 1), skip_group_check=True)
                ins.then_inc(full[u].sem, 1)

            def square_sums(g):
                u = "ss"
                pe.wait_ge(sqsum_ready.sem, sqsum_ready.at(g, 1))
                if emptied[u].any(g, -1):
                    pe.wait_ge(emptied[u].sem, emptied[u].at(g, -1))
                for j in range(TILES):
                    ins = M(bank[UNIT_BANK[u]][0:H, j:j + 1], sq[:, 0, j * H:(j + 1) * H], ones[:, 0:1], start=True, stop=True,
                            skip_group_check=True)
                ins.then_inc(full[u].sem, 1)

            def out_rows(g, s):
                u = f"ow{s}"
                for o in latest("oa", "ob", before=u):
                    pe.wait_ge(emptied[o].sem, emptied[o].at(g))
                if emptied[u].any(g, -1):
                    pe.wait_ge(emptied[u].sem, emptied[u].at(g, -1))
                for j in (2 * s, 2 * s + 1):
                    out = bank[UNIT_BANK[u]][0:H, (j % 2) * MODEL:(j % 2 + 1) * MODEL]
                    t = slice(j * H, (j + 1) * H)
                    M(out, gated[0:KA, 0, t], owa[:, :], start=True, stop=False, skip_group_check=True)
                    ins = M(out, gated[0:KB, 1, t], owb[:, :], start=False, stop=True, skip_group_check=True)
                ins.then_inc(full[u].sem, 1)

            def f_ready(g, u=None):
                for part in latest("t2a", "t2b", before=u):
                    pe.wait_ge(emptied[part].sem, emptied[part].at(g))

            def route(g):
                u = "route"
                f_ready(g, u)
                if emptied[u].any(g, -1):
                    pe.wait_ge(emptied[u].sem, emptied[u].at(g, -1))
                for j in range(TILES):
                    t = slice(j * H, (j + 1) * H)
                    ins = five_rows(bank[UNIT_BANK[u]][0:H, j * ROUTED:(j + 1) * ROUTED],
                                    (ra_hi[:, :], ra_lo[:, :], rb_hi[:, :], rb_lo[:, :]), fa_hi[:, t], fa_lo[:, t], fb_hl[:, t], True)
                ins.then_inc(full[u].sem, 1)

            def expert(g, t):
                if t == FTILES:
                    return
                if t == 0:
                    f_ready(g)
                if fh_ready.any(g, t + 1 - 2):
                    pe.wait_ge(fh_ready.sem, fh_ready.at(g, t + 1 - 2))
                cols = slice(t * 128, (t + 1) * 128)
                for w, (ps, full) in enumerate(((gate_ps, gate_full), (up_ps, up_full))):
                    five(ps[t % 2][:, 0:T], gua_hi[w][:, cols], gua_lo[w][:, cols], gub_hi[w][:, cols], gub_lo[w][:, cols],
                         fa_hi[:, :], fa_lo[:, :], fb_hl[:, :]).then_inc(full.sem, 1)

            def down(g, e, s):
                n = SEQS * e + s
                if s == 0:
                    pe.wait_ge(flo_ready.sem, flo_ready.at(g, NF * (e + 1)))
                    pe.wait_ge(fhi_ready.sem, fhi_ready.at(g, NF * (e + 1)))
                if down_free.any(g, n):
                    pe.wait_ge(down_free.sem, down_free.at(g, n))
                for j in (2 * s, 2 * s + 1):
                    t = slice(j * H, (j + 1) * H)
                    out = down_ps[0:H, (j % 2) * MODEL:(j % 2 + 1) * MODEL]
                    for k in range(NF):
                        w = slice((NF * e + k) * MODEL, (NF * e + k + 1) * MODEL)
                        hi, lo = fh_hi[:, e % 2, k, t], fh_lo[:, e % 2, k, t]
                        M(out, hi, down_hi[:, w], start=(k == 0), stop=False, skip_group_check=True)
                        M(out, hi, down_lo[:, w], start=False, stop=False, skip_group_check=True)
                        ins = M(out, lo, down_hi[:, w], start=False, stop=(k == NF - 1), skip_group_check=True)
                ins.then_inc(down_full.sem, 1)

            steps = {"ta": lambda g: transposes(g, ("ta", "tb"), xn, xn_ready), "t2a": lambda g: transposes(g, ("t2a", "t2b"), xn2, xn2_ready),
                     "dt": dt, "cum": cum, "cpart": cum_parts, "ss": square_sums, "route": route,
                     "oa": lambda g: out_project(g, 0), "ob": lambda g: out_project(g, 1)}
            for u in PROJ:
                steps[u] = lambda g, u=u: project(g, u)
            for s in range(SEQS):
                steps[f"embed{s}"] = lambda g, s=s: embed(g, s)
                steps[f"g{s}"] = lambda g, s=s: cb_products(g, s)
                steps[f"ow{s}"] = lambda g, s=s: out_rows(g, s)
            for j in range(TILES):
                steps[f"xt{j}"] = lambda g, j=j: x_rows(g, j)
            for h in range(HEADS):
                steps[f"cb{h}"] = lambda g, h=h: broadcast(g, h)
            for n in range(NI):
                steps[f"y{n}"] = lambda g, n=n: scan_out(g, n)
            for t in range(FTILES + 1):
                steps[f"f{t}"] = lambda g, t=t: expert(g, t)
            for e in range(EXPERTS):
                for s in range(SEQS):
                    steps[f"d{e}{s}"] = lambda g, e=e, s=s: down(g, e, s)
            turns(pe, steps)


def kernel(**inputs):
    import numpy as np
    import concourse.bacc as bacc
    from concourse.bass_utils import run_bass_kernel_spmd

    def rows(a, n):
        return np.ascontiguousarray(np.broadcast_to(a.reshape(1, -1), (n, a.size)))

    def by_tile(a, tiles):
        return np.ascontiguousarray(a.reshape(tiles, 128, -1).transpose(1, 0, 2).reshape(128, -1))

    a = {k.removeprefix("L0_"): np.asarray(v) for k, v in inputs.items()}
    side, p = 14, 16
    x = a["x"].reshape(GROUPS, SEQS, 3, side, p, side, p).transpose(0, 2, 4, 6, 1, 3, 5)
    x = x.reshape(GROUPS, KP, 128, T).transpose(0, 2, 1, 3).reshape(GROUPS, 128, KP * T)

    def experts(shared, routed):
        return np.concatenate([a[shared][None], a[routed]], 0)

    arrays = {
        "patches": x,
        "tok_w": by_tile(a["tok_W"].T, KP),
        "tok_b": rows(a["tok_b"], H),
        "pos": a["tok_pos"].reshape(2, H, MODEL).transpose(1, 0, 2).reshape(H, 2 * MODEL),
        "ln_w": a["attn_ln_w"].reshape(MODEL, 1),
        "ln_b": a["attn_ln_b"].reshape(MODEL, 1),
        "w1": np.concatenate([a["attn_in_proj_w"], a["attn_gate_w"]], 1),
        "conv_w": a["attn_conv_w"].reshape(4, 128, TAPS).transpose(1, 0, 2),
        "conv_b": a["attn_conv_b"].reshape(4, 128).T,
        "dt_bias": rows(a["attn_dt_bias"], H),
        "A_log": rows(a["attn_A_log"], H),
        "D": np.repeat(a["attn_D_param"], HD).reshape(NI, 128).T,
        "rms_w": a["attn_rms_w"].reshape(NI, 128).T,
        "out_proj": by_tile(a["attn_out_proj_w"], NI),
        "gate_b": a["attn_gate_b"].reshape(MODEL, 1),
        "out_w": a["attn_out_w"],
        "out_b": rows(a["attn_out_b"], H),
        "experts_gate": experts("ffn_shared_gate", "ffn_routed_gate").transpose(1, 0, 2).reshape(MODEL, EXPERTS * FF),
        "experts_up": experts("ffn_shared_up", "ffn_routed_up").transpose(1, 0, 2).reshape(MODEL, EXPERTS * FF),
        "down": by_tile(experts("ffn_shared_down", "ffn_routed_down").reshape(EXPERTS * FF, MODEL), FTILES),
        "router_w": a["ffn_router_w"],
        "routing_bias": rows(a["ffn_routing_bias"], H),
    }
    arrays = {k: np.ascontiguousarray(v) for k, v in arrays.items()}
    nc = bacc.Bacc("TRN2", target_bir_lowering=False, num_devices=1)
    dram = {k: nc.dram_tensor(f"in_{k}", v.shape, F32, kind="ExternalInput").ap() for k, v in arrays.items()}
    dram["out"] = nc.dram_tensor("out", [GROUPS, H, TILES * MODEL], F32, kind="ExternalOutput").ap()
    build(nc, dram)
    out = run_bass_kernel_spmd(nc, [{f"in_{k}": v for k, v in arrays.items()}], core_ids=[0]).results[0]["out"]
    out = out.reshape(GROUPS, H, SEQS, 2, MODEL).transpose(0, 2, 3, 1, 4)
    return np.ascontiguousarray(out.reshape(BATCH, TOKENS, MODEL))
```

```python
from contextlib import ExitStack

import concourse.bass as bass
from concourse import mybir
from concourse.alu_op_type import AluOpType as ALU

F32 = mybir.dt.float32
F16 = mybir.dt.float16
BF16 = mybir.dt.bfloat16
ACT = mybir.ActivationFunctionType

BATCH, TOKENS, MODEL = 128, 196, 192
SEQS = 2
GROUPS = BATCH // SEQS
T = SEQS * TOKENS
H = TOKENS // 2
TILES = T // H
KA, KB = 128, 64
PATCH = 768
KP = PATCH // 128
INNER, STATE, HEADS, HD = 384, 64, 6, 64
TAPS = 4
NI = INNER // 128
EXPERTS = 4
ROUTED = 3
FF = 384
NF = FF // 128
FTILES = EXPERTS * NF
EPS = 1e-5
CAUSAL = TOKENS + H
WSCALE = 64.0

COL_Z, COL_X, COL_BC, COL_DT, COL_GATE = 0, 384, 768, 896, 902
W1_COLS = COL_GATE + MODEL
PROJ = {"z0": (0, 128), "z1": (128, 128), "z2": (256, 128), "x0": (384, 128), "x1": (512, 128), "x2": (640, 128),
        "bc": (COL_BC, 128), "ga": (COL_GATE, KA), "gb": (COL_GATE + KA, KB)}
PROJ_AT = {name: n for n, name in enumerate(PROJ)}

ORDER = """
    embed0 comb0 f0 h0 comb1 embed1 xt0 cb0 norm1 f1 xt1 cb1 h1 f2 xn1 g0 comb2 comb3 comb4 xt2 g1 h2 f3 comb5
    w0 ta tb h3 cb2 f4 xt3 comb6 h4 w1 x0 dt soft0 soft1 f5 comb7 d00 soft2 soft3 soft4 w2 soft5 soft6 h5 w3 cb3
    x1 f6 cb4 cb5 soft7 h6 y0 d01 soft8 x2 comb8 w4 bc soft9 w5 conv0 y1 comb9 y2 comb10 conv1 soft10 conv2
    soft11 d10 silu0 f7 h7 soft12 oa soft13 conv3 z0 gate f8 h8 ob f9 ss d11 sz0 split cum ow0 store ow1 h9
    norm2 f10 z1 h10 z2 f11 xn2 silu1 d20 ga silu2 f12 h11 sz1 d21 t2a t2b gb d30 silu3 cpart route base sz2 d31
""".split()
FRONT, BACK, LATE = 0, 1, 2


def stage_of(step):
    kind = step.rstrip("0123456789")
    if kind in ("f", "h", "d", "comb", "store"):
        return LATE
    if step in ("norm2", "xn2") or kind in ("g", "cb", "w", "xt", "y", "gate", "oa", "ob", "ss", "ow", "t2a", "t2b", "route"):
        return BACK
    return FRONT


OTHER_STEPS = ("norm", "soft", "conv", "silu", "w", "gate", "split", "store", "base", "sz", "xn")
MIX_BANKS = 3
UNITS = [u for u in ORDER if stage_of(u) != LATE and u.rstrip("0123456789") not in OTHER_STEPS]
UNIT_BANK = {u: n % MIX_BANKS for n, u in enumerate(UNITS)}


def nth_unit(unit, stages):
    same = [u for u in UNITS if UNIT_BANK[u] == UNIT_BANK[unit] and stage_of(u) in stages]
    return same.index(unit) + 1


PIECE_STEPS = [f"f{t}" for t in range(11)]


def latest(*units, before=None):
    banks = [b for b in range(MIX_BANKS) if before is None or b != UNIT_BANK[before]]
    return [max((u for u in units if UNIT_BANK[u] == b), key=UNITS.index) for b in banks
            if any(UNIT_BANK[u] == b for u in units)]


SOFT_STEPS, COMB_STEPS = 14, 11
CONSTS = 15


class Count:

    def __init__(self, sem, per):
        self.sem, self.per = sem, per

    def at(self, group, nth):
        i, off = group
        return i * self.per + (self.per * off + nth)

    def any(self, group, nth):
        i, off = group
        return not isinstance(i, int) or self.per * (i + off) + nth > 0


class Unit(Count):

    def __init__(self, sem, unit):
        bank = [stage_of(u) for u in UNITS if UNIT_BANK[u] == UNIT_BANK[unit]]
        super().__init__(sem, len(bank))
        self.stage, self.backs = stage_of(unit), bank.count(BACK)
        self.first = nth_unit(unit, (FRONT,)) if self.stage == FRONT else 0
        self.nth = nth_unit(unit, (FRONT, BACK))
        self.last = nth_unit(unit, (BACK,)) if self.stage == BACK else 0

    def at(self, group, back=0):
        i, off = group
        off += self.stage
        if isinstance(i, int) and i + off == 0:
            return self.first + back
        nth = self.last if isinstance(i, int) and i + off == GROUPS else self.nth
        return i * self.per + (self.per * off - self.backs + nth + back)

    def any(self, group, back=0):
        i, off = group
        return not isinstance(i, int) or (i + off >= 0 and self.at(group, back) > 0)


class Chain(Count):

    def __init__(self, sem):
        super().__init__(sem, 0)
        self.marks = 0

    def begin(self, group):
        if self.marks:
            self.per = self.marks
        self.marks = 0
        self.group = group

    def mark(self):
        self.marks += 1
        return self.sem

    def now(self):
        return self.at(self.group, self.marks)


def build(nc, D):
    with ExitStack() as ctx:
        def sb(name, shape, dt=F32):
            return ctx.enter_context(nc.sbuf_tensor(name, shape, dt))

        def sem(name):
            return ctx.enter_context(nc.semaphore(name))

        bank = [ctx.enter_context(nc.psum_tensor(f"mix{b}", [128, 512], F32)) for b in range(MIX_BANKS)]
        bankb = [b[:, :].bitcast(BF16) for b in bank]
        gate_ps = [ctx.enter_context(nc.psum_tensor(f"gate{b}", [128, 512], F32)) for b in range(2)]
        up_ps = [ctx.enter_context(nc.psum_tensor(f"up{b}", [128, 512], F32)) for b in range(2)]
        down_ps = ctx.enter_context(nc.psum_tensor("down", [128, 512], F32))

        ident = sb("ident", [128, 128])
        identb = sb("identb", [128, 128], BF16)
        upper = sb("upper", [H, H])
        ones = sb("ones", [128, H])
        causal = sb("causal", [H, CAUSAL])
        pick = sb("pick", [96, HEADS, H], BF16)
        power = sb("power", [128, 8])
        zb, zt = sb("zb", [128, NI, T]), sb("zt", [128, NI, T])
        w1a_raw = zb[:, :, :].rearrange("p k t -> p (k t)")[:, 0:W1_COLS]
        w1b_raw = zt[:, :, :].rearrange("p k t -> p (k t)")[:, 0:W1_COLS]
        w1a_hi, w1a_lo = sb("w1a_hi", [KA, W1_COLS], F16), sb("w1a_lo", [KA, W1_COLS], F16)
        w1b_hi, w1b_lo = sb("w1b_hi", [128, W1_COLS], F16), sb("w1b_lo", [KB, W1_COLS], F16)
        lnwa, lnwb, lnba, lnbb = sb("lnwa", [KA, 1]), sb("lnwb", [128, 1]), sb("lnba", [KA, 1]), sb("lnbb", [KB, 1])
        conv = sb("conv", [128, 4, SEQS, TOKENS])
        tok_raw = conv[:, :, :, :].rearrange("p k s t -> p (k s t)")[:, 0:KP * MODEL]
        gua_hi = [sb(f"{n}a_hi", [KA, EXPERTS * FF], F16) for n in ("wg", "wu")]
        gua_lo = [sb(f"{n}a_lo", [KA, EXPERTS * FF], F16) for n in ("wg", "wu")]
        gub_hi = [sb(f"{n}b_hi", [128, EXPERTS * FF], F16) for n in ("wg", "wu")]
        gub_lo = sb("wgub_lo", [128, EXPERTS * FF], F16)
        down_hi, down_lo = sb("down_hi", [128, FTILES * MODEL], F16), sb("down_lo", [128, FTILES * MODEL], F16)
        tok_hi, tok_lo = sb("tok_hi", [128, KP * MODEL], F16), sb("tok_lo", [128, KP * MODEL], F16)
        outp = sb("outp", [128, NI * MODEL])
        rms = sb("rms", [128, NI])
        owa, owb = sb("owa", [KA, MODEL]), sb("owb", [KB, MODEL])
        ra_raw, rb_raw = sb("ra_raw", [KA, ROUTED]), sb("rb_raw", [128, ROUTED])
        ra_hi, ra_lo = sb("ra_hi", [KA, ROUTED], F16), sb("ra_lo", [KA, ROUTED], F16)
        rb_hi, rb_lo = sb("rb_hi", [128, ROUTED], F16), sb("rb_lo", [KB, ROUTED], F16)
        pos = sb("pos", [H, 2 * MODEL])
        tokb = sb("tokb", [H, MODEL])
        outb = sb("outb", [H, MODEL])
        convw, convb = sb("convw", [128, 4, TAPS]), sb("convb", [128, 4])
        dpar, dhalf = sb("dpar", [128, NI]), sb("dhalf", [128, NI])
        alog, aneg = sb("alog", [H, HEADS]), sb("aneg", [H, HEADS])
        dtb, dtbias = sb("dtb", [H, HEADS]), sb("dtbias", [H, HEADS])
        gba, gbb = sb("gba", [KA, 1]), sb("gbb", [KB, 1])
        rbias = sb("rbias", [H, ROUTED])
        pbias = sb("pbias", [128, len(PROJ)])
        gbias = sb("gbias", [128, 2])

        patches = sb("patches", [128, KP * T])
        pat_hi, pat_lo = sb("pat_hi", [128, KP * T], F16), sb("pat_lo", [128, KP * T], F16)
        h1 = sb("h1", [H, TILES, MODEL])
        base = sb("base", [H, TILES, MODEL])
        rows1 = sb("rows", [H, TILES, MODEL])
        rows2 = sb("rows2", [H, TILES, MODEL])
        stats, small = sb("stats", [H, TILES, 6]), sb("small", [H, 6, TILES])
        roots_in, roots = sb("roots_in", [H, 8]), sb("roots", [H, 8])
        stats2, small2 = sb("stats2", [H, TILES, 6]), sb("small2", [H, 5, TILES])
        roots2_in, roots2 = sb("roots2_in", [H, TILES]), sb("roots2", [H, TILES])
        xa_hi, xa_lo, xb_hl = sb("xa_hi", [KA, T], F16), sb("xa_lo", [KA, T], F16), sb("xb_hl", [128, T], F16)
        dt_raw = sb("dt_raw", [H, TILES, HEADS])
        sp = sb("sp", [H, 8, TILES * HEADS])
        dta = sb("dta", [H, TILES, HEADS])
        dth = sb("dth", [H, TILES, HEADS])
        csum = sb("csum", [H, TILES, HEADS])
        crest = sb("crest", [H, TILES, HEADS])
        cpt = sb("cpt", [H, TILES, 96], BF16)
        cumpart = sb("cumpart", [96, T], BF16)
        ncum = sb("ncum", [H, TILES, HEADS])
        xpad = sb("xpad", [128, 4, SEQS, TAPS - 1 + TOKENS])
        convt = sb("convt", [128, 4, SEQS, TOKENS])
        xs = sb("xs", [128, NI, T])
        bs, cs = sb("bs", [STATE, T]), sb("cs", [STATE, T])
        zs = sb("zs", [128, NI, T])
        gt = sb("gt", [128, 2, T])
        gm = sb("gm", [H, SEQS, CAUSAL])
        xdt = sb("xdt", [H, TILES, INNER])
        decay = sb("decay", [H, 2, SEQS, CAUSAL])
        wgt = sb("wgt", [H, HEADS, SEQS, CAUSAL])
        y1 = sb("y1", [128, NI, T])
        y2 = sb("y2", [128, NI, T])
        sq = sb("sq", [128, NI, T])
        gated = sb("gated", [128, 2, T])
        rinv_in, rinv = sb("rinv_in", [H, TILES]), sb("rinv", [H, TILES])
        h2 = sb("h2", [H, TILES, MODEL])
        fa_hi, fa_lo, fb_hl = sb("fa_hi", [KA, T], F16), sb("fa_lo", [KA, T], F16), sb("fb_hl", [128, T], F16)
        fb_up = sb("fb_up", [128, T], F16)
        rl = sb("rl", [H, TILES, ROUTED])
        rs = sb("rs", [H, 6, TILES, ROUTED])
        comb = sb("comb", [H, TILES, ROUTED])
        ft = sb("ft", [128, 2, T])
        fg = sb("fg", [128, 2, T])
        fh = sb("fh", [128, 2, T])
        fh_hi, fh_lo = sb("fh_hi", [128, 2, NF, T], F16), sb("fh_lo", [128, 2, NF, T], F16)
        acc = sb("acc", [H, TILES, MODEL])

        s_tok = sem("embedding_loaded")
        s_load, s_const, s_prep = sem("weights_loaded"), sem("constants_ready"), sem("prologue_step")
        s_split, s_bias = sem("weights_split"), sem("bias_products")
        piece_in = [sem(f"piece_buffer{b}_loaded") for b in range(3)]
        piece_hi, piece_lo = sem("piece_hi"), sem("piece_lo")
        bank_full, bank_emptied = ([sem(f"mix{b}_{state}") for b in range(MIX_BANKS)] for state in ("full", "emptied"))
        full = {u: Unit(bank_full[UNIT_BANK[u]], u) for u in UNITS}
        emptied = {u: Unit(bank_emptied[UNIT_BANK[u]], u) for u in UNITS}
        patch_in = Count(sem("patches_loaded"), 16)
        patch_hi = Count(sem("patches_hi"), 1)
        patch_lo = Count(sem("patches_lo"), 1)
        roots_asked, roots_done = Count(sem("roots1_asked"), 1), Count(sem("roots1_done"), 1)
        roots2_asked, roots2_done = Count(sem("roots2_asked"), 1), Count(sem("roots2_done"), 2)
        xn_ready, xn2_ready = Count(sem("xn_ready"), 1), Count(sem("xn2_ready"), 1)
        shift_ready, shift2_ready = Count(sem("shift_ready"), 1), Count(sem("shift2_ready"), 1)
        normed = Count(sem("residual_norm_ready"), 1)
        base_ready = Count(sem("base_ready"), 1)
        hi_ready, hi2_ready = Count(sem("projection_hi_ready"), 2), Count(sem("expert_hi_ready"), 2)
        soft_in, soft_e = Count(sem("softplus_in"), 1), Count(sem("softplus_exp"), 1)
        dta_ready = Count(sem("dta_ready"), 1)
        ncum_ready = Count(sem("ncum_ready"), 1)
        cpt_ready = Count(sem("cum_parts_ready"), 1)
        tap0_ready = Count(sem("first_tap_ready"), 4)
        zs_ready = Count(sem("zs_ready"), NI)
        conv_ready, convt_ready = Count(sem("conv_ready"), 4), Count(sem("conv_tanh"), 4)
        silu_ready = Count(sem("silu_ready"), 4)
        decay_ready, wgt_ready = Count(sem("decay_ready"), HEADS), Count(sem("wgt_ready"), HEADS)
        y2_ready = Count(sem("y2_ready"), NI)
        sq_ready, sqsum_ready = Count(sem("squares"), NI), Count(sem("square_sums"), 1)
        router_e = Count(sem("router_exp"), 1)
        gate_full, up_full = Count(sem("gate_full"), FTILES), Count(sem("up_full"), FTILES)
        ft_ready = Count(sem("expert_tanh"), FTILES)
        fg_ready = Count(sem("fg_ready"), FTILES)
        fh_ready = Count(sem("fh_ready"), FTILES)
        fhi_ready, flo_ready = Count(sem("fh_hi_ready"), FTILES), Count(sem("fh_lo_ready"), FTILES)
        down_full, down_free = Count(sem("down_full"), SEQS * EXPERTS), Count(sem("down_emptied"), SEQS * EXPERTS)
        stored = Count(sem("stored"), 16)
        dve_front, dve_back = Chain(sem("dve_front_step")), Chain(sem("dve_back_step"))
        dve_soft, dve_comb = Chain(sem("softplus_step")), Chain(sem("combine_step"))
        act_front = Chain(sem("act_front_step"))
        pool_front, pool_back = Chain(sem("pool_front_step")), Chain(sem("pool_back_step"))

        def before(g):
            return g[0], g[1] - 1

        def turns(eng, steps, begin=lambda *stages: None):
            def turn(i, front=True, back=True, late=True, split=True):
                runs = (front, back, late)
                begin(i, *runs)
                for name in ORDER:
                    if not back and not late and name in PIECE_STEPS and "piece" in steps:
                        steps["piece"](PIECE_STEPS.index(name))
                    if name not in steps:
                        continue
                    if name == "split":
                        if split:
                            steps[name]((i, 1))
                    elif runs[stage_of(name)]:
                        steps[name]((i, -stage_of(name)))
            turn(0, back=False, late=False)
            turn(1, late=False)
            turn(2)
            with eng.Fori(3, GROUPS - 1) as i:
                turn(i)
            turn(GROUPS - 1, split=False)
            turn(GROUPS, front=False, split=False)
            turn(GROUPS + 1, front=False, back=False, split=False)

        block = ctx.enter_context(nc.Block())

        loads = [
            (w1a_raw, D["w1"][0:KA, :]), (w1b_raw[0:KB, :], D["w1"][KA:MODEL, :]), (w1b_raw[KB:128, :], D["w1"][KA:MODEL, :]),
            (lnwa, D["ln_w"][0:KA, :]), (lnwb[0:KB, :], D["ln_w"][KA:MODEL, :]), (lnwb[KB:128, :], D["ln_w"][KA:MODEL, :]),
            (lnba, D["ln_b"][0:KA, :]), (lnbb, D["ln_b"][KA:MODEL, :]),
            (outp, D["out_proj"]), (rms, D["rms_w"]), (owa, D["out_w"][0:KA, :]), (owb, D["out_w"][KA:MODEL, :]),
            (ra_raw, D["router_w"][0:KA, :]), (rb_raw[0:KB, :], D["router_w"][KA:MODEL, :]), (rb_raw[KB:128, :], D["router_w"][KA:MODEL, :]),
            (pos, D["pos"]), (tokb, D["tok_b"]), (outb, D["out_b"]), (convw, D["conv_w"]), (convb, D["conv_b"]), (dpar, D["D"]),
            (alog, D["A_log"]), (dtb, D["dt_bias"]), (gba, D["gate_b"][0:KA, :]), (gbb, D["gate_b"][KA:MODEL, :]), (rbias, D["routing_bias"]),
        ]
        PIECE = 2 * FF
        piece_raw = [t[:, :, :].rearrange("p k t -> p (k t)")[:, 0:PIECE] for t in (ft, fg, fh)]
        pieces = []
        for c in range(0, FTILES * MODEL, PIECE):
            cols = slice(c, c + PIECE)
            pieces.append((down_hi[:, cols], down_lo[:, cols], slice(0, 128), [(slice(0, 128), D["down"][:, cols])]))
        for w, src in enumerate((D["experts_gate"], D["experts_up"])):
            for c in range(0, EXPERTS * FF, PIECE):
                cols = slice(c, c + PIECE)
                pieces.append((gua_hi[w][:, cols], gua_lo[w][:, cols], slice(0, KA), [(slice(0, KA), src[0:KA, cols])]))
                low = slice(w * KB, (w + 1) * KB)
                pieces.append((gub_hi[w][:, cols], gub_lo[low, cols], low,
                               [(slice(0, KB), src[KA:MODEL, cols]), (slice(KB, 128), src[KA:MODEL, cols])]))
        loads_to = [sum(len(p[3]) for p in pieces[n % len(piece_raw):n + 1:len(piece_raw)]) for n in range(len(pieces))]

        @block.sync
        def _(sp_eng):
            def load_patches(g):
                i, off = g
                if patch_lo.any(g, 0):
                    sp_eng.wait_ge(patch_lo.sem, patch_lo.at(g, 0))
                at = i + off
                src = D["patches"][at] if isinstance(at, int) else D["patches"][bass.ds(at, 1)].rearrange("g p n -> (g p) n")
                sp_eng.dma_start(patches[:, :], src).then_inc(patch_in.sem, 16)

            def store(g):
                i, off = g
                sp_eng.wait_ge(down_free.sem, down_free.at(g, SEQS * EXPERTS))
                at = i + off
                dst = D["out"][at] if isinstance(at, int) else D["out"][bass.ds(at, 1)].rearrange("g p n -> (g p) n")
                sp_eng.dma_start(dst, acc[:, :, :].rearrange("p j n -> p (j n)")).then_inc(stored.sem, 16)

            def load_piece(n):
                if n >= len(piece_raw):
                    sp_eng.wait_ge(piece_lo, n + 1 - len(piece_raw))
                for rows, src in pieces[n][3]:
                    sp_eng.dma_start(piece_raw[n % len(piece_raw)][rows, :], src).then_inc(piece_in[n % len(piece_raw)], 16)

            def piece(n):
                if n + len(piece_raw) < len(pieces):
                    load_piece(n + len(piece_raw))

            sp_eng.dma_start(tok_raw, D["tok_w"]).then_inc(s_tok, 16)
            load_patches((0, 0))
            for dst, src in loads:
                sp_eng.dma_start(dst if isinstance(dst, bass.AP) else dst[:], src).then_inc(s_load, 16)
            for n in range(len(piece_raw)):
                load_piece(n)
            turns(sp_eng, {"embed0": lambda g: None, "split": load_patches, "store": store, "piece": piece})
            sp_eng.wait_ge(stored.sem, 16 * GROUPS)

        @block.gpsimd
        def _(pool):
            gp = nc.gpsimd

            fills = ((ident, 0.0), (upper, 1.0), (causal, 0.25), (ones, 1.0), (power, -0.5), (pick, 0.0), (cpt, 0.0),
                     (xpad, 0.0))
            for tensor, value in fills:
                gp.memset(tensor[:], value).then_inc(s_const, 1)
            pool.wait_ge(s_const, len(fills))
            gp.affine_select(out=ident[:, :], in_=ident[:, :], compare_op=ALU.not_equal, fill=1.0, base=0,
                             pattern=[[-1, 128]], channel_multiplier=1).then_inc(s_const, 1)
            pool.wait_ge(s_const, len(fills) + 1)
            for n, part in enumerate((upper[:, :], causal[:, 0:TOKENS], causal[:, TOKENS:CAUSAL])):
                gp.affine_select(out=part, in_=part, compare_op=ALU.is_ge, fill=0.0, base=0,
                                 pattern=[[1, part.shape[1]]], channel_multiplier=-1).then_inc(s_const, 1)
                pool.wait_ge(s_const, len(fills) + 2 + n)
            for n in range(3):
                rows = pick[32 * n:32 * n + 32, :, :]
                gp.affine_select(out=rows, in_=rows, compare_op=ALU.not_equal, fill=1.0, base=0,
                                 pattern=[[-1, HEADS], [0, H]], channel_multiplier=1).then_inc(s_const, 1)
                pool.wait_ge(s_const, len(fills) + 5 + n)

            def piece(n):
                hi, lo, rows, _ = pieces[n]
                pool.wait_ge(piece_hi, n + 1)
                gp.tensor_tensor(lo, piece_raw[n % len(piece_raw)][rows, :], hi[rows], ALU.subtract).then_inc(piece_lo, 1)
                pool.wait_ge(piece_lo, n + 1)

            def split_lo(g):
                pool.wait_ge(patch_hi.sem, patch_hi.at(g, 1))
                gp.tensor_tensor(pat_lo[:, :], patches[:, :], pat_hi[:, :], ALU.subtract).then_inc(patch_lo.sem, 1)
                pool.wait_ge(patch_lo.sem, patch_lo.at(g, 1))

            def norm1(g):
                pool.wait_ge(roots_asked.sem, roots_asked.at(g, 1))
                gp.tensor_tensor(roots[:, :], roots_in[:, :], power[0:H, :], ALU.pow).then_inc(roots_done.sem, 1)

            def add_base(g):
                pool.wait_ge(normed.sem, normed.at(g, 1))
                flat = [t[:, :, :].rearrange("p j n -> p (j n)") for t in (base, h1)]
                gp.tensor_tensor(flat[0], flat[0], flat[1], ALU.add).then_inc(pool_front.mark(), 1)
                pool.wait_ge(pool_front.sem, pool_front.now())
                gp.tensor_tensor(base[:, :, :], base[:, :, :], outb[:, :].unsqueeze(1).to_broadcast([H, TILES, MODEL]),
                                 ALU.add).then_inc(base_ready.sem, 1)

            def gate_y(g, n):
                pool.wait_ge(emptied[f"y{n}"].sem, emptied[f"y{n}"].at(g))
                pool.wait_ge(zs_ready.sem, zs_ready.at(g, n + 1))
                if n == 0 and full["ob"].any(before(g)):
                    pool.wait_ge(full["ob"].sem, full["ob"].at(before(g)))
                    pool.wait_ge(sq_ready.sem, sq_ready.at(g, 0))
                gp.tensor_tensor(y2[:, n, :], y1[:, n, :], zs[:, n, :], ALU.mult).then_inc(y2_ready.sem, 1)

            def sum_squares(g):
                pool.wait_ge(sq_ready.sem, sq_ready.at(g, NI))
                gp.tensor_tensor(sq[:, 0, :], sq[:, 0, :], sq[:, 1, :], ALU.add).then_inc(pool_back.mark(), 1)
                pool.wait_ge(pool_back.sem, pool_back.now())
                gp.tensor_tensor(sq[:, 0, :], sq[:, 0, :], sq[:, 2, :], ALU.add).then_inc(sqsum_ready.sem, 1)

            def ss(g):
                pool.wait_ge(emptied["ss"].sem, emptied["ss"].at(g))
                gp.tensor_tensor(rinv[:, :], rinv_in[:, :], power[0:H, 0:TILES], ALU.pow).then_inc(roots2_done.sem, 1)

            def norm2(g):
                pool.wait_ge(roots2_asked.sem, roots2_asked.at(g, 1))
                gp.tensor_tensor(roots2[:, :], roots2_in[:, :], power[0:H, 0:TILES], ALU.pow).then_inc(roots2_done.sem, 1)

            def lo(g, t):
                if t:
                    pool.wait_ge(fhi_ready.sem, fhi_ready.at(g, t))
                    e, k = divmod(t - 1, NF)
                    gp.tensor_tensor(fh_lo[:, e % 2, k, :], fh[:, (t - 1) % 2, :], fh_hi[:, e % 2, k, :],
                                     ALU.subtract).then_inc(flo_ready.sem, 1)

            steps = {"piece": piece, "split": split_lo, "norm1": norm1, "base": add_base, "oa": sum_squares, "ss": ss, "norm2": norm2}
            for n in range(NI):
                steps[f"y{n}"] = lambda g, n=n: gate_y(g, n)
            for t in range(FTILES + 1):
                steps[f"f{t}"] = lambda g, t=t: lo(g, t)
            split_lo((0, 0))

            def begin(i, front, back, late):
                if front:
                    pool_front.begin((i, 0))
                if back:
                    pool_back.begin((i, -1))
            turns(pool, steps, begin)

        @block.scalar
        def _(act):
            A = nc.scalar.activation

            def split_hi(g):
                act.wait_ge(patch_in.sem, patch_in.at(g, 16))
                if not (isinstance(g[0], int) and g == (0, 0)):
                    if full["embed1"].any(before(g)):
                        act.wait_ge(full["embed1"].sem, full["embed1"].at(before(g)))
                A(pat_hi[:, :], patches[:, :], ACT.Copy).then_inc(patch_hi.sem, 1)

            def hi_a(g, u, out, ready):
                act.wait_ge(full[u].sem, full[u].at(g))
                A(out, bank[UNIT_BANK[u]][0:out.shape[0], 0:T], ACT.Copy).then_inc(ready.sem, 1)

            def ta(g):
                if full["gb"].any(before(g)):
                    act.wait_ge(full["gb"].sem, full["gb"].at(before(g)))
                hi_a(g, "ta", xa_hi[:, :], hi_ready)

            def tb(g):
                hi_a(g, "tb", xb_hl[0:KB, :], hi_ready)

            def t2a(g):
                if up_full.any(before(g), FTILES):
                    act.wait_ge(up_full.sem, up_full.at(before(g), FTILES))
                if full["route"].any(before(g)):
                    act.wait_ge(full["route"].sem, full["route"].at(before(g)))
                hi_a(g, "t2a", fa_hi[:, :], hi2_ready)

            def t2b(g):
                act.wait_ge(full["t2b"].sem, full["t2b"].at(g))
                A(fb_up[KB:128, :], bank[UNIT_BANK["t2b"]][0:KB, 0:T], ACT.Copy)
                hi_a(g, "t2b", fb_hl[0:KB, :], hi2_ready)

            def project_x(g, k):
                u = f"x{k}" if k < NI else "bc"
                act.wait_ge(full[u].sem, full[u].at(g))
                if conv_ready.any(g, k + 1 - 4):
                    act.wait_ge(conv_ready.sem, conv_ready.at(g, k + 1 - 4))
                n = PROJ_AT[u]
                A(xpad[:, k, :, TAPS - 1:], bank[UNIT_BANK[u]][:, 0:T].rearrange("p (s t) -> p s t", s=SEQS),
                  ACT.Identity, bias=pbias[:, n:n + 1], scale=1.0 / WSCALE).then_inc(emptied[u].sem, 1)
                act.wait_ge(emptied[u].sem, emptied[u].at(g))
                if silu_ready.any(g, k + 1 - 4):
                    act.wait_ge(silu_ready.sem, silu_ready.at(g, k + 1 - 4))
                A(conv[:, k, :, :], xpad[:, k, :, 0:TOKENS], ACT.Identity, bias=convb[:, k:k + 1],
                  scale=convw[:, k, 0:1]).then_inc(tap0_ready.sem, 1)

            def cum_parts(g):
                act.wait_ge(full["cpart"].sem, full["cpart"].at(g))
                if full["cb5"].any(before(g)):
                    act.wait_ge(full["cb5"].sem, full["cb5"].at(before(g)))
                A(cumpart[:, :], bankb[UNIT_BANK["cpart"]][0:96, 0:T], ACT.Copy).then_inc(emptied["cpart"].sem, 1)

            def norm_residual(g):
                act.wait_ge(shift_ready.sem, shift_ready.at(g, 1))
                if emptied["ow1"].any(before(g)):
                    act.wait_ge(emptied["ow1"].sem, emptied["ow1"].at(before(g)))
                for j in range(TILES):
                    ins = A(base[:, j, :], h1[:, j, :], ACT.Identity, bias=small[:, 4, j:j + 1], scale=roots[:, j:j + 1])
                ins.then_inc(normed.sem, 1)

            def xn1(g):
                act.wait_ge(shift_ready.sem, shift_ready.at(g, 1))
                if full["tb"].any(before(g)):
                    act.wait_ge(full["tb"].sem, full["tb"].at(before(g)))
                for j in range(TILES):
                    ins = A(rows1[:, j, :], h1[:, j, :], ACT.Identity, bias=small[:, 5, j:j + 1],
                            scale=roots[:, TILES + j:TILES + j + 1])
                ins.then_inc(xn_ready.sem, 1)

            def xn2(g):
                act.wait_ge(shift2_ready.sem, shift2_ready.at(g, 1))
                if full["t2b"].any(before(g)):
                    act.wait_ge(full["t2b"].sem, full["t2b"].at(before(g)))
                for j in range(TILES):
                    ins = A(rows2[:, j, :], h2[:, j, :], ACT.Identity, bias=small2[:, 4, j:j + 1], scale=roots2[:, j:j + 1])
                ins.then_inc(xn2_ready.sem, 1)

            def tanh_conv(g, k):
                act.wait_ge(conv_ready.sem, conv_ready.at(g, k + 1))
                if silu_ready.any(g, k + 1 - 4):
                    act.wait_ge(silu_ready.sem, silu_ready.at(g, k + 1 - 4))
                A(convt[:, k, :, :], conv[:, k, :, :], ACT.Tanh, scale=0.5).then_inc(convt_ready.sem, 1)

            def project_z(g, k):
                u = f"z{k}"
                act.wait_ge(full[u].sem, full[u].at(g))
                if zs_ready.any(g, k + 1 - NI):
                    act.wait_ge(zs_ready.sem, zs_ready.at(g, k + 1 - NI))
                n = PROJ_AT[u]
                A(zb[:, k, :], bank[UNIT_BANK[u]][:, 0:T], ACT.Identity, bias=pbias[:, n:n + 1],
                  scale=1.0 / WSCALE).then_inc(act_front.mark(), 1)
                act.wait_ge(act_front.sem, act_front.now())
                A(zt[:, k, :], zb[:, k, :], ACT.Tanh, scale=0.5).then_inc(emptied[u].sem, 1)

            def gate_tanh(g, k):
                u = ("ga", "gb")[k]
                rows = (KA, KB)[k]
                act.wait_ge(full[u].sem, full[u].at(g))
                if emptied[("oa", "ob")[k]].any(before(g)):
                    act.wait_ge(emptied[("oa", "ob")[k]].sem, emptied[("oa", "ob")[k]].at(before(g)))
                A(gt[0:rows, k, :], bank[UNIT_BANK[u]][0:rows, 0:T], ACT.Tanh, bias=gbias[0:rows, k:k + 1],
                  scale=0.5 / WSCALE).then_inc(emptied[u].sem, 1)

            def soft(g):
                act.wait_ge(soft_in.sem, soft_in.at(g, 1))
                A(sp[:, 1, :], sp[:, 0, :], ACT.Exp, scale=-1.0).then_inc(soft_e.sem, 1)

            def decays(g, h):
                u = f"cb{h}"
                act.wait_ge(full[u].sem, full[u].at(g))
                if h == 0:
                    act.wait_ge(ncum_ready.sem, ncum_ready.at(g, 1))
                if wgt_ready.any(g, h + 1 - 2):
                    act.wait_ge(wgt_ready.sem, wgt_ready.at(g, h + 1 - 2))
                ps = bank[UNIT_BANK[u]]
                for s in range(SEQS):
                    t0 = s * TOKENS
                    A(decay[:, h % 2, s, 0:TOKENS], ps[0:H, t0:t0 + TOKENS], ACT.Exp, bias=ncum[:, 2 * s, h:h + 1])
                    ins = A(decay[:, h % 2, s, TOKENS:CAUSAL], ps[0:H, t0 + H:t0 + TOKENS], ACT.Exp,
                            bias=ncum[:, 2 * s + 1, h:h + 1])
                ins.then_inc(emptied[u].sem, 1)

            def square(g, m):
                act.wait_ge(y2_ready.sem, y2_ready.at(g, m + 1))
                if m == 0:
                    if full["ss"].any(before(g)):
                        act.wait_ge(full["ss"].sem, full["ss"].at(before(g)))
                A(sq[:, m, :], y2[:, m, :], ACT.Square).then_inc(sq_ready.sem, 1)

            def expert(g, t):
                if t < FTILES:
                    act.wait_ge(gate_full.sem, gate_full.at(g, t + 1))
                    if fh_ready.any(g, t + 1 - 2):
                        act.wait_ge(fh_ready.sem, fh_ready.at(g, t + 1 - 2))
                    A(ft[:, t % 2, :], gate_ps[t % 2][:, 0:T], ACT.Tanh, scale=0.5).then_inc(ft_ready.sem, 1)
                if t:
                    e, k = divmod(t - 1, NF)
                    act.wait_ge(fh_ready.sem, fh_ready.at(g, t))
                    if down_full.any(g, SEQS * (e - 1)):
                        act.wait_ge(down_full.sem, down_full.at(g, SEQS * (e - 1)))
                    A(fh_hi[:, e % 2, k, :], fh[:, (t - 1) % 2, :], ACT.Copy).then_inc(fhi_ready.sem, 1)

            def route_exp(g):
                act.wait_ge(emptied["route"].sem, emptied["route"].at(g))
                A(rs[:, 0, :, :], rl[:, :, :], ACT.Exp, scale=-1.0).then_inc(router_e.sem, 1)

            def piece(n):
                act.wait_ge(piece_in[n % len(piece_raw)], 16 * loads_to[n])
                A(pieces[n][0], piece_raw[n % len(piece_raw)], ACT.Copy).then_inc(piece_hi, 1)

            steps = {"piece": piece, "xn1": xn1, "xn2": xn2, "ta": ta, "tb": tb, "t2a": t2a, "t2b": t2b, "soft0": soft, "route": route_exp, "split": split_hi,
                     "cpart": cum_parts, "base": norm_residual,
                     "oa": lambda g: [square(g, m) for m in range(NI)],
                     "ga": lambda g: gate_tanh(g, 0), "gb": lambda g: gate_tanh(g, 1)}
            for k in range(4):
                steps[f"x{k}" if k < NI else "bc"] = lambda g, k=k: project_x(g, k)
                steps[f"conv{k}"] = lambda g, k=k: tanh_conv(g, k)
            for k in range(NI):
                steps[f"z{k}"] = lambda g, k=k: project_z(g, k)
            for h in range(HEADS):
                steps[f"cb{h}"] = lambda g, h=h: decays(g, h)
            for t in range(FTILES + 1):
                steps[f"f{t}"] = lambda g, t=t: expert(g, t)
            split_hi((0, 0))
            act.wait_ge(s_load, 16 * len(loads))
            A(aneg[:, :], alog[:, :], ACT.Exp).then_inc(s_bias, 1)
            turns(act, steps, lambda i, front, back, late: act_front.begin((i, 0)) if front else None)

        @block.vector
        def _(dve):
            V = nc.vector
            prep = Chain(s_prep)
            prep.begin((0, 0))

            def split(hi, lo, raw):
                V.tensor_copy(hi, raw).then_inc(prep.mark(), 1)
                dve.wait_ge(s_prep, prep.now())
                rows = lo.shape[0]
                return V.tensor_tensor(lo, raw[0:rows], hi[0:rows], ALU.subtract)

            dve.wait_ge(s_tok, 16)
            split(tok_hi[:, :], tok_lo[:, :], tok_raw).then_inc(s_split, 1)
            dve.wait_ge(s_load, 16 * len(loads))
            dve.wait_ge(s_bias, 1 + 1)
            V.tensor_scalar(aneg[:, :], aneg[:, :], -1.0, None, ALU.mult).then_inc(prep.mark(), 1)
            np_ = len(PROJ)
            V.tensor_copy(pbias[:, 0:np_ - 1], gate_ps[0][:, 0:np_ - 1]).then_inc(prep.mark(), 1)
            V.tensor_copy(pbias[0:KB, np_ - 1:np_], gate_ps[0][0:KB, np_ - 1:np_]).then_inc(prep.mark(), 1)
            V.tensor_tensor(dtbias[:, :], gate_ps[0][0:H, 16:16 + HEADS], dtb[:, :], ALU.add).then_inc(prep.mark(), 1)
            dve.wait_ge(s_prep, prep.now())
            ia, ib = PROJ_AT["ga"], PROJ_AT["gb"]
            V.tensor_tensor(gbias[:, 0:1], pbias[:, ia:ia + 1], gba[:, :], ALU.add).then_inc(prep.mark(), 1)
            V.tensor_tensor(gbias[0:KB, 1:2], pbias[0:KB, ib:ib + 1], gbb[:, :], ALU.add).then_inc(prep.mark(), 1)
            dve.wait_ge(s_prep, prep.now())
            V.tensor_scalar(gbias[:, 0:1], gbias[:, 0:1], 0.5, None, ALU.mult).then_inc(prep.mark(), 1)
            V.tensor_scalar(gbias[0:KB, 1:2], gbias[0:KB, 1:2], 0.5, None, ALU.mult).then_inc(prep.mark(), 1)
            V.tensor_scalar(dhalf[:, :], dpar[:, :], 0.5, None, ALU.mult).then_inc(prep.mark(), 1)
            for s in range(2):
                V.tensor_tensor(pos[:, s * MODEL:(s + 1) * MODEL], pos[:, s * MODEL:(s + 1) * MODEL], tokb[:, :], ALU.add).then_inc(prep.mark(), 1)
            for k in range(NI):
                V.tensor_scalar(outp[:, k * MODEL:(k + 1) * MODEL], outp[:, k * MODEL:(k + 1) * MODEL], rms[:, k:k + 1],
                                    None, ALU.mult).then_inc(prep.mark(), 1)
            V.tensor_scalar(w1a_raw[:, :], w1a_raw[:, :], lnwa[:, 0:1], WSCALE, ALU.mult, ALU.mult).then_inc(prep.mark(), 1)
            V.tensor_scalar(w1b_raw[:, :], w1b_raw[:, :], lnwb[:, 0:1], WSCALE, ALU.mult, ALU.mult).then_inc(prep.mark(), 1)
            dve.wait_ge(s_prep, prep.now())

            split(w1a_hi[:, :], w1a_lo[:, :], w1a_raw[:, :]).then_inc(prep.mark(), 1)
            split(w1b_hi[:, :], w1b_lo[:, :], w1b_raw[:, :]).then_inc(prep.mark(), 1)
            split(ra_hi[:, :], ra_lo[:, :], ra_raw[:, :]).then_inc(prep.mark(), 1)
            split(rb_hi[:, :], rb_lo[:, :], rb_raw[:, :]).then_inc(s_split, 1)
            dve.wait_ge(s_split, 2)
            dve.wait_ge(s_const, CONSTS)

            V.tensor_copy(identb[:, :], ident[:, :]).then_inc(prep.mark(), 1)

            def embed(g, s):
                u = f"embed{s}"
                dve.wait_ge(full[u].sem, full[u].at(g))
                if s == 0:
                    if base_ready.any(g, 0):
                        dve.wait_ge(base_ready.sem, base_ready.at(g, 0))
                ins = V.tensor_tensor(h1[:, 2 * s:2 * s + 2, :].rearrange("p j n -> p (j n)"),
                                      bank[UNIT_BANK[u]][0:H, 0:2 * MODEL], pos[:, :], ALU.add)
                ins.then_inc(emptied[u].sem, 1)

            def moments(src, stats, small, chain):
                for j in range(TILES):
                    ins = V.bn_stats(stats[:, j, :], src[:, j, :])
                ins.then_inc(chain.mark(), 1)
                dve.wait_ge(chain.sem, chain.now())
                me, mo, ve, vo = (stats[:, :, c] for c in (1, 4, 2, 5))
                V.tensor_tensor(small[:, 0, :], me, mo, ALU.add).then_inc(chain.mark(), 1)
                V.tensor_tensor(small[:, 1, :], me, mo, ALU.subtract).then_inc(chain.mark(), 1)
                V.tensor_tensor(small[:, 2, :], ve, vo, ALU.add).then_inc(chain.mark(), 1)
                dve.wait_ge(chain.sem, chain.now())
                V.tensor_scalar(small[:, 0, :], small[:, 0, :], 0.5, None, ALU.mult).then_inc(chain.mark(), 1)
                V.tensor_tensor(small[:, 1, :], small[:, 1, :], small[:, 1, :], ALU.mult).then_inc(chain.mark(), 1)
                dve.wait_ge(chain.sem, chain.now())
                V.scalar_tensor_tensor(small[:, 3, :], small[:, 1, :], MODEL / 4.0, small[:, 2, :], ALU.mult, ALU.add).then_inc(chain.mark(), 1)
                dve.wait_ge(chain.sem, chain.now())

            def norm1(g):
                for u in latest("embed0", "embed1"):
                    dve.wait_ge(emptied[u].sem, emptied[u].at(g))
                moments(h1, stats, small, dve_front)
                V.tensor_scalar(roots_in[:, 0:TILES], small[:, 3, :], 1.0 / MODEL, EPS, ALU.mult, ALU.add).then_inc(dve_front.mark(), 1)
                dve.wait_ge(dve_front.sem, dve_front.now())
                V.tensor_scalar(roots_in[:, TILES:8], small[:, 3, :], (1.0 + EPS) / MODEL, EPS * EPS, ALU.mult,
                                ALU.add).then_inc(roots_asked.sem, 1)

            def xn1(g):
                dve.wait_ge(roots_done.sem, roots_done.at(g, 1))
                V.scalar_tensor_tensor(small[:, 4:6, :], small[:, 0:1, :].to_broadcast([H, 2, TILES]), -1.0,
                                       roots[:, :].rearrange("p (n j) -> p n j", n=2), ALU.mult,
                                       ALU.mult).then_inc(shift_ready.sem, 1)

            def tb(g):
                dve.wait_ge(hi_ready.sem, hi_ready.at(g, 1))
                V.tensor_tensor(xa_lo[:, :], bank[UNIT_BANK["ta"]][0:KA, 0:T], xa_hi[:, :],
                                ALU.subtract).then_inc(emptied["ta"].sem, 1)
                dve.wait_ge(hi_ready.sem, hi_ready.at(g, 2))
                V.tensor_tensor(xb_hl[KB:128, :], bank[UNIT_BANK["tb"]][0:KB, 0:T], xb_hl[0:KB, :],
                                ALU.subtract).then_inc(emptied["tb"].sem, 1)

            def dt(g):
                u = "dt"
                dve.wait_ge(full[u].sem, full[u].at(g))
                cols = TILES * HEADS
                flat = dt_raw[:, :, :].rearrange("p j h -> p (j h)")
                ins = V.scalar_tensor_tensor(dt_raw[:, :, :], bank[UNIT_BANK[u]][0:H, 0:cols].rearrange("p (j h) -> p j h", j=TILES),
                                             1.0 / WSCALE, dtbias[:, :].unsqueeze(1).to_broadcast([H, TILES, HEADS]), ALU.mult, ALU.add)
                ins.then_inc(emptied[u].sem, 1)
                dve.wait_ge(emptied[u].sem, emptied[u].at(g))
                V.scalar_tensor_tensor(sp[:, 0, :], flat, -1.0, flat, ALU.mult, ALU.max).then_inc(soft_in.sem, 1)
                V.tensor_scalar(sp[:, 2, :], flat, 0.0, None, ALU.max).then_inc(dve_soft.mark(), 1)

            def soft(g, n):
                e, s, s2, p = sp[:, 1, :], sp[:, 3, :], sp[:, 4, :], sp[:, 5, :]
                if n == 0:
                    dve.wait_ge(soft_e.sem, soft_e.at(g, 1))
                dve.wait_ge(dve_soft.sem, dve_soft.now())
                if n == 0:
                    V.tensor_scalar(s, e, 2.0, None, ALU.add).then_inc(dve_soft.mark(), 1)
                elif n == 1:
                    V.reciprocal(s2, s).then_inc(dve_soft.mark(), 1)
                elif n == 2:
                    V.tensor_tensor(s, e, s2, ALU.mult).then_inc(dve_soft.mark(), 1)
                elif n == 3:
                    V.tensor_tensor(s2, s, s, ALU.mult).then_inc(dve_soft.mark(), 1)
                elif n == 4:
                    V.tensor_scalar(p, s2, 1.0 / 15, None, ALU.mult).then_inc(dve_soft.mark(), 1)
                elif n < 11:
                    V.scalar_tensor_tensor(p, p, 1.0 / (23 - 2 * n), s2, ALU.add, ALU.mult).then_inc(dve_soft.mark(), 1)
                elif n == 11:
                    V.scalar_tensor_tensor(p, p, 1.0, s, ALU.add, ALU.mult).then_inc(dve_soft.mark(), 1)
                elif n == 12:
                    V.scalar_tensor_tensor(s, p, 2.0, sp[:, 2, :], ALU.mult, ALU.add).then_inc(dve_soft.mark(), 1)
                else:
                    if emptied["xt3"].any(before(g)):
                        dve.wait_ge(emptied["xt3"].sem, emptied["xt3"].at(before(g)))
                    V.tensor_scalar(dth[:, :, :].rearrange("p j h -> p (j h)"), s, 0.5, None, ALU.mult).then_inc(dve_soft.mark(), 1)
                    V.tensor_tensor(dta[:, :, :], s.rearrange("p (j h) -> p j h", j=TILES),
                                    aneg[:, :].unsqueeze(1).to_broadcast([H, TILES, HEADS]), ALU.mult).then_inc(dta_ready.sem, 1)

            def cum(g):
                u = "cum"
                dve.wait_ge(full[u].sem, full[u].at(g))
                flat = csum[:, :, :].rearrange("p j h -> p (j h)")
                V.tensor_copy(flat, bank[UNIT_BANK[u]][0:H, 0:TILES * HEADS]).then_inc(emptied[u].sem, 1)
                dve.wait_ge(emptied[u].sem, emptied[u].at(g))
                if full["cpart"].any(before(g)):
                    dve.wait_ge(full["cpart"].sem, full["cpart"].at(before(g)))
                part = [cpt[:, :, 32 * n:32 * n + HEADS] for n in range(3)]
                V.tensor_copy(part[0], csum[:, :, :]).then_inc(dve_front.mark(), 1)
                dve.wait_ge(dve_front.sem, dve_front.now())
                V.tensor_tensor(part[1], csum[:, :, :], part[0], ALU.subtract).then_inc(dve_front.mark(), 1)
                V.tensor_tensor(crest[:, :, :], csum[:, :, :], part[0], ALU.subtract).then_inc(dve_front.mark(), 1)
                dve.wait_ge(dve_front.sem, dve_front.now())
                V.tensor_tensor(part[2], crest[:, :, :], part[1], ALU.subtract).then_inc(cpt_ready.sem, 1)
                if emptied["cb5"].any(before(g)):
                    dve.wait_ge(emptied["cb5"].sem, emptied["cb5"].at(before(g)))
                V.tensor_scalar(ncum[:, :, :].rearrange("p j h -> p (j h)"), flat, -1.0, None, ALU.mult).then_inc(ncum_ready.sem, 1)

            def convolve(g, k):
                u = f"x{k}" if k < NI else "bc"
                dve.wait_ge(emptied[u].sem, emptied[u].at(g))
                dve.wait_ge(tap0_ready.sem, tap0_ready.at(g, k + 1))
                out = conv[:, k, :, :]
                for tap in range(1, TAPS):
                    ins = V.scalar_tensor_tensor(out, xpad[:, k, :, tap:tap + TOKENS], convw[:, k, tap:tap + 1], out, ALU.mult,
                                                 ALU.add)
                    if tap < TAPS - 1:
                        ins.then_inc(dve_front.mark(), 1)
                        dve.wait_ge(dve_front.sem, dve_front.now())
                    else:
                        ins.then_inc(conv_ready.sem, 1)

            def silu(g, k):
                dve.wait_ge(convt_ready.sem, convt_ready.at(g, k + 1))
                dve.wait_ge(conv_ready.sem, conv_ready.at(g, k + 1))
                t, v = convt[:, k, :, :], conv[:, k, :, :]
                if k < NI:
                    if k == 0:
                        if emptied["y2"].any(before(g)):
                            dve.wait_ge(emptied["y2"].sem, emptied["y2"].at(before(g)))
                        if full["xt3"].any(before(g)):
                            dve.wait_ge(full["xt3"].sem, full["xt3"].at(before(g)))
                    V.scalar_tensor_tensor(xs[:, k, :].rearrange("p (s t) -> p s t", s=SEQS), t, 1.0, v, ALU.add,
                                           ALU.mult).then_inc(silu_ready.sem, 1)
                else:
                    if full["g1"].any(before(g)):
                        dve.wait_ge(full["g1"].sem, full["g1"].at(before(g)))
                    for n, dst in enumerate((bs, cs)):
                        rows = slice(n * STATE, (n + 1) * STATE)
                        ins = V.scalar_tensor_tensor(dst[:, :].rearrange("p (s t) -> p s t", s=SEQS), t[rows], 1.0, v[rows],
                                                     ALU.add, ALU.mult)
                        if n == 0:
                            ins.then_inc(dve_front.mark(), 1)
                        else:
                            ins.then_inc(silu_ready.sem, 1)

            def masked(g, s):
                u = f"g{s}"
                dve.wait_ge(full[u].sem, full[u].at(g))
                V.tensor_tensor(gm[:, s, :], bank[UNIT_BANK[u]][0:H, 0:CAUSAL], causal[:, :], ALU.mult).then_inc(
                    emptied[u].sem, 1)

            def x_dt(g, j):
                u = f"xt{j}"
                dve.wait_ge(full[u].sem, full[u].at(g))
                if j == 0:
                    if full["y2"].any(before(g)):
                        dve.wait_ge(full["y2"].sem, full["y2"].at(before(g)))
                    dve.wait_ge(dta_ready.sem, dta_ready.at(g, 1))
                ins = V.tensor_tensor(xdt[:, j, :].rearrange("p (h d) -> p h d", h=HEADS),
                                      bank[UNIT_BANK[u]][0:H, 0:INNER].rearrange("p (h d) -> p h d", h=HEADS),
                                      dth[:, j, :].unsqueeze(2).to_broadcast([H, HEADS, HD]), ALU.mult)
                ins.then_inc(emptied[u].sem, 1)

            def weight(g, h):
                for u in latest("cb0", "g0", "g1") if h == 0 else (f"cb{h}",):
                    dve.wait_ge(emptied[u].sem, emptied[u].at(g))
                if h == 0:
                    if full["y2"].any(before(g)):
                        dve.wait_ge(full["y2"].sem, full["y2"].at(before(g)))
                V.scalar_tensor_tensor(wgt[:, h, :, :].rearrange("p s n -> p (s n)"), decay[:, h % 2, :, :].rearrange("p s n -> p (s n)"),
                                       1.0, gm[:, :, :].rearrange("p s n -> p (s n)"), ALU.min, ALU.mult).then_inc(wgt_ready.sem, 1)

            def gate_z(g, k):
                dve.wait_ge(emptied[f"z{k}"].sem, emptied[f"z{k}"].at(g))
                if y2_ready.any(g, k + 1 - NI):
                    dve.wait_ge(y2_ready.sem, y2_ready.at(g, k + 1 - NI))
                V.scalar_tensor_tensor(zs[:, k, :], zt[:, k, :], 1.0, zb[:, k, :], ALU.add, ALU.mult).then_inc(zs_ready.sem, 1)

            def y_out(g, n):
                u = f"y{n}"
                dve.wait_ge(full[u].sem, full[u].at(g))
                dve.wait_ge(silu_ready.sem, silu_ready.at(g, n + 1))
                if y2_ready.any(g, n + 1 - NI):
                    dve.wait_ge(y2_ready.sem, y2_ready.at(g, n + 1 - NI))
                ins = V.scalar_tensor_tensor(y1[:, n, :], xs[:, n, :], dhalf[:, n:n + 1], bank[UNIT_BANK[u]][:, 0:T],
                                             ALU.mult, ALU.add)
                ins.then_inc(emptied[u].sem, 1)

            def gate_out(g, n):
                u, rows = ("oa", "ob")[n], (KA, KB)[n]
                dve.wait_ge(full[u].sem, full[u].at(g))
                gu = ("ga", "gb")[n]
                dve.wait_ge(emptied[gu].sem, emptied[gu].at(g))
                if full["ow1"].any(before(g)):
                    dve.wait_ge(full["ow1"].sem, full["ow1"].at(before(g)))
                V.scalar_tensor_tensor(gated[0:rows, n, :], gt[0:rows, n, :], 1.0, bank[UNIT_BANK[u]][0:rows, 0:T],
                                       ALU.add, ALU.mult).then_inc(emptied[u].sem, 1)

            def ss(g):
                u = "ss"
                dve.wait_ge(full[u].sem, full[u].at(g))
                ins = V.tensor_scalar(rinv_in[:, :], bank[UNIT_BANK[u]][0:H, 0:TILES], 0.25 / INNER, EPS, ALU.mult, ALU.add)
                ins.then_inc(emptied[u].sem, 1)

            def residual(g, s):
                u = f"ow{s}"
                if s == 0:
                    dve.wait_ge(roots2_done.sem, roots2_done.at(g, 1))
                    V.tensor_scalar(rinv[:, :], rinv[:, :], 0.25, None, ALU.mult).then_inc(dve_back.mark(), 1)
                    dve.wait_ge(dve_back.sem, dve_back.now())
                    dve.wait_ge(base_ready.sem, base_ready.at(g, 1))
                    if down_free.any(before(g), SEQS):
                        dve.wait_ge(down_free.sem, down_free.at(before(g), SEQS))
                dve.wait_ge(full[u].sem, full[u].at(g))
                for j in (2 * s, 2 * s + 1):
                    ins = V.scalar_tensor_tensor(h2[:, j, :], bank[UNIT_BANK[u]][0:H, (j % 2) * MODEL:(j % 2 + 1) * MODEL],
                                                 rinv[:, j:j + 1], base[:, j, :], ALU.mult, ALU.add)
                    if j % 2 == 0:
                        ins.then_inc(dve_back.mark(), 1)
                    else:
                        ins.then_inc(emptied[u].sem, 1)

            def norm2(g):
                dve.wait_ge(dve_back.sem, dve_back.now())
                for u in latest("ow0", "ow1"):
                    dve.wait_ge(emptied[u].sem, emptied[u].at(g))
                moments(h2, stats2, small2, dve_back)
                V.tensor_scalar(roots2_in[:, :], small2[:, 3, :], 1.0 / MODEL, EPS, ALU.mult, ALU.add).then_inc(roots2_asked.sem, 1)

            def xn2(g):
                dve.wait_ge(roots2_done.sem, roots2_done.at(g, 2))
                V.scalar_tensor_tensor(small2[:, 4, :], small2[:, 0, :], -1.0, roots2[:, :], ALU.mult,
                                       ALU.mult).then_inc(shift2_ready.sem, 1)

            def t2b(g):
                dve.wait_ge(hi2_ready.sem, hi2_ready.at(g, 1))
                V.tensor_tensor(fa_lo[:, :], bank[UNIT_BANK["t2a"]][0:KA, 0:T], fa_hi[:, :], ALU.subtract).then_inc(
                    emptied["t2a"].sem, 1)
                dve.wait_ge(hi2_ready.sem, hi2_ready.at(g, 2))
                V.tensor_tensor(fb_hl[KB:128, :], bank[UNIT_BANK["t2b"]][0:KB, 0:T], fb_hl[0:KB, :], ALU.subtract).then_inc(
                    emptied["t2b"].sem, 1)

            def route(g):
                u = "route"
                dve.wait_ge(full[u].sem, full[u].at(g))
                ins = V.tensor_tensor(rl[:, :, :], bank[UNIT_BANK[u]][0:H, 0:TILES * ROUTED].rearrange("p (j e) -> p j e", j=TILES),
                                      rbias[:, :].unsqueeze(1).to_broadcast([H, TILES, ROUTED]), ALU.add)
                ins.then_inc(emptied[u].sem, 1)

            def combine(g, n):
                e, s, keep, tmp = rs[:, 0, :, :], rs[:, 2, :, :], rs[:, 3, :, :], rs[:, 4, :, :]
                if n == 0:
                    dve.wait_ge(router_e.sem, router_e.at(g, 1))
                    V.tensor_scalar(e, e, 1.0, None, ALU.add).then_inc(dve_comb.mark(), 1)
                    return
                dve.wait_ge(dve_comb.sem, dve_comb.now())
                if n == 1:
                    V.reciprocal(s, e).then_inc(dve_comb.mark(), 1)
                elif n == 2:
                    V.tensor_tensor(tmp[:, :, 0], s[:, :, 1], s[:, :, 2], ALU.min).then_inc(dve_comb.mark(), 1)
                    V.tensor_tensor(tmp[:, :, 1], s[:, :, 0], s[:, :, 1], ALU.min).then_inc(dve_comb.mark(), 1)
                elif n == 3:
                    V.tensor_tensor(keep[:, :, 0], s[:, :, 0], tmp[:, :, 0], ALU.is_ge).then_inc(dve_comb.mark(), 1)
                    V.tensor_tensor(keep[:, :, 2], s[:, :, 2], tmp[:, :, 1], ALU.is_gt).then_inc(dve_comb.mark(), 1)
                elif n == 4:
                    V.tensor_tensor(tmp[:, :, 2], keep[:, :, 0], keep[:, :, 2], ALU.add).then_inc(dve_comb.mark(), 1)
                elif n == 5:
                    V.tensor_scalar(keep[:, :, 1], tmp[:, :, 2], -1.0, 2.0, ALU.mult, ALU.add).then_inc(dve_comb.mark(), 1)
                elif n == 6:
                    V.tensor_tensor(s, s, keep, ALU.mult).then_inc(dve_comb.mark(), 1)
                elif n == 7:
                    V.tensor_tensor(tmp[:, :, 0], s[:, :, 0], s[:, :, 1], ALU.add).then_inc(dve_comb.mark(), 1)
                elif n == 8:
                    V.tensor_tensor(tmp[:, :, 0], tmp[:, :, 0], s[:, :, 2], ALU.add).then_inc(dve_comb.mark(), 1)
                elif n == 9:
                    V.reciprocal(tmp[:, :, 1], tmp[:, :, 0]).then_inc(dve_comb.mark(), 1)
                else:
                    V.scalar_tensor_tensor(comb[:, :, :], s, 0.5, tmp[:, :, 1:2].to_broadcast([H, TILES, ROUTED]), ALU.mult,
                                           ALU.mult).then_inc(dve_comb.mark(), 1)

            def expert_gate(g, t):
                if t == FTILES:
                    return
                dve.wait_ge(ft_ready.sem, ft_ready.at(g, t + 1))
                V.scalar_tensor_tensor(fg[:, t % 2, :], ft[:, t % 2, :], 1.0, gate_ps[t % 2][:, 0:T], ALU.add,
                                       ALU.mult).then_inc(fg_ready.sem, 1)

            def expert_hidden(g, t):
                dve.wait_ge(fg_ready.sem, fg_ready.at(g, t + 1))
                dve.wait_ge(up_full.sem, up_full.at(g, t + 1))
                if flo_ready.any(g, t + 1 - 2):
                    dve.wait_ge(flo_ready.sem, flo_ready.at(g, t + 1 - 2))
                V.tensor_tensor(fh[:, t % 2, :], fg[:, t % 2, :], up_ps[t % 2][:, 0:T], ALU.mult).then_inc(fh_ready.sem, 1)

            def down(g, e, s):
                n = SEQS * e + s
                dve.wait_ge(down_full.sem, down_full.at(g, n + 1))
                if n == 0:
                    if stored.any(g, 0):
                        dve.wait_ge(stored.sem, stored.at(g, 0))
                elif e:
                    dve.wait_ge(down_free.sem, down_free.at(g, n + 1 - SEQS))
                    if n == SEQS:
                        dve.wait_ge(dve_comb.sem, dve_comb.now())
                for j in (2 * s, 2 * s + 1):
                    rows = down_ps[0:H, (j % 2) * MODEL:(j % 2 + 1) * MODEL]
                    if e == 0:
                        ins = V.scalar_tensor_tensor(acc[:, j, :], rows, 0.5, h2[:, j, :], ALU.mult, ALU.add)
                    else:
                        ins = V.scalar_tensor_tensor(acc[:, j, :], rows, comb[:, j, e - 1:e], acc[:, j, :], ALU.mult, ALU.add)
                ins.then_inc(down_free.sem, 1)

            steps = {"norm1": norm1, "xn1": xn1, "tb": tb, "dt": dt, "cum": cum, "ss": ss,
                     "gate": lambda g: [gate_out(g, n) for n in range(2)], "norm2": norm2, "xn2": xn2, "t2b": t2b, "route": route}
            for n in range(SOFT_STEPS):
                steps[f"soft{n}"] = lambda g, n=n: soft(g, n)
            for n in range(COMB_STEPS):
                steps[f"comb{n}"] = lambda g, n=n: combine(g, n)
            for t in range(FTILES):
                steps[f"h{t}"] = lambda g, t=t: expert_hidden(g, t)
            for s in range(SEQS):
                steps[f"embed{s}"] = lambda g, s=s: embed(g, s)
                steps[f"g{s}"] = lambda g, s=s: masked(g, s)
                steps[f"ow{s}"] = lambda g, s=s: residual(g, s)
            for k in range(4):
                steps[f"conv{k}"] = lambda g, k=k: convolve(g, k)
                steps[f"silu{k}"] = lambda g, k=k: silu(g, k)
                steps[f"xt{k}"] = lambda g, k=k: x_dt(g, k)
            for h in range(HEADS):
                steps[f"w{h}"] = lambda g, h=h: weight(g, h)
            for n in range(NI):
                steps[f"y{n}"] = lambda g, n=n: y_out(g, n)
                steps[f"sz{n}"] = lambda g, n=n: gate_z(g, n)
            for t in range(FTILES + 1):
                steps[f"f{t}"] = lambda g, t=t: expert_gate(g, t)
            for e in range(EXPERTS):
                for s in range(SEQS):
                    steps[f"d{e}{s}"] = lambda g, e=e, s=s: down(g, e, s)

            def begin(i, front, back, late):
                if front:
                    dve_front.begin((i, 0))
                    dve_soft.begin((i, 0))
                if back:
                    dve_back.begin((i, -1))
                if late:
                    dve_comb.begin((i, -2))
            turns(dve, steps, begin)

        @block.tensor
        def _(pe):
            M = nc.tensor.matmul

            pe.wait_ge(s_load, 16 * len(loads))
            pe.wait_ge(s_const, CONSTS)
            for n, (c, width) in enumerate(PROJ.values()):
                M(gate_ps[0][0:width, n:n + 1], w1a_raw[:, c:c + width], lnba[:, :], start=True, stop=False)
                M(gate_ps[0][0:width, n:n + 1], w1b_raw[0:KB, c:c + width], lnbb[:, :], start=False, stop=True)
            M(gate_ps[0][0:H, 16:16 + HEADS], lnba[:, 0:1].to_broadcast([KA, H]), w1a_raw[:, COL_DT:COL_DT + HEADS], start=True, stop=False)
            M(gate_ps[0][0:H, 16:16 + HEADS], lnbb[:, 0:1].to_broadcast([KB, H]), w1b_raw[0:KB, COL_DT:COL_DT + HEADS], start=False,
              stop=True).then_inc(s_bias, 1)
            pe.wait_ge(s_split, 1)

            def five(out, a_hi, a_lo, b_hi, b_lo, xa, xl, xb, first=True):
                M(out, a_hi, xa, start=first, stop=False, skip_group_check=True)
                M(out, a_lo, xa, start=False, stop=False, skip_group_check=True)
                M(out, a_hi, xl, start=False, stop=False, skip_group_check=True)
                M(out, b_hi, xb, start=False, stop=False, skip_group_check=True)
                return M(out, b_lo, xb[0:KB], start=False, stop=True, skip_group_check=True)

            def five_rows(out, w, xa, xl, xb, first):
                a_hi, a_lo, b_hi, b_lo = w
                M(out, xa, a_hi, start=first, stop=False, skip_group_check=True)
                M(out, xa, a_lo, start=False, stop=False, skip_group_check=True)
                M(out, xl, a_hi, start=False, stop=False, skip_group_check=True)
                M(out, xb, b_hi, start=False, stop=False, skip_group_check=True)
                return M(out, xb[0:KB], b_lo, start=False, stop=True, skip_group_check=True)

            def embed(g, s):
                u = f"embed{s}"
                pe.wait_ge(patch_lo.sem, patch_lo.at(g, 1))
                pe.wait_ge(patch_hi.sem, patch_hi.at(g, 1))
                if emptied[u].any(g, -1):
                    pe.wait_ge(emptied[u].sem, emptied[u].at(g, -1))
                hi = pat_hi[:, :].rearrange("p (k t) -> p k t", k=KP)
                lo = pat_lo[:, :].rearrange("p (k t) -> p k t", k=KP)
                for j in (2 * s, 2 * s + 1):
                    out = bank[UNIT_BANK[u]][0:H, (j % 2) * MODEL:(j % 2 + 1) * MODEL]
                    for k in range(KP):
                        xh, xl = hi[:, k, j * H:(j + 1) * H], lo[:, k, j * H:(j + 1) * H]
                        wh, wl = tok_hi[:, k * MODEL:(k + 1) * MODEL], tok_lo[:, k * MODEL:(k + 1) * MODEL]
                        M(out, xh, wh, start=(k == 0), stop=False, skip_group_check=True)
                        M(out, xh, wl, start=False, stop=False, skip_group_check=True)
                        ins = M(out, xl, wh, start=False, stop=(k == KP - 1), skip_group_check=True)
                ins.then_inc(full[u].sem, 1)

            def transposes(g, units, src, ready):
                pe.wait_ge(ready.sem, ready.at(g, 1))
                for u in units:
                    if emptied[u].any(g, -1):
                        pe.wait_ge(emptied[u].sem, emptied[u].at(g, -1))
                for u, c, width in zip(units, (0, KA), (KA, KB)):
                    for j in range(TILES):
                        ins = nc.tensor.transpose(bank[UNIT_BANK[u]][0:width, j * H:(j + 1) * H], src[:, j, c:c + width],
                                                  ident[0:H, 0:H])
                    ins.then_inc(full[u].sem, 1)

            def x_ready(g, u):
                if isinstance(g[0], int) and g == (0, 0):
                    pe.wait_ge(s_split, 2)
                for part in latest("ta", "tb", before=u):
                    pe.wait_ge(emptied[part].sem, emptied[part].at(g))

            def dt(g):
                u = "dt"
                x_ready(g, u)
                if emptied[u].any(g, -1):
                    pe.wait_ge(emptied[u].sem, emptied[u].at(g, -1))
                c = slice(COL_DT, COL_DT + HEADS)
                for j in range(TILES):
                    t = slice(j * H, (j + 1) * H)
                    ins = five_rows(bank[UNIT_BANK[u]][0:H, j * HEADS:(j + 1) * HEADS],
                                    (w1a_hi[:, c], w1a_lo[:, c], w1b_hi[:, c], w1b_lo[:, c]), xa_hi[:, t], xa_lo[:, t], xb_hl[:, t], True)
                ins.then_inc(full[u].sem, 1)

            def project(g, u):
                c, width = PROJ[u]
                if u == "x0":
                    x_ready(g, u)
                if emptied[u].any(g, -1):
                    pe.wait_ge(emptied[u].sem, emptied[u].at(g, -1))
                cols = slice(c, c + width)
                five(bank[UNIT_BANK[u]][0:width, 0:T], w1a_hi[:, cols], w1a_lo[:, cols], w1b_hi[:, cols], w1b_lo[:, cols],
                            xa_hi[:, :], xa_lo[:, :], xb_hl[:, :]).then_inc(full[u].sem, 1)

            def cum(g):
                u = "cum"
                pe.wait_ge(dta_ready.sem, dta_ready.at(g, 1))
                if emptied[u].any(g, -1):
                    pe.wait_ge(emptied[u].sem, emptied[u].at(g, -1))
                halves = dta[:, :, :].rearrange("p (s f) h -> p f s h", s=SEQS)
                out = bank[UNIT_BANK[u]][0:H, 0:TILES * HEADS].rearrange("p (s f h) -> p f s h", s=SEQS, f=2)
                M(out[:, 0], upper[:, :], halves[:, 0], start=True, stop=True, skip_group_check=True)
                M(out[:, 1], ones[0:H, :], halves[:, 0], start=True, stop=False, skip_group_check=True)
                M(out[:, 1], upper[:, :], halves[:, 1], start=False, stop=True, skip_group_check=True).then_inc(full[u].sem, 1)

            def cum_parts(g):
                u = "cpart"
                pe.wait_ge(cpt_ready.sem, cpt_ready.at(g, 1))
                if emptied[u].any(g, -1):
                    pe.wait_ge(emptied[u].sem, emptied[u].at(g, -1))
                for j in range(TILES):
                    ins = nc.tensor.transpose(bankb[UNIT_BANK[u]][0:96, j * H:(j + 1) * H], cpt[:, j, :], identb[0:H, 0:H])
                ins.then_inc(full[u].sem, 1)

            def cb_products(g, s):
                u = f"g{s}"
                pe.wait_ge(silu_ready.sem, silu_ready.at(g, 4))
                if emptied[u].any(g, -1):
                    pe.wait_ge(emptied[u].sem, emptied[u].at(g, -1))
                t0 = s * TOKENS
                M(bank[UNIT_BANK[u]][0:H, 0:TOKENS], bs[:, t0:t0 + H], cs[:, t0:t0 + TOKENS], start=True, stop=True,
                  skip_group_check=True)
                M(bank[UNIT_BANK[u]][0:H, TOKENS:CAUSAL], bs[:, t0 + H:t0 + TOKENS], cs[:, t0 + H:t0 + TOKENS], start=True,
                         stop=True, skip_group_check=True).then_inc(full[u].sem, 1)

            def x_rows(g, j):
                u = f"xt{j}"
                pe.wait_ge(silu_ready.sem, silu_ready.at(g, NI))
                if emptied[u].any(g, -1):
                    pe.wait_ge(emptied[u].sem, emptied[u].at(g, -1))
                for k in range(NI):
                    ins = nc.tensor.transpose(bank[UNIT_BANK[u]][0:H, k * 128:(k + 1) * 128], xs[:, k, j * H:(j + 1) * H], ident[:, :])
                ins.then_inc(full[u].sem, 1)

            def broadcast(g, h):
                u = f"cb{h}"
                for part in latest("cpart", before=u):
                    pe.wait_ge(emptied[part].sem, emptied[part].at(g))
                if emptied[u].any(g, -1):
                    pe.wait_ge(emptied[u].sem, emptied[u].at(g, -1))
                M(bank[UNIT_BANK[u]][0:H, 0:T], pick[:, h, :], cumpart[:, :], start=True, stop=True, skip_group_check=True).then_inc(full[u].sem, 1)

            def scan_out(g, n):
                u = f"y{n}"
                pe.wait_ge(wgt_ready.sem, wgt_ready.at(g, 2 * n + 2))
                for x in latest("xt0", "xt1", "xt2", "xt3", before=u):
                    pe.wait_ge(emptied[x].sem, emptied[x].at(g))
                if emptied[u].any(g, -1):
                    pe.wait_ge(emptied[u].sem, emptied[u].at(g, -1))
                for head in (2 * n, 2 * n + 1):
                    rows = slice((head % 2) * HD, (head % 2 + 1) * HD)
                    cols = slice(head * HD, (head + 1) * HD)
                    for s in range(SEQS):
                        t0 = s * TOKENS
                        M(bank[UNIT_BANK[u]][rows, t0:t0 + TOKENS], xdt[:, 2 * s, cols], wgt[:, head, s, 0:TOKENS],
                          start=(s == 0), stop=False, skip_group_check=True)
                        ins = M(bank[UNIT_BANK[u]][rows, t0 + H:t0 + TOKENS], xdt[:, 2 * s + 1, cols], wgt[:, head, s, TOKENS:CAUSAL],
                                start=False, stop=True, skip_group_check=True)
                ins.then_inc(full[u].sem, 1)

            def out_project(g, n):
                u, c, width = (("oa", 0, KA), ("ob", KA, KB))[n]
                pe.wait_ge(y2_ready.sem, y2_ready.at(g, NI))
                if emptied[u].any(g, -1):
                    pe.wait_ge(emptied[u].sem, emptied[u].at(g, -1))
                for k in range(NI):
                    ins = M(bank[UNIT_BANK[u]][0:width, 0:T], outp[:, k * MODEL + c:k * MODEL + c + width], y2[:, k, :],
                            start=(k == 0), stop=(k == NI - 1), skip_group_check=True)
                ins.then_inc(full[u].sem, 1)

            def square_sums(g):
                u = "ss"
                pe.wait_ge(sqsum_ready.sem, sqsum_ready.at(g, 1))
                if emptied[u].any(g, -1):
                    pe.wait_ge(emptied[u].sem, emptied[u].at(g, -1))
                for j in range(TILES):
                    ins = M(bank[UNIT_BANK[u]][0:H, j:j + 1], sq[:, 0, j * H:(j + 1) * H], ones[:, 0:1], start=True, stop=True,
                            skip_group_check=True)
                ins.then_inc(full[u].sem, 1)

            def out_rows(g, s):
                u = f"ow{s}"
                for o in latest("oa", "ob", before=u):
                    pe.wait_ge(emptied[o].sem, emptied[o].at(g))
                if emptied[u].any(g, -1):
                    pe.wait_ge(emptied[u].sem, emptied[u].at(g, -1))
                for j in (2 * s, 2 * s + 1):
                    out = bank[UNIT_BANK[u]][0:H, (j % 2) * MODEL:(j % 2 + 1) * MODEL]
                    t = slice(j * H, (j + 1) * H)
                    M(out, gated[0:KA, 0, t], owa[:, :], start=True, stop=False, skip_group_check=True)
                    ins = M(out, gated[0:KB, 1, t], owb[:, :], start=False, stop=True, skip_group_check=True)
                ins.then_inc(full[u].sem, 1)

            def f_ready(g, u=None):
                for part in latest("t2a", "t2b", before=u):
                    pe.wait_ge(emptied[part].sem, emptied[part].at(g))

            def route(g):
                u = "route"
                f_ready(g, u)
                if emptied[u].any(g, -1):
                    pe.wait_ge(emptied[u].sem, emptied[u].at(g, -1))
                for j in range(TILES):
                    t = slice(j * H, (j + 1) * H)
                    ins = five_rows(bank[UNIT_BANK[u]][0:H, j * ROUTED:(j + 1) * ROUTED],
                                    (ra_hi[:, :], ra_lo[:, :], rb_hi[:, :], rb_lo[:, :]), fa_hi[:, t], fa_lo[:, t], fb_hl[:, t], True)
                ins.then_inc(full[u].sem, 1)

            def expert(g, t):
                if t == FTILES:
                    return
                if t == 0:
                    f_ready(g)
                    if isinstance(g[0], int) and g[0] + g[1] == 0:
                        pe.wait_ge(piece_hi, len(pieces))
                        pe.wait_ge(piece_lo, len(pieces))
                if fh_ready.any(g, t + 1 - 2):
                    pe.wait_ge(fh_ready.sem, fh_ready.at(g, t + 1 - 2))
                cols = slice(t * 128, (t + 1) * 128)
                out = gate_ps[t % 2][:, 0:T], up_ps[t % 2][:, 0:T]
                for w in range(2):
                    M(out[w], gua_hi[w][:, cols], fa_hi[:, :], start=True, stop=False, skip_group_check=True)
                    M(out[w], gua_lo[w][:, cols], fa_hi[:, :], start=False, stop=False, skip_group_check=True)
                    M(out[w], gua_hi[w][:, cols], fa_lo[:, :], start=False, stop=False, skip_group_check=True)
                    M(out[w], gub_hi[w][:, cols], fb_hl[:, :], start=False, stop=False, skip_group_check=True)
                M(out[0], gub_lo[0:KB, cols], fb_hl[0:KB, :], start=False, stop=True, skip_group_check=True).then_inc(gate_full.sem, 1)
                M(out[1], gub_lo[KB:128, cols], fb_up[KB:128, :], start=False, stop=True, skip_group_check=True).then_inc(up_full.sem, 1)

            def down(g, e, s):
                n = SEQS * e + s
                if s == 0:
                    pe.wait_ge(flo_ready.sem, flo_ready.at(g, NF * (e + 1)))
                    pe.wait_ge(fhi_ready.sem, fhi_ready.at(g, NF * (e + 1)))
                if down_free.any(g, n):
                    pe.wait_ge(down_free.sem, down_free.at(g, n))
                for j in (2 * s, 2 * s + 1):
                    t = slice(j * H, (j + 1) * H)
                    out = down_ps[0:H, (j % 2) * MODEL:(j % 2 + 1) * MODEL]
                    for k in range(NF):
                        w = slice((NF * e + k) * MODEL, (NF * e + k + 1) * MODEL)
                        hi, lo = fh_hi[:, e % 2, k, t], fh_lo[:, e % 2, k, t]
                        M(out, hi, down_hi[:, w], start=(k == 0), stop=False, skip_group_check=True)
                        M(out, hi, down_lo[:, w], start=False, stop=False, skip_group_check=True)
                        ins = M(out, lo, down_hi[:, w], start=False, stop=(k == NF - 1), skip_group_check=True)
                ins.then_inc(down_full.sem, 1)

            steps = {"ta": lambda g: transposes(g, ("ta", "tb"), rows1, xn_ready), "t2a": lambda g: transposes(g, ("t2a", "t2b"), rows2, xn2_ready),
                     "dt": dt, "cum": cum, "cpart": cum_parts, "ss": square_sums, "route": route,
                     "oa": lambda g: out_project(g, 0), "ob": lambda g: out_project(g, 1)}
            for u in PROJ:
                steps[u] = lambda g, u=u: project(g, u)
            for s in range(SEQS):
                steps[f"embed{s}"] = lambda g, s=s: embed(g, s)
                steps[f"g{s}"] = lambda g, s=s: cb_products(g, s)
                steps[f"ow{s}"] = lambda g, s=s: out_rows(g, s)
            for j in range(TILES):
                steps[f"xt{j}"] = lambda g, j=j: x_rows(g, j)
            for h in range(HEADS):
                steps[f"cb{h}"] = lambda g, h=h: broadcast(g, h)
            for n in range(NI):
                steps[f"y{n}"] = lambda g, n=n: scan_out(g, n)
            for t in range(FTILES + 1):
                steps[f"f{t}"] = lambda g, t=t: expert(g, t)
            for e in range(EXPERTS):
                for s in range(SEQS):
                    steps[f"d{e}{s}"] = lambda g, e=e, s=s: down(g, e, s)
            turns(pe, steps)


def kernel(**inputs):
    import numpy as np
    import concourse.bacc as bacc
    from concourse.bass_utils import run_bass_kernel_spmd

    def rows(a, n):
        return np.ascontiguousarray(np.broadcast_to(a.reshape(1, -1), (n, a.size)))

    def by_tile(a, tiles):
        return np.ascontiguousarray(a.reshape(tiles, 128, -1).transpose(1, 0, 2).reshape(128, -1))

    a = {k.removeprefix("L0_"): np.asarray(v) for k, v in inputs.items()}
    side, p = 14, 16
    x = a["x"].reshape(GROUPS, SEQS, 3, side, p, side, p).transpose(0, 2, 4, 6, 1, 3, 5)
    x = x.reshape(GROUPS, KP, 128, T).transpose(0, 2, 1, 3).reshape(GROUPS, 128, KP * T)

    def experts(shared, routed):
        return np.concatenate([a[shared][None], a[routed]], 0)

    arrays = {
        "patches": x,
        "tok_w": by_tile(a["tok_W"].T, KP),
        "tok_b": rows(a["tok_b"], H),
        "pos": a["tok_pos"].reshape(2, H, MODEL).transpose(1, 0, 2).reshape(H, 2 * MODEL),
        "ln_w": a["attn_ln_w"].reshape(MODEL, 1),
        "ln_b": a["attn_ln_b"].reshape(MODEL, 1),
        "w1": np.concatenate([a["attn_in_proj_w"], a["attn_gate_w"]], 1),
        "conv_w": a["attn_conv_w"].reshape(4, 128, TAPS).transpose(1, 0, 2),
        "conv_b": a["attn_conv_b"].reshape(4, 128).T,
        "dt_bias": rows(a["attn_dt_bias"], H),
        "A_log": rows(a["attn_A_log"], H),
        "D": np.repeat(a["attn_D_param"], HD).reshape(NI, 128).T,
        "rms_w": a["attn_rms_w"].reshape(NI, 128).T,
        "out_proj": by_tile(a["attn_out_proj_w"], NI),
        "gate_b": a["attn_gate_b"].reshape(MODEL, 1),
        "out_w": a["attn_out_w"],
        "out_b": rows(a["attn_out_b"], H),
        "experts_gate": experts("ffn_shared_gate", "ffn_routed_gate").transpose(1, 0, 2).reshape(MODEL, EXPERTS * FF),
        "experts_up": experts("ffn_shared_up", "ffn_routed_up").transpose(1, 0, 2).reshape(MODEL, EXPERTS * FF),
        "down": by_tile(experts("ffn_shared_down", "ffn_routed_down").reshape(EXPERTS * FF, MODEL), FTILES),
        "router_w": a["ffn_router_w"],
        "routing_bias": rows(a["ffn_routing_bias"], H),
    }
    arrays = {k: np.ascontiguousarray(v) for k, v in arrays.items()}
    nc = bacc.Bacc("TRN2", target_bir_lowering=False, num_devices=1)
    dram = {k: nc.dram_tensor(f"in_{k}", v.shape, F32, kind="ExternalInput").ap() for k, v in arrays.items()}
    dram["out"] = nc.dram_tensor("out", [GROUPS, H, TILES * MODEL], F32, kind="ExternalOutput").ap()
    build(nc, dram)
    out = run_bass_kernel_spmd(nc, [{f"in_{k}": v for k, v in arrays.items()}], core_ids=[0]).results[0]["out"]
    out = out.reshape(GROUPS, H, SEQS, 2, MODEL).transpose(0, 2, 3, 1, 4)
    return np.ascontiguousarray(out.reshape(BATCH, TOKENS, MODEL))
```
